# Optimizing a Trainium2 kernel written in Bass

```python
import numpy as np
import jax
import jax.numpy as jnp

def _softmax(x, axis=-1):
    return jax.nn.softmax(x, axis=axis)

def _gelu(x):
    return jax.nn.gelu(x, approximate=True)

def _silu(x):
    return jax.nn.silu(x)

def _sigmoid(x):
    return jax.nn.sigmoid(x)

def _layernorm(x, axis=-1, eps=1e-05):
    m = jnp.mean(x, axis=axis, keepdims=True)
    v = jnp.var(x, axis=axis, keepdims=True)
    return (x - m) / jnp.sqrt(v + eps)

def _scatter_add(tgt, idx, src, axis=0):
    return tgt.at[idx].add(src)

def _segment_sum(src, seg, n):
    return jax.ops.segment_sum(src, seg, n)
kernel_name = 'mk_seq_postln_d2_jaxref_r8_fd7a3c'

def setup_inputs(seed: int=0):
    np.random.seed(seed)
    _w = jnp.asarray

    def _L0_attn_setup():
        import jax, jax.numpy as jnp
        import numpy as np
        from jax import lax
        B, L, HS = (4, 512, 128)
        NH, DK, DV = (4, 32, 32)
        CONV, CHUNK, FIRS, FIRL = (4, 32, 5, 64)
        GIN, GH = (HS + 16, HS * 2 // 2)
        DECAY = 1.0 - 1.0 / 3000.0
        EPS_FLOOR = 0.08 * DECAY
        RMS_EPS = 1e-05

        def _l2norm(x):
            return x * lax.rsqrt(jnp.sum(x * x, -1, keepdims=True) + 1e-06)

        def _dwconv_causal(x, filt):
            K = filt.shape[-1]
            xf = jnp.transpose(x, (0, 2, 1))
            xf = jnp.pad(xf, ((0, 0), (0, 0), (K - 1, 0)))
            y = lax.conv_general_dilated(xf, filt[:, None, :], (1,), 'VALID', feature_group_count=filt.shape[0], dimension_numbers=('NCH', 'OIH', 'NCH'))
            return jnp.transpose(y, (0, 2, 1))

        def _delta_rule_chunkwise(q, k, v, beta, chunk=CHUNK):
            b, h, Lq, dk = q.shape
            dv = v.shape[-1]
            n = Lq // chunk
            q = _l2norm(q)
            k = _l2norm(k)
            v = v * beta[..., None]
            kb = k * beta[..., None]
            r = lambda x: x.reshape(b, h, n, chunk, -1)
            q, k, v, kb = (r(q), r(k), r(v), r(kb))
            strict_low = jnp.tril(jnp.ones((chunk, chunk), bool), -1)
            A = jnp.where(strict_low, -jnp.einsum('bhnid,bhnjd->bhnij', kb, k), 0.0)
            eye = jnp.eye(chunk, dtype=q.dtype)
            T = jax.scipy.linalg.solve_triangular(eye - A, jnp.broadcast_to(eye, A.shape), lower=True, unit_diagonal=True)
            u = T @ v
            w = T @ kb
            low = jnp.tril(jnp.ones((chunk, chunk), bool))

            def step(S, inp):
                qi, ki, ui, wi = inp
                attn = jnp.where(low, jnp.einsum('bhid,bhjd->bhij', qi, ki), 0.0)
                u_i = ui - wi @ S
                o_i = qi @ S + attn @ u_i
                S = S + jnp.einsum('bhcd,bhce->bhde', ki, u_i)
                return (S, o_i)
            mv = lambda x: jnp.moveaxis(x, 2, 0)
            S0 = jnp.zeros((b, h, dk, dv), q.dtype)
            S, o = lax.scan(step, S0, (mv(q), mv(k), mv(u), mv(w)))
            o = jnp.moveaxis(o, 0, 2).reshape(b, h, Lq, dv)
            return (o, S)

        def _stats(x):
            mean = jnp.mean(x, -1, keepdims=True)
            var = jnp.var(x, -1, keepdims=True)
            am = jnp.mean(jnp.abs(x), -1, keepdims=True)
            l2 = jnp.linalg.norm(x, axis=-1, keepdims=True)
            return jnp.concatenate([mean, var, am, l2], -1)
        key = jax.random.key(seed)
        ks = jax.random.split(key, 16)
        s = 0.02
        fs = jnp.zeros((NH, DV, FIRS)).at[..., -1].set(1.0) + 0.015 * jax.random.normal(ks[8], (NH, DV, FIRS))
        fl = jnp.zeros((NH, DV, FIRL)).at[..., -1].set(1.0) + 0.015 * jax.random.normal(ks[9], (NH, DV, FIRL))
        return {'hidden_states': jax.random.normal(ks[0], (B, L, HS), jnp.float32), 'Wq': s * jax.random.normal(ks[1], (NH * DK, HS)), 'Wk': s * jax.random.normal(ks[2], (NH * DK, HS)), 'Wv': s * jax.random.normal(ks[3], (NH * DV, HS)), 'Wb': s * jax.random.normal(ks[4], (NH, HS)), 'conv_q_w': s * jax.random.normal(ks[5], (NH * DK, CONV)), 'conv_k_w': s * jax.random.normal(ks[6], (NH * DK, CONV)), 'conv_v_w': s * jax.random.normal(ks[7], (NH * DV, CONV)), 'fir_short_filt': fs, 'fir_long_filt': fl, 'gate_W1': s * jax.random.normal(ks[10], (GH, GIN)), 'gate_b1': jnp.zeros((GH,)), 'gate_W2': s * jax.random.normal(ks[11], (4, GH)), 'gate_b2': jnp.zeros((4,)), 'gate_copy_bias': jnp.full((NH,), 4.0), 'gate_log_temp': jnp.log(jnp.full((NH,), 2.0)), 'o_norm_w': jnp.ones((DV,)), 'Wo': s * jax.random.normal(ks[12], (HS, NH * DV))}
    _L0_attn_in = _L0_attn_setup()

    def _L0_ffn_setup():
        import jax, jax.numpy as jnp
        import numpy as np
        DIM = 128
        NQ = 16
        NKV = 4
        HD = DIM // NQ
        HID = 256
        E = 8
        B, S = (1, 128)
        EPS = 1e-06

        def rmsnorm(x, w):
            ms = jnp.mean(x * x, axis=-1, keepdims=True)
            return w * (x * jax.lax.rsqrt(ms + EPS))

        def rope_tables(seq_len, head_dim):
            inv_freq = 1.0 / 10000.0 ** (jnp.arange(0, head_dim, 2, dtype=jnp.float32) / head_dim)
            t = jnp.arange(seq_len, dtype=jnp.float32)
            freqs = jnp.einsum('i,j->ij', t, inv_freq)
            return (jnp.cos(freqs), jnp.sin(freqs))

        def apply_rope(x, cos, sin):
            c = cos[None, :, None, :]
            s = sin[None, :, None, :]
            half = x.shape[-1] // 2
            x1, x2 = (x[..., :half], x[..., half:])
            return jnp.concatenate([x1 * c - x2 * s, x1 * s + x2 * c], axis=-1)

        def _forward(x, ln1_w, ln2_w, Wq, bq, Wk, bk, Wv, bv, qn_w, kn_w, Wg, bg, Wo, bo, Wr, br, W1, b1, W2, b2):
            batch, seq, _ = x.shape
            cos, sin = rope_tables(seq, HD)
            h = rmsnorm(x, ln1_w)
            q = (h @ Wq + bq).reshape(batch, seq, NQ, HD)
            k = (h @ Wk + bk).reshape(batch, seq, NKV, HD)
            v = (h @ Wv + bv).reshape(batch, seq, NKV, HD)
            q = rmsnorm(apply_rope(q, cos, sin), qn_w)
            k = rmsnorm(apply_rope(k, cos, sin), kn_w)
            rep = NQ // NKV
            k = jnp.repeat(k, rep, axis=2)
            v = jnp.repeat(v, rep, axis=2)
            scores = jnp.einsum('bthd,bshd->bhts', q, k) / np.sqrt(HD)
            causal = jnp.tril(jnp.ones((seq, seq), dtype=bool))
            scores = jnp.where(causal[None, None], scores, -jnp.inf)
            attn = jax.nn.softmax(scores, axis=-1)
            out = jnp.einsum('bhts,bshd->bthd', attn, v)
            gate = jax.nn.sigmoid(out @ Wg + bg)
            out = (out * gate).reshape(batch, seq, DIM)
            x = x + out @ Wo + bo
            h2 = rmsnorm(x, ln2_w)
            logits = h2 @ Wr + br
            top1 = jnp.argmax(logits, axis=-1).reshape(-1)
            xt = h2.reshape(-1, DIM)
            u = jnp.einsum('td,edf->tef', xt, W1) + b1
            u1, u2 = (u[..., :HID], u[..., HID:])
            act = u1 * jax.nn.sigmoid(u2)
            y_all = jnp.einsum('teh,ehd->ted', act, W2) + b2
            y = jnp.take_along_axis(y_all, top1[:, None, None], axis=1)[:, 0, :]
            return x + y.reshape(batch, seq, DIM)
        key = jax.random.key(seed)
        ks = jax.random.split(key, 20)
        sc = lambda fan_in: 1.0 / np.sqrt(fan_in)
        d = {}
        d['x'] = jax.random.normal(ks[0], (B, S, DIM), dtype=jnp.float32)
        d['ln1_w'] = jnp.ones((DIM,), jnp.float32)
        d['ln2_w'] = jnp.ones((DIM,), jnp.float32)
        d['Wq'] = jax.random.normal(ks[1], (DIM, DIM), jnp.float32) * sc(DIM)
        d['bq'] = jnp.zeros((DIM,), jnp.float32)
        d['Wk'] = jax.random.normal(ks[2], (DIM, HD * NKV), jnp.float32) * sc(DIM)
        d['bk'] = jnp.zeros((HD * NKV,), jnp.float32)
        d['Wv'] = jax.random.normal(ks[3], (DIM, HD * NKV), jnp.float32) * sc(DIM)
        d['bv'] = jnp.zeros((HD * NKV,), jnp.float32)
        d['qn_w'] = jnp.ones((HD,), jnp.float32)
        d['kn_w'] = jnp.ones((HD,), jnp.float32)
        d['Wg'] = jax.random.normal(ks[4], (HD, HD), jnp.float32) * sc(HD)
        d['bg'] = jnp.zeros((HD,), jnp.float32)
        d['Wo'] = jax.random.normal(ks[5], (DIM, DIM), jnp.float32) * sc(DIM)
        d['bo'] = jnp.zeros((DIM,), jnp.float32)
        d['Wr'] = jax.random.normal(ks[6], (DIM, E), jnp.float32) * sc(DIM)
        d['br'] = jnp.zeros((E,), jnp.float32)
        d['W1'] = jax.random.normal(ks[7], (E, DIM, 2 * HID), jnp.float32) * sc(DIM)
        d['b1'] = jnp.zeros((E, 2 * HID), jnp.float32)
        d['W2'] = jax.random.normal(ks[8], (E, HID, DIM), jnp.float32) * sc(HID)
        d['b2'] = jnp.zeros((E, DIM), jnp.float32)
        return d
    _L0_ffn_in = _L0_ffn_setup()

    def _L1_attn_setup():
        import jax, jax.numpy as jnp
        import numpy as np
        B, T, D, H = (2, 256, 128, 8)
        HD = D // H
        key = jax.random.key(seed)
        ks = jax.random.split(key, 6)
        s = 1.0 / np.sqrt(D)
        x = jax.random.normal(ks[0], (B, T, D), dtype=jnp.float32)
        Wq = jax.random.normal(ks[1], (D, D), dtype=jnp.float32) * s
        Wk = jax.random.normal(ks[2], (D, D), dtype=jnp.float32) * s
        Wv = jax.random.normal(ks[3], (D, D), dtype=jnp.float32) * s
        Wo = jax.random.normal(ks[4], (D, D), dtype=jnp.float32) * s
        bo = jnp.zeros((D,), dtype=jnp.float32)
        theta = (1.0 / 10000.0 ** (2.0 * jnp.arange(H, dtype=jnp.float32) / H)).astype(jnp.float32)
        gamma = jnp.ones((D,), dtype=jnp.float32)
        beta = jnp.zeros((D,), dtype=jnp.float32)
        return {'x': x, 'Wq': Wq, 'Wk': Wk, 'Wv': Wv, 'Wo': Wo, 'bo': bo, 'theta': theta, 'gamma': gamma, 'beta': beta}
    _L1_attn_in = _L1_attn_setup()

    def _L1_ffn_setup():
        import jax, jax.numpy as jnp
        import numpy as np
        B, S, D, F, E = (4, 256, 128, 512, 8)
        LN_EPS = 1e-05
        key = jax.random.key(seed)
        ks = jax.random.split(key, 6)
        sc = 0.02
        return {'x': jax.random.normal(ks[0], (B, S, D), dtype=jnp.float32), 'Wr': jax.random.normal(ks[1], (D, E), dtype=jnp.float32) * sc, 'br': jnp.zeros((E,), jnp.float32), 'ln_g': jnp.ones((D,), jnp.float32), 'ln_b': jnp.zeros((D,), jnp.float32), 'W1': jax.random.normal(ks[2], (E, D, F), dtype=jnp.float32) * sc, 'b1': jnp.zeros((E, F), jnp.float32), 'W2': jax.random.normal(ks[3], (E, F, D), dtype=jnp.float32) * sc, 'b2': jnp.zeros((E, D), jnp.float32)}
    _L1_ffn_in = _L1_ffn_setup()
    _d = {'L0_attn_hidden_states': _L0_attn_in['hidden_states'], 'L0_attn_Wq': _L0_attn_in['Wq'], 'L0_attn_Wk': _L0_attn_in['Wk'], 'L0_attn_Wv': _L0_attn_in['Wv'], 'L0_attn_Wb': _L0_attn_in['Wb'], 'L0_attn_conv_q_w': _L0_attn_in['conv_q_w'], 'L0_attn_conv_k_w': _L0_attn_in['conv_k_w'], 'L0_attn_conv_v_w': _L0_attn_in['conv_v_w'], 'L0_attn_fir_short_filt': _L0_attn_in['fir_short_filt'], 'L0_attn_fir_long_filt': _L0_attn_in['fir_long_filt'], 'L0_attn_gate_W1': _L0_attn_in['gate_W1'], 'L0_attn_gate_b1': _L0_attn_in['gate_b1'], 'L0_attn_gate_W2': _L0_attn_in['gate_W2'], 'L0_attn_gate_b2': _L0_attn_in['gate_b2'], 'L0_attn_gate_copy_bias': _L0_attn_in['gate_copy_bias'], 'L0_attn_gate_log_temp': _L0_attn_in['gate_log_temp'], 'L0_attn_o_norm_w': _L0_attn_in['o_norm_w'], 'L0_attn_Wo': _L0_attn_in['Wo'], 'L0_ffn_ln1_w': _L0_ffn_in['ln1_w'], 'L0_ffn_ln2_w': _L0_ffn_in['ln2_w'], 'L0_ffn_Wq': _L0_ffn_in['Wq'], 'L0_ffn_bq': _L0_ffn_in['bq'], 'L0_ffn_Wk': _L0_ffn_in['Wk'], 'L0_ffn_bk': _L0_ffn_in['bk'], 'L0_ffn_Wv': _L0_ffn_in['Wv'], 'L0_ffn_bv': _L0_ffn_in['bv'], 'L0_ffn_qn_w': _L0_ffn_in['qn_w'], 'L0_ffn_kn_w': _L0_ffn_in['kn_w'], 'L0_ffn_Wg': _L0_ffn_in['Wg'], 'L0_ffn_bg': _L0_ffn_in['bg'], 'L0_ffn_Wo': _L0_ffn_in['Wo'], 'L0_ffn_bo': _L0_ffn_in['bo'], 'L0_ffn_Wr': _L0_ffn_in['Wr'], 'L0_ffn_br': _L0_ffn_in['br'], 'L0_ffn_W1': _L0_ffn_in['W1'], 'L0_ffn_b1': _L0_ffn_in['b1'], 'L0_ffn_W2': _L0_ffn_in['W2'], 'L0_ffn_b2': _L0_ffn_in['b2'], 'L1_attn_Wq': _L1_attn_in['Wq'], 'L1_attn_Wk': _L1_attn_in['Wk'], 'L1_attn_Wv': _L1_attn_in['Wv'], 'L1_attn_Wo': _L1_attn_in['Wo'], 'L1_attn_bo': _L1_attn_in['bo'], 'L1_attn_theta': _L1_attn_in['theta'], 'L1_attn_gamma': _L1_attn_in['gamma'], 'L1_attn_beta': _L1_attn_in['beta'], 'L1_ffn_Wr': _L1_ffn_in['Wr'], 'L1_ffn_br': _L1_ffn_in['br'], 'L1_ffn_ln_g': _L1_ffn_in['ln_g'], 'L1_ffn_ln_b': _L1_ffn_in['ln_b'], 'L1_ffn_W1': _L1_ffn_in['W1'], 'L1_ffn_b1': _L1_ffn_in['b1'], 'L1_ffn_W2': _L1_ffn_in['W2'], 'L1_ffn_b2': _L1_ffn_in['b2']}
    _x0 = _d['L0_attn_hidden_states']
    _d['L0_attn_hidden_states'] = jax.random.normal(jax.random.fold_in(jax.random.key(seed), 1), (8, 256, 128), dtype=_x0.dtype)
    del _x0
    return _d

def reference(L0_attn_hidden_states, L0_attn_Wq, L0_attn_Wk, L0_attn_Wv, L0_attn_Wb, L0_attn_conv_q_w, L0_attn_conv_k_w, L0_attn_conv_v_w, L0_attn_fir_short_filt, L0_attn_fir_long_filt, L0_attn_gate_W1, L0_attn_gate_b1, L0_attn_gate_W2, L0_attn_gate_b2, L0_attn_gate_copy_bias, L0_attn_gate_log_temp, L0_attn_o_norm_w, L0_attn_Wo, L0_ffn_ln1_w, L0_ffn_ln2_w, L0_ffn_Wq, L0_ffn_bq, L0_ffn_Wk, L0_ffn_bk, L0_ffn_Wv, L0_ffn_bv, L0_ffn_qn_w, L0_ffn_kn_w, L0_ffn_Wg, L0_ffn_bg, L0_ffn_Wo, L0_ffn_bo, L0_ffn_Wr, L0_ffn_br, L0_ffn_W1, L0_ffn_b1, L0_ffn_W2, L0_ffn_b2, L1_attn_Wq, L1_attn_Wk, L1_attn_Wv, L1_attn_Wo, L1_attn_bo, L1_attn_theta, L1_attn_gamma, L1_attn_beta, L1_ffn_Wr, L1_ffn_br, L1_ffn_ln_g, L1_ffn_ln_b, L1_ffn_W1, L1_ffn_b1, L1_ffn_W2, L1_ffn_b2):

    def _L0_attn_ref(hidden_states, Wq, Wk, Wv, Wb, conv_q_w, conv_k_w, conv_v_w, fir_short_filt, fir_long_filt, gate_W1, gate_b1, gate_W2, gate_b2, gate_copy_bias, gate_log_temp, o_norm_w, Wo):
        import jax, jax.numpy as jnp
        import numpy as np
        from jax import lax
        B, L, HS = (4, 512, 128)
        NH, DK, DV = (4, 32, 32)
        CONV, CHUNK, FIRS, FIRL = (4, 32, 5, 64)
        GIN, GH = (HS + 16, HS * 2 // 2)
        DECAY = 1.0 - 1.0 / 3000.0
        EPS_FLOOR = 0.08 * DECAY
        RMS_EPS = 1e-05

        def _l2norm(x):
            return x * lax.rsqrt(jnp.sum(x * x, -1, keepdims=True) + 1e-06)

        def _dwconv_causal(x, filt):
            K = filt.shape[-1]
            xf = jnp.transpose(x, (0, 2, 1))
            xf = jnp.pad(xf, ((0, 0), (0, 0), (K - 1, 0)))
            y = lax.conv_general_dilated(xf, filt[:, None, :], (1,), 'VALID', feature_group_count=filt.shape[0], dimension_numbers=('NCH', 'OIH', 'NCH'))
            return jnp.transpose(y, (0, 2, 1))

        def _delta_rule_chunkwise(q, k, v, beta, chunk=CHUNK):
            b, h, Lq, dk = q.shape
            dv = v.shape[-1]
            n = Lq // chunk
            q = _l2norm(q)
            k = _l2norm(k)
            v = v * beta[..., None]
            kb = k * beta[..., None]
            r = lambda x: x.reshape(b, h, n, chunk, -1)
            q, k, v, kb = (r(q), r(k), r(v), r(kb))
            strict_low = jnp.tril(jnp.ones((chunk, chunk), bool), -1)
            A = jnp.where(strict_low, -jnp.einsum('bhnid,bhnjd->bhnij', kb, k), 0.0)
            eye = jnp.eye(chunk, dtype=q.dtype)
            T = jax.scipy.linalg.solve_triangular(eye - A, jnp.broadcast_to(eye, A.shape), lower=True, unit_diagonal=True)
            u = T @ v
            w = T @ kb
            low = jnp.tril(jnp.ones((chunk, chunk), bool))

            def step(S, inp):
                qi, ki, ui, wi = inp
                attn = jnp.where(low, jnp.einsum('bhid,bhjd->bhij', qi, ki), 0.0)
                u_i = ui - wi @ S
                o_i = qi @ S + attn @ u_i
                S = S + jnp.einsum('bhcd,bhce->bhde', ki, u_i)
                return (S, o_i)
            mv = lambda x: jnp.moveaxis(x, 2, 0)
            S0 = jnp.zeros((b, h, dk, dv), q.dtype)
            S, o = lax.scan(step, S0, (mv(q), mv(k), mv(u), mv(w)))
            o = jnp.moveaxis(o, 0, 2).reshape(b, h, Lq, dv)
            return (o, S)

        def _stats(x):
            mean = jnp.mean(x, -1, keepdims=True)
            var = jnp.var(x, -1, keepdims=True)
            am = jnp.mean(jnp.abs(x), -1, keepdims=True)
            l2 = jnp.linalg.norm(x, axis=-1, keepdims=True)
            return jnp.concatenate([mean, var, am, l2], -1)
        b, l, _ = hidden_states.shape
        silu = jax.nn.silu
        q = silu(_dwconv_causal(hidden_states @ Wq.T, conv_q_w))
        k = silu(_dwconv_causal(hidden_states @ Wk.T, conv_k_w))
        v = silu(_dwconv_causal(hidden_states @ Wv.T, conv_v_w))
        beta = jax.nn.sigmoid(hidden_states @ Wb.T)
        qh = q.reshape(b, l, NH, DK).transpose(0, 2, 1, 3)
        kh = k.reshape(b, l, NH, DK).transpose(0, 2, 1, 3)
        vh = v.reshape(b, l, NH, DV).transpose(0, 2, 1, 3)
        o_d, _S = _delta_rule_chunkwise(qh, kh, vh, beta.transpose(0, 2, 1))
        o_d = o_d.transpose(0, 2, 1, 3)
        v_direct = v.reshape(b, l, NH, DV)
        vc = v_direct.reshape(b, l, NH * DV)
        fir_s = _dwconv_causal(vc, fir_short_filt.reshape(NH * DV, FIRS)).reshape(b, l, NH, DV)
        fir_l = _dwconv_causal(vc, fir_long_filt.reshape(NH * DV, FIRL)).reshape(b, l, NH, DV)
        stats = jnp.concatenate([_stats(fir_s), _stats(fir_l), _stats(o_d), _stats(v_direct)], -1)
        gin = jnp.concatenate([jnp.broadcast_to(hidden_states[:, :, None, :], (b, l, NH, HS)), stats], -1)
        h1 = jax.nn.gelu(gin @ gate_W1.T + gate_b1)
        logits = h1 @ gate_W2.T + gate_b2
        bias_val = gate_copy_bias * DECAY
        logits = logits + bias_val[None, None, :, None] * jnp.array([0.0, 0.0, 0.0, 1.0], logits.dtype)
        temp = jnp.exp(gate_log_temp)
        wgt = jax.nn.softmax(logits / temp[None, None, :, None], -1)
        wgt = wgt * (1.0 - 4.0 * EPS_FLOOR) + EPS_FLOOR
        o = wgt[..., 0:1] * fir_s + wgt[..., 1:2] * fir_l + wgt[..., 2:3] * o_d + wgt[..., 3:4] * v_direct
        o = o * lax.rsqrt(jnp.mean(o * o, -1, keepdims=True) + RMS_EPS) * o_norm_w
        return o.reshape(b, l, NH * DV) @ Wo.T

    def _L0_ffn_ref(x, ln1_w, ln2_w, Wq, bq, Wk, bk, Wv, bv, qn_w, kn_w, Wg, bg, Wo, bo, Wr, br, W1, b1, W2, b2):
        import jax, jax.numpy as jnp
        import numpy as np
        DIM = 128
        NQ = 16
        NKV = 4
        HD = DIM // NQ
        HID = 256
        E = 8
        B, S = (1, 128)
        EPS = 1e-06

        def rmsnorm(x, w):
            ms = jnp.mean(x * x, axis=-1, keepdims=True)
            return w * (x * jax.lax.rsqrt(ms + EPS))

        def rope_tables(seq_len, head_dim):
            inv_freq = 1.0 / 10000.0 ** (jnp.arange(0, head_dim, 2, dtype=jnp.float32) / head_dim)
            t = jnp.arange(seq_len, dtype=jnp.float32)
            freqs = jnp.einsum('i,j->ij', t, inv_freq)
            return (jnp.cos(freqs), jnp.sin(freqs))

        def apply_rope(x, cos, sin):
            c = cos[None, :, None, :]
            s = sin[None, :, None, :]
            half = x.shape[-1] // 2
            x1, x2 = (x[..., :half], x[..., half:])
            return jnp.concatenate([x1 * c - x2 * s, x1 * s + x2 * c], axis=-1)

        def _forward(x, ln1_w, ln2_w, Wq, bq, Wk, bk, Wv, bv, qn_w, kn_w, Wg, bg, Wo, bo, Wr, br, W1, b1, W2, b2):
            batch, seq, _ = x.shape
            cos, sin = rope_tables(seq, HD)
            h = rmsnorm(x, ln1_w)
            q = (h @ Wq + bq).reshape(batch, seq, NQ, HD)
            k = (h @ Wk + bk).reshape(batch, seq, NKV, HD)
            v = (h @ Wv + bv).reshape(batch, seq, NKV, HD)
            q = rmsnorm(apply_rope(q, cos, sin), qn_w)
            k = rmsnorm(apply_rope(k, cos, sin), kn_w)
            rep = NQ // NKV
            k = jnp.repeat(k, rep, axis=2)
            v = jnp.repeat(v, rep, axis=2)
            scores = jnp.einsum('bthd,bshd->bhts', q, k) / np.sqrt(HD)
            causal = jnp.tril(jnp.ones((seq, seq), dtype=bool))
            scores = jnp.where(causal[None, None], scores, -jnp.inf)
            attn = jax.nn.softmax(scores, axis=-1)
            out = jnp.einsum('bhts,bshd->bthd', attn, v)
            gate = jax.nn.sigmoid(out @ Wg + bg)
            out = (out * gate).reshape(batch, seq, DIM)
            x = x + out @ Wo + bo
            h2 = rmsnorm(x, ln2_w)
            logits = h2 @ Wr + br
            top1 = jnp.argmax(logits, axis=-1).reshape(-1)
            xt = h2.reshape(-1, DIM)
            u = jnp.einsum('td,edf->tef', xt, W1) + b1
            u1, u2 = (u[..., :HID], u[..., HID:])
            act = u1 * jax.nn.sigmoid(u2)
            y_all = jnp.einsum('teh,ehd->ted', act, W2) + b2
            y = jnp.take_along_axis(y_all, top1[:, None, None], axis=1)[:, 0, :]
            return x + y.reshape(batch, seq, DIM)
        return _forward(x, ln1_w, ln2_w, Wq, bq, Wk, bk, Wv, bv, qn_w, kn_w, Wg, bg, Wo, bo, Wr, br, W1, b1, W2, b2)

    def _L1_attn_ref(x, Wq, Wk, Wv, Wo, bo, theta, gamma, beta):
        import jax, jax.numpy as jnp
        import numpy as np
        B, T, D, H = (2, 256, 128, 8)
        HD = D // H
        b, t, d = x.shape
        h = theta.shape[0]
        hd = d // h
        q = (x @ Wq).reshape(b, t, h, hd)
        k = (x @ Wk).reshape(b, t, h, hd)
        v = (x @ Wv).reshape(b, t, h, hd)
        pos = jnp.arange(t, dtype=jnp.float32)
        n = pos[:, None] - pos[None, :]
        nn = jnp.maximum(n, 0.0)
        decay_mask = jnp.where(n >= 0, jnp.mean(jnp.exp(-theta[None, None, :] * nn[:, :, None]), axis=-1), 0.0)
        scores = jnp.einsum('bthd,bshd->bths', q, k) / np.sqrt(hd)
        scores = scores * decay_mask[None, :, None, :]
        causal = (n >= 0)[None, :, None, :]
        scores = jnp.where(causal, scores, -jnp.inf)
        retention = jax.nn.softmax(scores, axis=-1)
        out = jnp.einsum('bths,bshd->bthd', retention, v)
        mu = out.mean(axis=-1, keepdims=True)
        var = out.var(axis=-1, keepdims=True)
        out = (out - mu) / jnp.sqrt(var + 1e-05)
        out = out.reshape(b, t, d) * gamma + beta
        return out @ Wo + bo

    def _L1_ffn_ref(x, Wr, br, ln_g, ln_b, W1, b1, W2, b2):
        import jax, jax.numpy as jnp
        import numpy as np
        B, S, D, F, E = (4, 256, 128, 512, 8)
        LN_EPS = 1e-05
        tokens_shape = x.shape[:-1]
        xt = x.reshape(-1, x.shape[-1])
        router_logits = xt @ Wr + br
        router_probs = jax.nn.softmax(router_logits, axis=-1)
        gates = jnp.max(router_probs, axis=-1, keepdims=True)
        idx = jnp.argmax(router_probs, axis=-1)
        onehot = jax.nn.one_hot(idx, E, dtype=xt.dtype)
        mu = jnp.mean(xt, axis=-1, keepdims=True)
        var = jnp.mean(jnp.square(xt - mu), axis=-1, keepdims=True)
        xn = (xt - mu) * jax.lax.rsqrt(var + LN_EPS) * ln_g + ln_b
        h = jnp.einsum('te,td,edf->tf', onehot, xn, W1) + b1[idx]
        h = jax.nn.relu(h)
        y = jnp.einsum('te,tf,efd->td', onehot, h, W2) + b2[idx]
        y = y * gates
        return y.reshape(tokens_shape + (y.shape[-1],))
    x = L0_attn_hidden_states
    x = _layernorm(x + _L0_attn_ref(x, L0_attn_Wq, L0_attn_Wk, L0_attn_Wv, L0_attn_Wb, L0_attn_conv_q_w, L0_attn_conv_k_w, L0_attn_conv_v_w, L0_attn_fir_short_filt, L0_attn_fir_long_filt, L0_attn_gate_W1, L0_attn_gate_b1, L0_attn_gate_W2, L0_attn_gate_b2, L0_attn_gate_copy_bias, L0_attn_gate_log_temp, L0_attn_o_norm_w, L0_attn_Wo), axis=-1)
    x = _layernorm(x + _L0_ffn_ref(x, L0_ffn_ln1_w, L0_ffn_ln2_w, L0_ffn_Wq, L0_ffn_bq, L0_ffn_Wk, L0_ffn_bk, L0_ffn_Wv, L0_ffn_bv, L0_ffn_qn_w, L0_ffn_kn_w, L0_ffn_Wg, L0_ffn_bg, L0_ffn_Wo, L0_ffn_bo, L0_ffn_Wr, L0_ffn_br, L0_ffn_W1, L0_ffn_b1, L0_ffn_W2, L0_ffn_b2), axis=-1)
    x = _layernorm(x + _L1_attn_ref(x, L1_attn_Wq, L1_attn_Wk, L1_attn_Wv, L1_attn_Wo, L1_attn_bo, L1_attn_theta, L1_attn_gamma, L1_attn_beta), axis=-1)
    x = _layernorm(x + _L1_ffn_ref(x, L1_ffn_Wr, L1_ffn_br, L1_ffn_ln_g, L1_ffn_ln_b, L1_ffn_W1, L1_ffn_b1, L1_ffn_W2, L1_ffn_b2), axis=-1)
    return x

_drawn_inputs = setup_inputs


def setup_inputs(seed=0):
    import zlib

    import numpy as np

    out = dict(_drawn_inputs(seed))
    spreads = {'L0_attn_gate_b1': (0.0, 0.8),
     'L0_attn_gate_b2': (0.0, 0.634),
     'L0_attn_gate_copy_bias': (4.0, 0.6),
     'L0_attn_gate_log_temp': (0.6931471824645996, 0.6),
     'L0_attn_o_norm_w': (1.0, 0.2),
     'L0_ffn_ln1_w': (1.0, 0.2),
     'L0_ffn_ln2_w': (1.0, 0.2),
     'L0_ffn_bq': (0.0, 0.1),
     'L0_ffn_bk': (0.0, 0.1),
     'L0_ffn_bv': (0.0, 0.1),
     'L0_ffn_qn_w': (1.0, 0.2),
     'L0_ffn_kn_w': (1.0, 0.2),
     'L0_ffn_bg': (0.0, 0.314),
     'L0_ffn_bo': (0.0, 0.1),
     'L0_ffn_br': (0.0, 0.1),
     'L0_ffn_b1': (0.0, 0.1),
     'L0_ffn_b2': (0.0, 0.1),
     'L1_attn_bo': (0.0, 0.1),
     'L1_attn_gamma': (1.0, 0.2),
     'L1_attn_beta': (0.0, 0.1),
     'L1_ffn_br': (0.0, 0.529),
     'L1_ffn_ln_g': (1.0, 0.6),
     'L1_ffn_ln_b': (0.0, 0.8),
     'L1_ffn_b1': (0.0, 0.8),
     'L1_ffn_b2': (0.0, 0.458)}
    factors = {'L0_attn_Wb': 3.491,
     'L0_attn_gate_W1': 6.37,
     'L0_attn_gate_W2': 6.378,
     'L1_attn_theta': 8.0,
     'L1_ffn_Wr': 2.699,
     'L1_ffn_W1': 5.301,
     'L1_ffn_W2': 4.109}
    for name, (base, spread) in spreads.items():
        noise = np.random.default_rng([zlib.crc32(name.encode()), seed]).standard_normal(out[name].shape)
        drawn = base * np.exp(spread * noise) if base else spread * noise
        out[name] = jnp.asarray(drawn.astype(out[name].dtype))
    for name, factor in factors.items():
        out[name] = (out[name] * factor).astype(out[name].dtype)
    return out
```

```python
from contextlib import ExitStack

import numpy as np
import concourse.bass as bass
from concourse import mybir

F32 = mybir.dt.float32
BF16 = mybir.dt.bfloat16
I32 = mybir.dt.int32
U32 = mybir.dt.uint32
ALU = mybir.AluOpType
ACT = mybir.ActivationFunctionType
X = mybir.AxisListType.X

P = 128
BATCH, SEQ, D = 8, 256, 128
TOKENS = BATCH * SEQ
TILES = TOKENS // P
GT = 4
GTOK = GT * P
GB = GTOK // SEQ
GROUPS = TOKENS // GTOK
H0, DK = 4, 32
CHUNK = 32
GCH = GTOK // CHUNK
SCH = SEQ // CHUNK
CONV, FIRS, FIRL = 4, 5, 64
FBLK = TOKENS // FIRL
NBR, NSTAT = 4, 4
DECAY = 1.0 - 1.0 / 3000.0
EPS_FLOOR = 0.08 * DECAY
NQ, NKV, HD0 = 16, 4, 8
REP = NQ // NKV
H1, HD1 = 8, 16
E = 8
SLOT_TILES = TILES + E
NEG = -30000.0

CONST_PARTS = [("ident", 128), ("block_ones", 128), ("before", 128), ("ones", 128), ("neg_st", 128), ("neg_ts", 128),
               ("minus_lower", 32), ("causal_t", 32), ("cos", 8), ("sin", 8), ("lag", 384), ("lag_ok", 384),
               ("tile_starts", 16), ("experts", 8), ("slots", SLOT_TILES), ("head_ones", 128)]
CONST_AT, _n = {}, 0
for _name, _w in CONST_PARTS:
    CONST_AT[_name] = (_n, _n + _w)
    _n += _w
CONST_W = _n


def constants():
    c = np.zeros((P, CONST_W), np.float32)

    def put(name, a):
        lo, hi = CONST_AT[name]
        c[:, lo:hi] = a

    i, j = np.arange(P)[:, None], np.arange(P)[None, :]
    put("ident", i == j)
    put("block_ones", i // DK == j // DK)
    put("before", i < j)
    put("head_ones", i // HD0 == j // HD0)
    put("ones", 1.0)
    put("neg_st", np.where(i > j, NEG, 0.0))
    put("neg_ts", np.where(j > i, NEG, 0.0))
    r, k = i % CHUNK, np.arange(CHUNK)[None, :]
    put("minus_lower", np.where(k < r, -1.0, 0.0))
    put("causal_t", k >= r)
    half = HD0 // 2
    freq = (np.float32(1.0) / np.float32(10000.0) ** (np.arange(0, HD0, 2, dtype=np.float32) / np.float32(HD0))).astype(np.float32)
    ang = np.arange(SEQ, dtype=np.float32)[:, None] * freq[None, :]
    put("cos", np.cos(ang).reshape(2, P, half).transpose(1, 0, 2).reshape(P, 8))
    put("sin", np.sin(ang).reshape(2, P, half).transpose(1, 0, 2).reshape(P, 8))
    lag = np.concatenate([i - j, i + P - np.arange(SEQ)[None, :]], 1)
    put("lag", np.maximum(lag, 0))
    put("lag_ok", lag >= 0)
    put("tile_starts", np.arange(16)[None, :] * P)
    put("experts", np.arange(E)[None, :])
    put("slots", np.arange(SLOT_TILES)[None, :])
    return c


SCRATCH = {"taps_padded": (2 * P, P), "sorted0": (SLOT_TILES * P, P), "sorted1": (SLOT_TILES * P, P),
           "expert_out0": (SLOT_TILES * P, P), "expert_out1": (SLOT_TILES * P, P)}


def dump(nc, io, m, name, t):
    if "dump_" + name in io:
        s = m.nc.alloc_semaphore("dump_" + name)
        with nc.Block() as block:
            @block.sync
            def _(sp):
                sp.dma_start(io["dump_" + name], t).then_inc(s, 16)
                sp.wait_ge(s, 16)


def rows(ap, n):
    return bass.AP(ap.tensor, 0, [[0, P], [1, n]])


def last_first(ap):
    *outer, (step, n) = [list(d) for d in ap.ap]
    return bass.AP(ap.tensor, ap.offset + step * (n - 1), [*outer, [-step, n]])


class Chain:

    def __init__(self, eng, done):
        self.eng, self.done, self.n = eng, done, 0

    def link(self, ins):
        self.n += 1
        ins.then_inc(self.done, 1)
        self.eng.wait_ge(self.done, self.n)


class Memory:

    def __init__(self, nc, ctx, stage=""):
        self.nc, self.ctx, self.stage, self.sems = nc, ctx, stage, []

    def sb(self, name, shape, dt=F32):
        return self.ctx.enter_context(self.nc.sbuf_tensor(self.stage + name, list(shape), dt))

    def sem(self, name):
        s = self.nc.alloc_semaphore(self.stage + name)
        self.sems.append(s)
        return s

    def clear(self):
        nums = sorted(s.num for s in self.sems)
        for lo in [n for n in nums if n - 1 not in nums]:
            hi = lo
            while hi in nums:
                hi += 1
            self.nc.sync.sem_clear(range(lo, hi))
        self.nc.all_engine_barrier()
        for s in self.sems:
            self.nc.release_semaphore(s)
        self.sems = []


def build_program(nc, io, out):
    ctx = ExitStack()
    with ctx:
        shared = Memory(nc, ctx)
        psum = ctx.enter_context(nc.psum_tensor("psum", [P, 8, 512], F32))
        banks = [psum[:, i, :] for i in range(8)]
        shared.psum = psum
        cst = shared.sb("cst", [P, CONST_W])
        shared.banks, shared.cst = banks, cst
        shared.c = lambda name: cst[:, CONST_AT[name][0]:CONST_AT[name][1]]
        const_loaded = nc.alloc_semaphore("const_loaded")
        with nc.Block() as block:
            @block.sync
            def _(sp):
                sp.dma_start(cst[:, :], io["consts"]).then_inc(const_loaded, 16)
                sp.wait_ge(const_loaded, 16)
        x1_all = shared.sb("x1_all", [P, TILES, P])
        layer0_mixer(nc, io, shared, x1_all)
        dump(nc, io, shared, "x1", x1_all[:, :, :])
        res_all = shared.sb("res_all", [P, TILES, P])
        h_all = shared.sb("h_all", [P, TILES, P])
        pick_all = shared.sb("pick_all", [P, TILES, E])
        layer0_attention(nc, io, shared, x1_all, res_all, h_all, pick_all)
        dump(nc, io, shared, "res", res_all[:, :, :])
        dump(nc, io, shared, "pick", pick_all[:, :, :])
        y_all = x1_all
        experts(nc, io, shared, 0, h_all, pick_all, y_all)
        prob_all = shared.sb("prob_all", [P, TILES])
        norm_all(nc, io, shared, "norm0_", res_all, y_all, res_all, None, h_all)
        dump(nc, io, shared, "x2", res_all[:, :, :])
        layer1_attention(nc, io, shared, res_all, y_all, h_all, pick_all, prob_all)
        dump(nc, io, shared, "x3", y_all[:, :, :])
        experts(nc, io, shared, 1, h_all, pick_all, res_all)
        norm_all(nc, io, shared, "norm1_", y_all, res_all, h_all, prob_all, y_all, out)


def layer0_mixer(nc, io, m, x1_all):
    banks, c = m.banks, m.c
    with ExitStack() as ctx:
        lay = Memory(nc, ctx)
        x_t = lay.sb("x_t", [P, GROUPS * GB, CONV - 1 + SEQ])
        q_t = lay.sb("q_t", [P, GROUPS, GTOK])
        k_t = lay.sb("k_t", [P, GROUPS, GTOK])
        v_t = lay.sb("v_t", [P, GROUPS * GB, FIRL + SEQ])
        beta_t = lay.sb("beta_t", [P, GROUPS, GTOK])
        fir_long = lay.sb("fir_long", [P, TILES, P])
        project(nc, io, m, x_t, q_t, k_t, v_t, beta_t)
        long_filter(nc, io, m, v_t, fir_long)
        dump(nc, io, m, "q_t", q_t[:, :, :])
        dump(nc, io, m, "v_t", v_t[:, :, :])
        dump(nc, io, m, "fir", fir_long[:, :, :])
        delta_and_gate(nc, io, m, x_t, q_t, k_t, v_t, beta_t, fir_long, x1_all)


def project(nc, io, m, x_t, q_t, k_t, v_t, beta_t):
    banks, c = m.banks, m.c
    with ExitStack() as ctx:
        s = Memory(nc, ctx, "project_")
        w_t = s.sb("w_t", [P, 3, P])
        taps = s.sb("taps", [P, 3, CONV, P])
        w_conv = s.sb("w_conv", [P, 3, CONV, P])
        wb = s.sb("wb", [P, H0])
        wb_rep = s.sb("wb_rep", [P, H0, DK])
        x_in = s.sb("x_in", [P, GT, P])
        loaded, scaled, zeroed = s.sem("weights_loaded"), s.sem("weights_scaled"), s.sem("pads_zeroed")
        with nc.Block() as block:
            @block.sync
            def _(sp):
                for n, name in enumerate(("q", "k", "v")):
                    sp.dma_start(w_t[:, n, :], io[f"W{name}_t"]).then_inc(loaded, 16)
                    sp.dma_start(taps[:, n, :, :], rows(io[f"conv_{name}_t"], CONV * P)).then_inc(loaded, 16)
                sp.dma_start(wb[:, :], io["Wb_t"]).then_inc(loaded, 16)

            @block.gpsimd
            def _(pool):
                nc.gpsimd.memset(x_t[:, :, 0:CONV - 1], 0.0)
                nc.gpsimd.memset(v_t[:, :, 0:FIRL], 0.0).then_inc(zeroed, 1)

            @block.vector
            def _(dve):
                dve.wait_ge(loaded, 7 * 16)
                for n in range(3):
                    nc.vector.tensor_tensor(w_conv[:, n, :, :], w_t[:, n, :].unsqueeze(1).broadcast_to([P, CONV, P]),
                                            taps[:, n, :, :], ALU.mult)
                nc.vector.tensor_copy(wb_rep[:, :, :], wb[:, :].unsqueeze(2).broadcast_to([P, H0, DK])).then_inc(scaled, 1)
        s.clear()
        with nc.Fori(0, GROUPS) as g:
            x_here, x_turned, x_kept = s.sem("x_here"), s.sem("x_turned"), s.sem("x_kept")
            projected = s.sem("projected")
            with nc.Block() as block:
                @block.sync
                def _(sp):
                    sp.dma_start(x_in[:, :, :], io["x"][bass.ds(g * GTOK, GTOK), :].rearrange("(n p) d -> p n d", p=P)).then_inc(x_here, 16)

                @block.tensor
                def _(pe):
                    pe.wait_ge(x_here, 16)
                    for t in range(GT):
                        last = nc.tensor.transpose(banks[0][:, t * P:(t + 1) * P], x_in[:, t, :], c("ident"))
                    last.then_inc(x_turned, 1)
                    pe.wait_ge(x_kept, 1)
                    for n in range(3):
                        for j in range(CONV):
                            last = nc.tensor.matmul(banks[1 + n][:, :], w_conv[:, n, j, :], x_t[:, bass.ds(g * GB, GB), j:j + SEQ],
                                                    start=(j == 0), stop=(j == CONV - 1))
                        last.then_inc(projected, 1)
                    nc.tensor.matmul(banks[4][:, :], wb_rep[:, :, :], x_t[:, bass.ds(g * GB, GB), CONV - 1:CONV - 1 + SEQ],
                                     start=True, stop=True).then_inc(projected, 1)

                @block.scalar
                def _(act):
                    act.wait_ge(x_turned, 1)
                    nc.scalar.copy(x_t[:, bass.ds(g * GB, GB), CONV - 1:], banks[0][:, :].rearrange("p (b t) -> p b t", b=GB)).then_inc(x_kept, 1)
                    act.wait_ge(projected, 1)
                    nc.scalar.activation(q_t[:, bass.ds(g, 1), :], banks[1][:, :].unsqueeze(1), ACT.Silu)
                    act.wait_ge(projected, 2)
                    nc.scalar.activation(k_t[:, bass.ds(g, 1), :], banks[2][:, :].unsqueeze(1), ACT.Silu)
                    act.wait_ge(projected, 3)
                    nc.scalar.activation(v_t[:, bass.ds(g * GB, GB), FIRL:], banks[3][:, :].rearrange("p (b t) -> p b t", b=GB), ACT.Silu)
                    act.wait_ge(projected, 4)
                    nc.scalar.activation(beta_t[:, bass.ds(g, 1), :], banks[4][:, :].unsqueeze(1), ACT.Sigmoid)
            s.clear()


def long_filter(nc, io, m, v_t, fir_long):
    banks, c = m.banks, m.c
    with ExitStack() as ctx:
        s = Memory(nc, ctx, "filter_")
        tri = s.sb("tri", [P, P, FIRL])
        win = s.sb("win", [P, P, FBLK])
        taps = s.sb("taps", [P, P])
        taps_here, taps_zeroed, taps_out = s.sem("taps_here"), s.sem("taps_zeroed"), s.sem("taps_out")
        tri_here = s.sem("tri_here")
        turned, kept, filtered, used = s.sem("turned"), s.sem("kept"), s.sem("filtered"), s.sem("used")
        reversed_ = s.sem("reversed")
        v_back = s.sb("v_back", [P, (TOKENS // SEQ) * (FIRL + SEQ)])
        pad = io["taps_padded"]

        def unload(eng, copy, first):
            for k in range(first, 8, 2):
                eng.wait_ge(filtered, k + 1)
                for half in range(2):
                    copy(fir_long[64 * half:64 * half + 64, :, 16 * k:16 * k + 16],
                         banks[k][0:64, :].rearrange("p (c t h) -> p t c h", c=16, h=2)[:, :, :, half])

        with nc.Block() as block:
            @block.sync
            def _(sp):
                sp.wait_ge(taps_zeroed, 1)
                sp.dma_start(taps[:, 0:FIRL], io["fir_long_rev"]).then_inc(taps_here, 16)
                sp.wait_ge(taps_here, 16)
                sp.dma_start(pad[P:2 * P, :], taps[:, :]).then_inc(taps_out, 16)
                sp.dma_start(pad[0:P, FIRL:P], taps[:, FIRL:P]).then_inc(taps_out, 16)
                sp.wait_ge(taps_out, 32)
                for q in range(4):
                    sp.dma_start(tri[32 * q:32 * q + 32, :, :],
                                 bass.AP(pad.tensor, P * P + 1 - FIRL + 32 * q, [[1, 32], [P, P], [1, FIRL]])).then_inc(tri_here, 16)

            @block.vector
            def _(dve):
                nc.vector.memset(taps[:, :], 0.0).then_inc(taps_zeroed, 1)
                nc.vector.tensor_copy(v_back[:, :], last_first(v_t[:, :, :].rearrange("p b t -> p (b t)"))).then_inc(reversed_, 1)
                for w in range(0, FBLK, 8):
                    dve.wait_ge(turned, w // 4 + 2)
                    for k in range(2):
                        b = (w // 4 + k) % 4
                        nc.vector.tensor_copy(win[:, :, w + 4 * k:w + 4 * k + 4],
                                              banks[b][:, :].rearrange("p (w c) -> p c w", w=4)).then_inc(kept, 1)
                unload(dve, nc.vector.tensor_copy, 0)

            @block.scalar
            def _(act):
                unload(act, nc.scalar.copy, 1)

            @block.tensor
            def _(pe):
                pe.wait_ge(reversed_, 1)
                for w in range(FBLK):
                    if w >= 16 and w % 4 == 0:
                        pe.wait_ge(kept, w // 4 - 3)
                    end, at = (TOKENS // SEQ) * (FIRL + SEQ), (w // 4) * (FIRL + SEQ) + FIRL * (w % 4)
                    last = nc.tensor.transpose(banks[(w // 4) % 4][:, (w % 4) * P:(w % 4 + 1) * P], v_back[:, end - at - P:end - at], c("ident"))
                    if w % 4 == 3:
                        last.then_inc(turned, 1)
                pe.wait_ge(kept, 8)
                pe.wait_ge(tri_here, 64)
                for ch in range(P):
                    last = nc.tensor.matmul(banks[ch // 16][0:64, (ch % 16) * FBLK:(ch % 16 + 1) * FBLK],
                                            tri[:, ch, :], win[:, ch, :], start=True, stop=True)
                    if ch % 16 == 15:
                        last.then_inc(filtered, 1)
        s.clear()


def head_block(t, h, width=CHUNK):
    return t[h * width:(h + 1) * width, :, h * width:(h + 1) * width]


def delta_and_gate(nc, io, m, x_t, q_t, k_t, v_t, beta_t, fir_long, x1_all):
    banks, c = m.banks, m.c
    with ExitStack() as ctx:
        s = Memory(nc, ctx, "mixer_")
        w1_x, w1_s, w2_t = s.sb("w1_x", [P, P]), s.sb("w1_s", [P, P]), s.sb("w2_t", [P, NBR])
        b1, wo, o_norm = s.sb("b1", [P, 1]), s.sb("wo", [P, P]), s.sb("o_norm", [P, 1])
        taps, tap_diag = s.sb("taps", [P, FIRS]), s.sb("tap_diag", [P, FIRS, P])
        b2, copy_bias, log_temp = s.sb("b2", [P, NBR]), s.sb("copy_bias", [P, H0]), s.sb("log_temp", [P, H0])
        logit_bias, inv_temp = s.sb("logit_bias", [P, H0, NBR]), s.sb("inv_temp", [P, H0])
        bd_q, bd_k, bd_kb, bd_ktok, bd_attn = (s.sb(n, [P, GCH, P]) for n in ("bd_q", "bd_k", "bd_kb", "bd_ktok", "bd_attn"))
        bd_pow = [s.sb(f"bd_pow{n}", [P, GCH, P]) for n in range(2)]
        bd_w = bd_kb
        q_n, k_n, kb_n, vb_n = (s.sb(n, [P, GTOK]) for n in ("q_n", "k_n", "kb_n", "vb_n"))
        sq_q, sq_k = s.sb("sq_q", [P, GTOK]), s.sb("sq_k", [P, GTOK])
        power = [s.sb(f"power{n}", [P, GTOK]) for n in range(2)]
        rhs = s.sb("rhs", [P, GCH, 2 * DK])
        state = s.sb("state", [P, GB, DK])
        od_t = s.sb("od_t", [P, GTOK])
        v_s = s.sb("v_s", [P, GB, FIRL + SEQ])
        branch, branch_sq = s.sb("branch", [P, NBR, GTOK]), s.sb("branch_sq", [P, NBR, GTOK])
        sums = s.sb("sums", [P, 6, NBR * GT * H0])
        stats = s.sb("stats", [P, GT, H0, 8, NSTAT])
        stats_t = s.sb("stats_t", [P, GTOK])
        hidden = s.sb("hidden", [P, H0, GTOK])
        gate = [s.sb(f"gate{n}", [P, GT * H0, NBR]) for n in range(2)]
        small = s.sb("small", [P, 8, GT * H0])
        mixed, mixed_t = s.sb("mixed", [P, GTOK]), s.sb("mixed_t", [P, GTOK])
        x_in = s.sb("x_in", [P, GT, P])
        loaded, cleared, dve_done, temp_done = s.sem("loaded"), s.sem("cleared"), s.sem("dve_done"), s.sem("temp_done")
        w1s_zeroed = s.sem("w1s_zeroed")
        with nc.Block() as block:
            @block.sync
            def _(sp):
                sp.wait_ge(w1s_zeroed, 1)
                for dst, src in ((w1_x, "gate_w1x_t"), (w2_t, "gate_w2_t"), (wo, "Wo_t"), (taps, "fir_short"), (b1, "gate_b1")):
                    sp.dma_start(dst[:, :], io[src]).then_inc(loaded, 16)
                for h in range(H0):
                    sp.dma_start(w1_s[32 * h:32 * h + 16, :], io["gate_w1s_t"]).then_inc(loaded, 16)
                    sp.dma_start(o_norm[32 * h:32 * h + 32, :], io["o_norm"]).then_inc(loaded, 16)
                for dst, src, n in ((b2, "gate_b2", NBR), (copy_bias, "copy_bias", H0), (log_temp, "log_temp", H0)):
                    sp.dma_start(dst[:, :], rows(io[src], n)).then_inc(loaded, 16)

            @block.gpsimd
            def _(pool):
                nc.gpsimd.memset(w1_s[:, :], 0.0).then_inc(w1s_zeroed, 1)
                for t in (bd_q, bd_k, bd_kb, bd_ktok, bd_attn, *bd_pow):
                    nc.gpsimd.memset(t[:, :, :], 0.0)
                nc.gpsimd.memset(stats[:, :, :, :, :], 0.0)

            @block.scalar
            def _(act):
                act.wait_ge(loaded, 16 * 16)
                nc.scalar.activation(inv_temp[:, :], log_temp[:, :], ACT.Exp, scale=-1.0)

            @block.vector
            def _(dve):
                dve.wait_ge(loaded, 16 * 16)
                ch = Chain(dve, dve_done)
                for j in range(FIRS):
                    nc.vector.tensor_scalar(tap_diag[:, j, :], c("ident"), taps[:, j:j + 1], None, ALU.mult)
                ch.link(nc.vector.tensor_copy(logit_bias[:, :, :], b2[:, :].unsqueeze(1).broadcast_to([P, H0, NBR])))
                nc.vector.scalar_tensor_tensor(logit_bias[:, :, 3], copy_bias[:, :], DECAY, logit_bias[:, :, 3], ALU.mult, ALU.add)
                nc.vector.tensor_scalar(wo[:, :], wo[:, :], o_norm[:, 0:1], None, ALU.mult)
        s.clear()

        with nc.Fori(0, GROUPS) as g:
            squared, summed, floored, rooted = s.sem("squared"), s.sem("summed"), s.sem("floored"), s.sem("rooted")
            keyed, v_kept, x_here = s.sem("keyed"), s.sem("v_kept"), s.sem("x_here")
            d_done = s.sem("d_done")
            with nc.Block() as block:
                @block.sync
                def _(sp):
                    sp.dma_start(x_in[:, :, :], io["x"][bass.ds(g * GTOK, GTOK), :].rearrange("(n p) d -> p n d", p=P)).then_inc(x_here, 16)
                    sp.wait_ge(x_here, 16)

                @block.scalar
                def _(act):
                    nc.scalar.activation(sq_q[:, :].unsqueeze(1), q_t[:, bass.ds(g, 1), :], ACT.Square).then_inc(squared, 1)
                    nc.scalar.activation(sq_k[:, :].unsqueeze(1), k_t[:, bass.ds(g, 1), :], ACT.Square).then_inc(squared, 1)
                    nc.scalar.copy(v_s[:, :, :], v_t[:, bass.ds(g * GB, GB), :])
                    for n, t in enumerate((sq_q, sq_k)):
                        act.wait_ge(floored, n + 1)
                        nc.scalar.activation(t[:, :], t[:, :], ACT.Sqrt).then_inc(rooted, 1)

                @block.tensor
                def _(pe):
                    for n, t in enumerate((sq_q, sq_k)):
                        pe.wait_ge(squared, n + 1)
                        nc.tensor.matmul(banks[n][:, :], c("block_ones"), t[:, :], start=True, stop=True).then_inc(summed, 1)

                @block.vector
                def _(dve):
                    ch = Chain(dve, d_done)
                    for n, t in enumerate((sq_q, sq_k)):
                        dve.wait_ge(summed, n + 1)
                        nc.vector.tensor_scalar(t[:, :], banks[n][:, :], 1e-6, None, ALU.add).then_inc(floored, 1)
                    for n, (t, src, dst) in enumerate(((sq_q, q_t, q_n), (sq_k, k_t, k_n))):
                        dve.wait_ge(rooted, n + 1)
                        ch.link(nc.vector.reciprocal(t[:, :], t[:, :]))
                        ch.link(nc.vector.tensor_tensor(dst[:, :].unsqueeze(1), t[:, :].unsqueeze(1), src[:, bass.ds(g, 1), :], ALU.mult))
                    ch.link(nc.vector.tensor_tensor(kb_n[:, :].unsqueeze(1), k_n[:, :].unsqueeze(1), beta_t[:, bass.ds(g, 1), :], ALU.mult))
                    ch.link(nc.vector.tensor_tensor(vb_n[:, :].rearrange("p (b t) -> p b t", b=GB), v_t[:, bass.ds(g * GB, GB), FIRL:],
                                                    beta_t[:, bass.ds(g, 1), :].rearrange("p o (b t) -> p (o b) t", b=GB), ALU.mult))
                    nc.vector.transpose(rhs[:, :, 0:DK], vb_n[:, :])
                    nc.vector.transpose(rhs[:, :, DK:], kb_n[:, :])
                    for h in range(H0):
                        last = nc.vector.transpose(head_block(bd_ktok, h), k_n[32 * h:32 * h + 32, :])
                    last.then_inc(keyed, 1)

                @block.gpsimd
                def _(pool):
                    pool.wait_ge(d_done, 5)
                    for t, bd in ((k_n, bd_k), (q_n, bd_q), (kb_n, bd_kb)):
                        for h in range(H0):
                            nc.gpsimd.tensor_copy(head_block(bd, h), t[32 * h:32 * h + 32, :].rearrange("p (n t) -> p n t", n=GCH))

            produced, powered, kept, applied, added = s.sem("produced"), s.sem("powered"), s.sem("kept"), s.sem("applied"), s.sem("added")
            attended, a_done = s.sem("attended"), s.sem("a_done")
            with nc.Block() as block:
                @block.tensor
                def _(pe):
                    for n in range(GCH):
                        last = nc.tensor.matmul(banks[0][:, n * CHUNK:(n + 1) * CHUNK], bd_kb[:, n, :], k_n[:, n * CHUNK:(n + 1) * CHUNK],
                                                start=True, stop=True)
                    last.then_inc(produced, 1)
                    for n in range(GCH):
                        last = nc.tensor.matmul(banks[4][:, n * CHUNK:(n + 1) * CHUNK], bd_k[:, n, :], q_n[:, n * CHUNK:(n + 1) * CHUNK],
                                                start=True, stop=True)
                    last.then_inc(attended, 1)
                    for lv in range(5):
                        pe.wait_ge(kept, lv + 1)
                        if lv < 4:
                            for n in range(GCH):
                                last = nc.tensor.matmul(banks[(lv + 1) % 2][:, n * CHUNK:(n + 1) * CHUNK], bd_pow[lv % 2][:, n, :],
                                                        power[lv % 2][:, n * CHUNK:(n + 1) * CHUNK], start=True, stop=True)
                            last.then_inc(produced, 1)
                        if lv:
                            pe.wait_ge(added, lv)
                        for n in range(GCH):
                            last = nc.tensor.matmul(banks[2 + n // 8][:, (n % 8) * 2 * DK:(n % 8 + 1) * 2 * DK], bd_pow[lv % 2][:, n, :],
                                                    rhs[:, n, :], start=True, stop=True)
                        last.then_inc(applied, 1)

                @block.vector
                def _(dve):
                    ch = Chain(dve, a_done)
                    for lv in range(5):
                        dve.wait_ge(produced, lv + 1)
                        if lv >= 2:
                            dve.wait_ge(applied, lv - 1)
                        if lv == 0:
                            ch.link(nc.vector.tensor_tensor(power[0][:, :].rearrange("p (n t) -> p n t", n=GCH),
                                                            banks[0][:, :].rearrange("p (n t) -> p n t", n=GCH),
                                                            c("minus_lower").unsqueeze(1).broadcast_to([P, GCH, CHUNK]), ALU.mult))
                        else:
                            ch.link(nc.vector.tensor_copy(power[lv % 2][:, :], banks[lv % 2][:, :]))
                        for h in range(H0):
                            last = nc.vector.transpose(head_block(bd_pow[lv % 2], h), power[lv % 2][32 * h:32 * h + 32, :])
                        last.then_inc(kept, 1)
                        if lv == 0:
                            dve.wait_ge(attended, 1)
                            for h in range(H0):
                                nc.vector.tensor_tensor(head_block(bd_attn, h), banks[4][32 * h:32 * h + 32, :].rearrange("p (n t) -> p n t", n=GCH),
                                                        c("causal_t")[32 * h:32 * h + 32, :].unsqueeze(1).broadcast_to([CHUNK, GCH, CHUNK]), ALU.mult)
                        dve.wait_ge(applied, lv + 1)
                        for k in range(2):
                            last = nc.vector.tensor_tensor(rhs[:, 8 * k:8 * k + 8, :], rhs[:, 8 * k:8 * k + 8, :],
                                                           banks[2 + k][:, :].rearrange("p (n t) -> p n t", n=8), ALU.add)
                        last.then_inc(added, 1)
                    dve.wait_ge(added, 5)
                    for h in range(H0):
                        nc.vector.transpose(head_block(bd_w, h), rhs[32 * h:32 * h + 32, :, DK:])

            corrected, fixed, stepped, advanced, scanned = s.sem("corrected"), s.sem("fixed"), s.sem("stepped"), s.sem("advanced"), s.sem("scanned")
            with nc.Block() as block:
                @block.tensor
                def _(pe):
                    for i in range(SCH):
                        if i:
                            pe.wait_ge(advanced, i)
                            for b in range(GB):
                                last = nc.tensor.matmul(banks[0][:, b * DK:(b + 1) * DK], bd_w[:, b * SCH + i, :], state[:, b, :], start=True, stop=True)
                            last.then_inc(corrected, 1)
                            pe.wait_ge(fixed, i)
                        if i < SCH - 1:
                            for b in range(GB):
                                last = nc.tensor.matmul(banks[2][:, b * DK:(b + 1) * DK], bd_ktok[:, b * SCH + i, :],
                                                        rhs[:, b * SCH + i, 0:DK], start=True, stop=True)
                            last.then_inc(stepped, 1)
                        for b in range(GB):
                            n = b * SCH + i
                            dst = banks[1][:, n * DK:(n + 1) * DK]
                            if i:
                                nc.tensor.matmul(dst, bd_q[:, n, :], state[:, b, :], start=True, stop=False)
                            last = nc.tensor.matmul(dst, bd_attn[:, n, :], rhs[:, n, 0:DK], start=(i == 0), stop=True)
                        last.then_inc(scanned, 1)

                @block.vector
                def _(dve):
                    for i in range(SCH):
                        values = rhs[:, i::SCH, 0:DK]
                        if i:
                            dve.wait_ge(corrected, i)
                            nc.vector.tensor_tensor(values, values, banks[0][:, 0:GB * DK].rearrange("p (b d) -> p b d", b=GB),
                                                    ALU.subtract).then_inc(fixed, 1)
                        if i < SCH - 1:
                            dve.wait_ge(stepped, i + 1)
                            new = banks[2][:, 0:GB * DK].rearrange("p (b d) -> p b d", b=GB)
                            if i:
                                dve.wait_ge(scanned, i)
                                dve.wait_ge(advanced, i)
                                dve.wait_ge(scanned, i + 1)
                                nc.vector.tensor_tensor(state[:, :, :], state[:, :, :], new, ALU.add).then_inc(advanced, 1)
                            else:
                                nc.vector.tensor_copy(state[:, :, :], new).then_inc(advanced, 1)
                    dve.wait_ge(scanned, SCH)
                    nc.vector.transpose(od_t[:, :], banks[1][:, :])

            turned, evacuated, fir_copied, squares, means = s.sem("turned"), s.sem("evacuated"), s.sem("fir_copied"), s.sem("squares"), s.sem("means")
            norms, listed, listed_t = s.sem("norms"), s.sem("listed"), s.sem("listed_t")
            b_done = s.sem("b_done")
            with nc.Block() as block:
                @block.tensor
                def _(pe):
                    for t in range(GT):
                        last = nc.tensor.transpose(banks[3][:, t * P:(t + 1) * P], v_s[:, t // 2, FIRL + (t % 2) * P:FIRL + (t % 2 + 1) * P], c("ident"))
                    last.then_inc(turned, 1)
                    for t in range(GT):
                        last = nc.tensor.transpose(banks[2][:, t * P:(t + 1) * P], od_t[:, t * P:(t + 1) * P], c("ident"))
                    last.then_inc(turned, 1)
                    for t in range(GT):
                        for j in range(FIRS):
                            at = FIRL + (t % 2) * P - (FIRS - 1) + j
                            last = nc.tensor.matmul(banks[0][:, t * P:(t + 1) * P], v_s[:, t // 2, at:at + P], tap_diag[:, j, :],
                                                    start=(j == 0), stop=(j == FIRS - 1))
                    last.then_inc(turned, 1)
                    pe.wait_ge(listed, 1)
                    for t in range(GT):
                        last = nc.tensor.transpose(banks[4][:, t * P:(t + 1) * P], stats[:, t, :, :, :].rearrange("p h b s -> p (h b s)"), c("ident"))
                    last.then_inc(listed_t, 1)

                @block.gpsimd
                def _(pool):
                    nc.gpsimd.tensor_copy(branch[:, 1, :].rearrange("p (t c) -> p t c", t=GT), fir_long[:, bass.ds(g * GT, GT), :]).then_inc(fir_copied, 1)

                @block.scalar
                def _(act):
                    for n, (br, bank) in enumerate(((3, 3), (2, 2), (0, 0))):
                        act.wait_ge(turned, n + 1)
                        nc.scalar.copy(branch[:, br, :], banks[bank][:, :]).then_inc(evacuated, 1)
                    act.wait_ge(fir_copied, 1)
                    act.wait_ge(evacuated, 3)
                    nc.scalar.activation(branch_sq[:, :, :], branch[:, :, :], ACT.Square).then_inc(squares, 1)
                    act.wait_ge(means, 1)
                    nc.scalar.activation(sums[:, 4, :], sums[:, 1, :], ACT.Sqrt).then_inc(norms, 1)
                    act.wait_ge(listed_t, 1)
                    nc.scalar.copy(stats_t[:, :], banks[4][:, :])

                @block.vector
                def _(dve):
                    ch = Chain(dve, b_done)
                    by_head = lambda t: t[:, :, :].rearrange("p b (th d) -> p (b th) d", d=DK)
                    slot = lambda n: stats[:, :, :, 0:NBR, n].rearrange("p t h b -> p b (t h)")
                    row = lambda n: sums[:, n, :].rearrange("p (b th) -> p b th", b=NBR)
                    dve.wait_ge(fir_copied, 1)
                    dve.wait_ge(evacuated, 3)
                    nc.vector.tensor_reduce(sums[:, 0, :], by_head(branch), X, ALU.add)
                    nc.vector.tensor_reduce(sums[:, 2, :], by_head(branch), X, ALU.add, apply_absolute_value=True)
                    dve.wait_ge(squares, 1)
                    nc.vector.tensor_reduce(sums[:, 1, :], by_head(branch_sq), X, ALU.add).then_inc(means, 1)
                    dve.wait_ge(means, 1)
                    nc.vector.tensor_scalar(slot(0), row(0), 1.0 / DK, None, ALU.mult)
                    nc.vector.tensor_scalar(slot(2), row(2), 1.0 / DK, None, ALU.mult)
                    ch.link(nc.vector.tensor_tensor(sums[:, 3, :], sums[:, 0, :], sums[:, 0, :], ALU.mult))
                    ch.link(nc.vector.scalar_tensor_tensor(sums[:, 5, :], sums[:, 3, :], -1.0 / DK, sums[:, 1, :], ALU.mult, ALU.add))
                    nc.vector.tensor_scalar(slot(1), row(5), 1.0 / DK, None, ALU.mult)
                    dve.wait_ge(norms, 1)
                    nc.vector.tensor_copy(slot(3), row(4)).then_inc(listed, 1)

            raised, bent, scored, centred, exped, weighed = s.sem("raised"), s.sem("bent"), s.sem("scored"), s.sem("centred"), s.sem("exped"), s.sem("weighed")
            mixing, mean_sq, rms, mixed_up, mixed_turned, mixed_kept, projected = (s.sem(n) for n in (
                "mixing", "mean_sq", "rms", "mixed_up", "mixed_turned", "mixed_kept", "projected"))
            var_ready, sd_ready, g_done = s.sem("var_ready"), s.sem("sd_ready"), s.sem("g_done")
            with nc.Block() as block:
                @block.tensor
                def _(pe):
                    for h in range(H0):
                        nc.tensor.matmul(banks[h][:, :], w1_x[:, :], x_t[:, bass.ds(g * GB, GB), CONV - 1:], start=True, stop=False)
                        nc.tensor.matmul(banks[h][:, :], w1_s[32 * h:32 * h + 32, :], stats_t[32 * h:32 * h + 32, :], start=False, stop=True).then_inc(raised, 1)
                    for h in range(H0):
                        pe.wait_ge(bent, h + 1)
                        for t in range(GT):
                            at = (t * H0 + h) * NBR
                            last = nc.tensor.matmul(banks[4][:, at:at + NBR], hidden[:, h, t * P:(t + 1) * P], w2_t[:, :], start=True, stop=True)
                    last.then_inc(scored, 1)
                    pe.wait_ge(mixed_up, 1)
                    for t in range(GT):
                        last = nc.tensor.transpose(banks[5][:, t * P:(t + 1) * P], mixed[:, t * P:(t + 1) * P], c("ident"))
                    last.then_inc(mixed_turned, 1)
                    pe.wait_ge(mixed_kept, 1)
                    for t in range(GT):
                        last = nc.tensor.matmul(banks[6][:, t * P:(t + 1) * P], mixed_t[:, t * P:(t + 1) * P], wo[:, :], start=True, stop=True)
                    last.then_inc(projected, 1)

                @block.scalar
                def _(act):
                    for h in range(H0):
                        act.wait_ge(raised, h + 1)
                        nc.scalar.activation(hidden[:, h, :], banks[h][:, :], ACT.Gelu_apprx_tanh, bias=b1[:, 0:1]).then_inc(bent, 1)
                    act.wait_ge(centred, 1)
                    nc.scalar.activation(gate[1][:, :, :], gate[0][:, :, :], ACT.Exp).then_inc(exped, 1)
                    act.wait_ge(mean_sq, 1)
                    nc.scalar.activation(small[:, 4, :], small[:, 3, :], ACT.Sqrt).then_inc(rms, 1)
                    act.wait_ge(mixed_turned, 1)
                    nc.scalar.copy(mixed_t[:, :], banks[5][:, :]).then_inc(mixed_kept, 1)
                    act.wait_ge(var_ready, 1)
                    nc.scalar.activation(small[:, 7, 0:GT], small[:, 6, 0:GT], ACT.Sqrt).then_inc(sd_ready, 1)

                @block.vector
                def _(dve):
                    ch = Chain(dve, g_done)
                    per_tile = lambda t: t.unsqueeze(1).broadcast_to([P, GT, H0 * NBR])
                    by_tile = gate[0][:, :, :].rearrange("p (t h) n -> p t (h n)", t=GT)
                    over = lambda n: small[:, n, :].unsqueeze(2).broadcast_to([P, GT * H0, NBR])
                    dve.wait_ge(scored, 1)
                    ch.link(nc.vector.tensor_tensor(by_tile, banks[4][:, 0:GT * H0 * NBR].rearrange("p (t n) -> p t n", t=GT),
                                                    per_tile(logit_bias[:, :, :].rearrange("p h n -> p (h n)")), ALU.add))
                    ch.link(nc.vector.tensor_tensor(gate[0][:, :, :].rearrange("p (t h) n -> p t h n", t=GT),
                                                    gate[0][:, :, :].rearrange("p (t h) n -> p t h n", t=GT),
                                                    inv_temp[:, :].unsqueeze(1).unsqueeze(3).broadcast_to([P, GT, H0, NBR]), ALU.mult))
                    ch.link(nc.vector.tensor_reduce(small[:, 0, :], gate[0][:, :, :], X, ALU.max))
                    nc.vector.tensor_tensor(gate[0][:, :, :], gate[0][:, :, :], over(0), ALU.subtract).then_inc(centred, 1)
                    dve.wait_ge(exped, 1)
                    ch.link(nc.vector.tensor_reduce(small[:, 1, :], gate[1][:, :, :], X, ALU.add))
                    ch.link(nc.vector.reciprocal(small[:, 1, :], small[:, 1, :]))
                    ch.link(nc.vector.tensor_tensor(gate[0][:, :, :], gate[1][:, :, :], over(1), ALU.mult))
                    ch.link(nc.vector.tensor_scalar(gate[0][:, :, :], gate[0][:, :, :], 1.0 - 4.0 * EPS_FLOOR, EPS_FLOOR, ALU.mult, ALU.add))
                    ch.link(nc.vector.tensor_tensor(branch_sq[:, :, :].rearrange("p b (th d) -> p b th d", d=DK),
                                                    branch[:, :, :].rearrange("p b (th d) -> p b th d", d=DK),
                                                    gate[0][:, :, :].rearrange("p th b -> p b th").unsqueeze(3).broadcast_to([P, NBR, GT * H0, DK]), ALU.mult))
                    ch.link(nc.vector.tensor_tensor(branch[:, 0:2, :], branch_sq[:, 0:2, :], branch_sq[:, 2:4, :], ALU.add))
                    ch.link(nc.vector.tensor_tensor(mixed[:, :], branch[:, 0, :], branch[:, 1, :], ALU.add))
                    ch.link(nc.vector.tensor_tensor(branch[:, 2, :], mixed[:, :], mixed[:, :], ALU.mult))
                    ch.link(nc.vector.tensor_reduce(small[:, 2, :], branch[:, 2, :].rearrange("p (th d) -> p th d", d=DK), X, ALU.add))
                    nc.vector.tensor_scalar(small[:, 3, :], small[:, 2, :], 1.0 / DK, 1e-5, ALU.mult, ALU.add).then_inc(mean_sq, 1)
                    dve.wait_ge(rms, 1)
                    ch.link(nc.vector.reciprocal(small[:, 5, :], small[:, 4, :]))
                    nc.vector.tensor_tensor(mixed[:, :].rearrange("p (th d) -> p th d", d=DK), mixed[:, :].rearrange("p (th d) -> p th d", d=DK),
                                            small[:, 5, :].unsqueeze(2).broadcast_to([P, GT * H0, DK]), ALU.mult).then_inc(mixed_up, 1)
                    dve.wait_ge(projected, 1)
                    ch.link(nc.vector.tensor_tensor(x_in[:, :, :], x_in[:, :, :], banks[6][:, :].rearrange("p (t c) -> p t c", t=GT), ALU.add))
                    layer_norm(nc, dve, ch, x_in[:, :, :], branch[:, 3, :].rearrange("p (t c) -> p t c", t=GT), x1_all[:, bass.ds(g * GT, GT), :],
                               small[:, 6, 0:GT], small[:, 7, 0:GT], var_ready, sd_ready, 1)
            s.clear()


def layer_norm(nc, dve, ch, x, scratch, out, var, sd, var_ready, sd_ready, turn):
    tiles, width = x.shape[1], x.shape[2]
    wide = lambda t: t.unsqueeze(2).broadcast_to([P, tiles, width])
    ch.link(nc.vector.tensor_reduce(var, x, X, ALU.add))
    ch.link(nc.vector.tensor_scalar(var, var, -1.0 / width, None, ALU.mult))
    ch.link(nc.vector.tensor_tensor(x, x, wide(var), ALU.add))
    ch.link(nc.vector.tensor_tensor(scratch, x, x, ALU.mult))
    ch.link(nc.vector.tensor_reduce(var, scratch, X, ALU.add))
    nc.vector.tensor_scalar(var, var, 1.0 / width, 1e-5, ALU.mult, ALU.add).then_inc(var_ready, 1)
    dve.wait_ge(sd_ready, turn)
    ch.link(nc.vector.reciprocal(sd, sd))
    ch.link(nc.vector.tensor_tensor(out, x, wide(sd), ALU.mult))


def layer0_attention(nc, io, m, x1_all, res_all, h_all, pick_all):
    banks, c, psum = m.banks, m.c, m.psum
    QKV, QK, HEADS = (NQ + 2 * NKV) * HD0, (NQ + NKV) * HD0, NQ + NKV
    VA = HD0 + 1
    SC = 3 * P
    with ExitStack() as ctx:
        s = Memory(nc, ctx, "attn0_")
        w_qkv, wo, wg = s.sb("w_qkv", [P, QKV]), s.sb("wo", [P, P]), s.sb("wg", [P, P])
        wr, ln1, ln2, bg = s.sb("wr", [P, E]), s.sb("ln1", [P, 1]), s.sb("ln2", [P, 1]), s.sb("bg", [P, 1])
        b_qkv, qk_w, bo, br = s.sb("b_qkv", [P, QKV]), s.sb("qk_w", [P, QK]), s.sb("bo", [P, P]), s.sb("br", [P, E])
        bound = s.sb("bound", [P, 3])
        id16, neg16 = s.sb("id16", [P, P], BF16), s.sb("neg16", [P, P], BF16)
        h, h_t, sq = s.sb("h", [P, GT, P]), s.sb("h_t", [P, GTOK]), s.sb("sq", [P, GT, P])
        qkv = s.sb("qkv", [P, GT, QKV])
        rot = [s.sb(f"rot{n}", [P, GT, QK]) for n in range(2)]
        small = s.sb("small", [P, 4, GT])
        head_ms = s.sb("head_ms", [P, GT, HEADS])
        q_pad, k_pad = s.sb("q_pad", [P, GT, REP, NKV, 32]), s.sb("k_pad", [P, GT, NKV, 32])
        q_t, k_t = s.sb("q_t", [P, REP, GTOK]), s.sb("k_t", [P, GTOK])
        v_one = s.sb("v_one", [P, GT, NKV, VA])
        probs = s.sb("probs", [P, 3, 2, SC])
        inv = s.sb("inv", [P, GT, NQ])
        att, att_t, gate_t = s.sb("att", [P, GT, P]), s.sb("att_t", [P, GTOK]), s.sb("gate_t", [P, GTOK])
        x2 = s.sb("x2", [P, GT, P])
        logits, best = s.sb("logits", [P, GT, E]), s.sb("best", [P, GT])
        loaded, done0 = s.sem("loaded"), s.sem("done0")
        with nc.Block() as block:
            @block.sync
            def _(sp):
                for dst, src in ((w_qkv, "w_qkv"), (wo, "ffn_Wo"), (wg, "Wg_tiled"), (wr, "ffn_Wr"), (ln1, "ln1"), (ln2, "ln2"), (bg, "bg_tiled")):
                    sp.dma_start(dst[:, :], io[src]).then_inc(loaded, 16)
                for dst, src, n in ((b_qkv, "b_qkv", QKV), (qk_w, "qk_w", QK), (bo, "ffn_bo", P), (br, "ffn_br", E)):
                    sp.dma_start(dst[:, :], rows(io[src], n)).then_inc(loaded, 16)

            @block.gpsimd
            def _(pool):
                nc.gpsimd.memset(q_pad[:, :, :, :, :], 0.0)
                nc.gpsimd.memset(k_pad[:, :, :, :], 0.0)
                nc.gpsimd.memset(v_one[:, :, :, HD0:], 1.0)

            @block.vector
            def _(dve):
                ch = Chain(dve, done0)
                dve.wait_ge(loaded, 11 * 16)
                nc.vector.tensor_scalar(w_qkv[:, :], w_qkv[:, :], ln1[:, 0:1], None, ALU.mult)
                nc.vector.tensor_scalar(wr[:, :], wr[:, :], ln2[:, 0:1], None, ALU.mult)
                nc.vector.tensor_tensor(wg[:, :], wg[:, :], c("head_ones"), ALU.mult)
                nc.vector.tensor_copy(id16[:, :], c("ident"))
                nc.vector.tensor_copy(neg16[:, :], c("neg_st"))
                nc.vector.tensor_reduce(bound[:, 0:1], qk_w[:, 0:NQ * HD0], X, ALU.max, apply_absolute_value=True)
                ch.link(nc.vector.tensor_reduce(bound[:, 1:2], qk_w[:, NQ * HD0:], X, ALU.max, apply_absolute_value=True))
                ch.link(nc.vector.tensor_tensor(bound[:, 2:3], bound[:, 0:1], bound[:, 1:2], ALU.mult))
                nc.vector.tensor_scalar(bound[:, 2:3], bound[:, 2:3], -float(HD0) ** 0.5, None, ALU.mult)
        s.clear()

        with nc.Fori(0, GROUPS) as g:
            squared, ms_ready, root_ready, turned, kept, projected, d_done = (s.sem(n) for n in (
                "squared", "ms_ready", "root_ready", "turned", "kept", "projected", "d_done"))
            padded, q_turned, q_kept = s.sem("padded"), s.sem("q_turned"), s.sem("q_kept")
            x1 = lambda: x1_all[:, bass.ds(g * GT, GT), :]
            wide = lambda t: t.unsqueeze(2).broadcast_to([P, GT, P])
            with nc.Block() as block:
                @block.scalar
                def _(act):
                    nc.scalar.activation(sq[:, :, :], x1(), ACT.Square).then_inc(squared, 1)
                    act.wait_ge(ms_ready, 1)
                    nc.scalar.activation(small[:, 1, :], small[:, 0, :], ACT.Sqrt).then_inc(root_ready, 1)
                    act.wait_ge(turned, 1)
                    nc.scalar.copy(h_t[:, :], banks[0]).then_inc(kept, 1)
                    act.wait_ge(ms_ready, 2)
                    nc.scalar.activation(head_ms[:, :, :], head_ms[:, :, :], ACT.Sqrt).then_inc(root_ready, 1)
                    for r in range(REP):
                        act.wait_ge(q_turned, r + 1)
                        nc.scalar.copy(q_t[:, r, :], banks[3 + r])
                    act.wait_ge(q_turned, REP + 1)
                    nc.scalar.copy(k_t[:, :], banks[7])

                @block.tensor
                def _(pe):
                    pe.wait_ge(d_done, 3)
                    for t in range(GT):
                        last = nc.tensor.transpose(banks[0][:, t * P:(t + 1) * P], h[:, t, :], c("ident"))
                    last.then_inc(turned, 1)
                    pe.wait_ge(kept, 1)
                    for t in range(GT):
                        last = nc.tensor.matmul(psum[:, 1 + t // 2, (t % 2) * 256:(t % 2) * 256 + QKV], h_t[:, t * P:(t + 1) * P], w_qkv[:, :],
                                                start=True, stop=True)
                    last.then_inc(projected, 1)
                    pe.wait_ge(padded, 1)
                    for r in range(REP + 1):
                        for t in range(GT):
                            src = q_pad[:, t, r, :, :] if r < REP else k_pad[:, t, :, :]
                            last = nc.tensor.transpose(banks[3 + r][:, t * P:(t + 1) * P], src.rearrange("p i d -> p (i d)"), c("ident"))
                        last.then_inc(q_turned, 1)

                @block.vector
                def _(dve):
                    ch = Chain(dve, d_done)
                    dve.wait_ge(squared, 1)
                    ch.link(nc.vector.tensor_reduce(small[:, 0, :], sq[:, :, :], X, ALU.add))
                    nc.vector.tensor_scalar(small[:, 0, :], small[:, 0, :], 1.0 / D, 1e-6, ALU.mult, ALU.add).then_inc(ms_ready, 1)
                    dve.wait_ge(root_ready, 1)
                    ch.link(nc.vector.reciprocal(small[:, 2, :], small[:, 1, :]))
                    ch.link(nc.vector.tensor_tensor(h[:, :, :], x1(), wide(small[:, 2, :]), ALU.mult))
                    dve.wait_ge(projected, 1)
                    ch.link(nc.vector.tensor_tensor(qkv[:, :, :].rearrange("p (a b) n -> p a b n", b=2),
                                                    psum[:, 1:3, :].rearrange("p a (b n) -> p a b n", b=2)[:, :, :, 0:QKV],
                                                    b_qkv[:, :].unsqueeze(1).unsqueeze(1).broadcast_to([P, 2, 2, QKV]), ALU.add))
                    half = HD0 // 2
                    halves = lambda t: t.rearrange("p t (h d) -> p t h d", d=half)
                    for t in range(GT):
                        for n, name in enumerate(("cos", "sin")):
                            table = c(name)[:, (t % 2) * half:(t % 2 + 1) * half].unsqueeze(1).broadcast_to([P, 2 * HEADS, half])
                            last = nc.vector.tensor_tensor(rot[n][:, t, :].rearrange("p (h d) -> p h d", d=half),
                                                           qkv[:, t, 0:QK].rearrange("p (h d) -> p h d", d=half), table, ALU.mult)
                    ch.link(last)
                    lo = lambda t: halves(t)[:, :, 0::2, :]
                    hi = lambda t: halves(t)[:, :, 1::2, :]
                    nc.vector.tensor_tensor(lo(qkv[:, :, 0:QK]), lo(rot[0][:, :, :]), hi(rot[1][:, :, :]), ALU.subtract)
                    ch.link(nc.vector.tensor_tensor(hi(qkv[:, :, 0:QK]), lo(rot[1][:, :, :]), hi(rot[0][:, :, :]), ALU.add))
                    ch.link(nc.vector.tensor_tensor(rot[0][:, :, :], qkv[:, :, 0:QK], qkv[:, :, 0:QK], ALU.mult))
                    ch.link(nc.vector.tensor_reduce(head_ms[:, :, :], rot[0][:, :, :].rearrange("p t (h d) -> p t h d", d=HD0), X, ALU.add))
                    nc.vector.tensor_scalar(head_ms[:, :, :], head_ms[:, :, :], 1.0 / HD0, 1e-6, ALU.mult, ALU.add).then_inc(ms_ready, 1)
                    nc.vector.tensor_copy(v_one[:, :, :, 0:HD0], qkv[:, :, QK:].rearrange("p t (i d) -> p t i d", d=HD0))
                    dve.wait_ge(root_ready, 2)
                    ch.link(nc.vector.reciprocal(head_ms[:, :, :], head_ms[:, :, :]))
                    ch.link(nc.vector.tensor_tensor(rot[1][:, :, :].rearrange("p t (h d) -> p t h d", d=HD0),
                                                    qkv[:, :, 0:QK].rearrange("p t (h d) -> p t h d", d=HD0),
                                                    head_ms[:, :, :].unsqueeze(3).broadcast_to([P, GT, HEADS, HD0]), ALU.mult))
                    for t in range(GT):
                        for r in range(REP):
                            nc.vector.tensor_tensor(q_pad[:, t, r, :, 0:HD0],
                                                    rot[1][:, t, 0:NQ * HD0].rearrange("p (i r d) -> p r i d", r=REP, d=HD0)[:, r, :, :],
                                                    qk_w[:, 0:NQ * HD0].rearrange("p (i r d) -> p r i d", r=REP, d=HD0)[:, r, :, :], ALU.mult)
                        last = nc.vector.tensor_tensor(k_pad[:, t, :, 0:HD0], rot[1][:, t, NQ * HD0:].rearrange("p (i d) -> p i d", d=HD0),
                                                       qk_w[:, NQ * HD0:].rearrange("p (i d) -> p i d", d=HD0), ALU.mult)
                    last.then_inc(padded, 1)

            scored, exped, used, summed = s.sem("scored"), s.sem("exped"), s.sem("used"), s.sem("summed")
            turns = [(b, r, i2) for b in range(GB) for r in range(REP) for i2 in range(2)]
            with nc.Block() as block:
                @block.tensor
                def _(pe):
                    def score(n):
                        b, r, i2 = turns[n]
                        if n >= 3:
                            pe.wait_ge(exped, n - 2)
                        for a in range(2):
                            i = 2 * i2 + a
                            at, dst = slice(32 * i, 32 * i + 32), banks[2 * (n % 3) + a]
                            k0, k1 = b * SEQ, b * SEQ + P
                            nc.tensor.matmul(dst[:, 0:2 * P], k_t[at, k0:k0 + P], q_t[at, r, k0:k0 + SEQ], start=True, stop=False, skip_group_check=True)
                            nc.tensor.matmul(dst[:, 2 * P:SC], k_t[at, k1:k1 + P], q_t[at, r, k1:k1 + P], start=False, stop=False, skip_group_check=True)
                            nc.tensor.matmul(dst[:, 0:P], id16[:, :], neg16[:, :], start=False, stop=False, skip_group_check=True)
                            last = nc.tensor.matmul(dst[:, 2 * P:SC], id16[:, :], neg16[:, :], start=False, stop=True, skip_group_check=True)
                        last.then_inc(scored, 1)

                    def weigh(n):
                        b, r, i2 = turns[n]
                        pe.wait_ge(exped, n + 1)
                        for a in range(2):
                            i = 2 * i2 + a
                            head, pr = REP * i + r, probs[:, n % 3, a, :]
                            dst = lambda t: banks[6 + b][:, (t * NQ + head) * VA:(t * NQ + head + 1) * VA]
                            nc.tensor.matmul(dst(0), pr[:, 0:P], v_one[:, 2 * b, i, :], start=True, stop=True)
                            nc.tensor.matmul(dst(1), pr[:, P:2 * P], v_one[:, 2 * b, i, :], start=True, stop=False)
                            last = nc.tensor.matmul(dst(1), pr[:, 2 * P:SC], v_one[:, 2 * b + 1, i, :], start=False, stop=True)
                        last.then_inc(used, 1)

                    for n in range(len(turns)):
                        score(n)
                        if n:
                            weigh(n - 1)
                    weigh(len(turns) - 1)

                @block.scalar
                def _(act):
                    for n in range(len(turns)):
                        act.wait_ge(scored, n + 1)
                        if n >= 3:
                            act.wait_ge(used, n - 2)
                        nc.scalar.activation(probs[:, n % 3, :, :], psum[:, 2 * (n % 3):2 * (n % 3) + 2, 0:SC], ACT.Exp,
                                             bias=bound[:, 2:3], scale=float(HD0) ** -0.5).then_inc(exped, 1)

                @block.vector
                def _(dve):
                    ch = Chain(dve, summed)
                    for b in range(GB):
                        dve.wait_ge(used, len(turns) // GB * (b + 1))
                        out = banks[6 + b][:, 0:2 * NQ * VA].rearrange("p (t h d) -> p t h d", t=2, d=VA)
                        ch.link(nc.vector.reciprocal(inv[:, 2 * b:2 * b + 2, :].unsqueeze(3), out[:, :, :, HD0:]))
                        nc.vector.tensor_tensor(att[:, 2 * b:2 * b + 2, :].rearrange("p t (h d) -> p t h d", d=HD0), out[:, :, :, 0:HD0],
                                                inv[:, 2 * b:2 * b + 2, :].unsqueeze(3).broadcast_to([P, 2, NQ, HD0]), ALU.mult)

            att_turned, att_kept, gated, gate_up, multiplied, out_ready = (s.sem(n) for n in (
                "att_turned", "att_kept", "gated", "gate_up", "multiplied", "out_ready"))
            x2_sq, r_ready, r_root, h_turned, h_kept, routed, e_done = (s.sem(n) for n in (
                "x2_sq", "r_ready", "r_root", "h_turned", "h_kept", "routed", "e_done"))
            with nc.Block() as block:
                @block.tensor
                def _(pe):
                    for t in range(GT):
                        last = nc.tensor.transpose(banks[0][:, t * P:(t + 1) * P], att[:, t, :], c("ident"))
                    last.then_inc(att_turned, 1)
                    pe.wait_ge(att_kept, 1)
                    nc.tensor.matmul(banks[1], wg[:, :], att_t[:, :], start=True, stop=True).then_inc(gated, 1)
                    pe.wait_ge(multiplied, 1)
                    for t in range(GT):
                        last = nc.tensor.matmul(banks[2][:, t * P:(t + 1) * P], att_t[:, t * P:(t + 1) * P], wo[:, :], start=True, stop=True)
                    last.then_inc(out_ready, 1)
                    pe.wait_ge(e_done, 4)
                    for t in range(GT):
                        last = nc.tensor.transpose(banks[3][:, t * P:(t + 1) * P], h[:, t, :], c("ident"))
                    last.then_inc(h_turned, 1)
                    pe.wait_ge(h_kept, 1)
                    for t in range(GT):
                        last = nc.tensor.matmul(banks[4][:, t * E:(t + 1) * E], h_t[:, t * P:(t + 1) * P], wr[:, :], start=True, stop=True)
                    last.then_inc(routed, 1)

                @block.scalar
                def _(act):
                    act.wait_ge(att_turned, 1)
                    nc.scalar.copy(att_t[:, :], banks[0]).then_inc(att_kept, 1)
                    act.wait_ge(gated, 1)
                    nc.scalar.activation(gate_t[:, :], banks[1], ACT.Sigmoid, bias=bg[:, 0:1]).then_inc(gate_up, 1)
                    act.wait_ge(e_done, 2)
                    nc.scalar.activation(sq[:, :, :], x2[:, :, :], ACT.Square).then_inc(x2_sq, 1)
                    act.wait_ge(r_ready, 1)
                    nc.scalar.activation(small[:, 1, :], small[:, 0, :], ACT.Sqrt).then_inc(r_root, 1)
                    act.wait_ge(h_turned, 1)
                    nc.scalar.copy(h_t[:, :], banks[3]).then_inc(h_kept, 1)

                @block.gpsimd
                def _(pool):
                    pool.wait_ge(e_done, 2)
                    nc.gpsimd.tensor_tensor(res_all[:, bass.ds(g * GT, GT), :], x2[:, :, :], x1(), ALU.add)
                    pool.wait_ge(e_done, 5)
                    nc.gpsimd.tensor_copy(h_all[:, bass.ds(g * GT, GT), :], h[:, :, :])

                @block.vector
                def _(dve):
                    ch = Chain(dve, e_done)
                    dve.wait_ge(gate_up, 1)
                    nc.vector.tensor_tensor(att_t[:, :], att_t[:, :], gate_t[:, :], ALU.mult).then_inc(multiplied, 1)
                    dve.wait_ge(out_ready, 1)
                    ch.link(nc.vector.tensor_tensor(x2[:, :, :], banks[2].rearrange("p (t c) -> p t c", t=GT),
                                                    bo[:, :].unsqueeze(1).broadcast_to([P, GT, P]), ALU.add))
                    ch.link(nc.vector.tensor_tensor(x2[:, :, :], x2[:, :, :], x1(), ALU.add))
                    dve.wait_ge(x2_sq, 1)
                    ch.link(nc.vector.tensor_reduce(small[:, 0, :], sq[:, :, :], X, ALU.add))
                    nc.vector.tensor_scalar(small[:, 0, :], small[:, 0, :], 1.0 / D, 1e-6, ALU.mult, ALU.add).then_inc(r_ready, 1)
                    dve.wait_ge(r_root, 1)
                    nc.vector.reciprocal(small[:, 2, :], small[:, 1, :]).then_inc(r_ready, 1)
                    dve.wait_ge(r_ready, 2)
                    ch.link(nc.vector.tensor_tensor(h[:, :, :], x2[:, :, :], wide(small[:, 2, :]), ALU.mult))
                    dve.wait_ge(routed, 1)
                    ch.link(nc.vector.tensor_tensor(logits[:, :, :], banks[4][:, 0:GT * E].rearrange("p (t e) -> p t e", t=GT),
                                                    br[:, :].unsqueeze(1).broadcast_to([P, GT, E]), ALU.add))
                    pick_first(nc, ch, m, logits, best, pick_all[:, bass.ds(g * GT, GT), :])
            s.clear()


def pick_first(nc, ch, m, logits, best, out):
    wide = best[:, :].unsqueeze(2).broadcast_to([P, GT, E])
    ch.link(nc.vector.tensor_reduce(best[:, :], logits[:, :, :], X, ALU.max))
    ch.link(nc.vector.tensor_tensor(logits[:, :, :], logits[:, :, :], wide, ALU.is_ge))
    ch.link(nc.vector.scalar_tensor_tensor(logits[:, :, :], logits[:, :, :], -float(E), m.c("experts").unsqueeze(1).broadcast_to([P, GT, E]),
                                           ALU.mult, ALU.add))
    ch.link(nc.vector.tensor_reduce(best[:, :], logits[:, :, :], X, ALU.min))
    ch.link(nc.vector.tensor_tensor(out, logits[:, :, :], wide, ALU.is_equal))


def experts(nc, io, m, layer, h_all, pick_all, y_all):
    banks, c = m.banks, m.c
    F1 = 2 * 256 if layer == 0 else 512
    F2 = 256 if layer == 0 else 512
    CH = F2 // P
    slots_in, slots_out = io[f"sorted{layer}"], io[f"expert_out{layer}"]
    with ExitStack() as ctx:
        s = Memory(nc, ctx, f"moe{layer}_")
        w1, w2 = s.sb("w1", [P, E, F1]), s.sb("w2", [P, E, CH, P])
        b1, b2 = s.sb("b1", [P, E * F1 // P]), s.sb("b2", [P, E * P // P])
        b1_parts, b2_parts = s.sb("b1_parts", [P, 3, E * F1 // P], BF16), s.sb("b2_parts", [P, 3, E], BF16)
        b1_rows, b2_rows = s.sb("b1_rows", [P, E * F1], BF16), s.sb("b2_rows", [P, E * P], BF16)
        ones16 = s.sb("ones16", [P, P], BF16)
        row_w = s.sb("row_w", [P, 1])
        zeros = s.sb("zeros", [P, P])
        PAD = 8
        counts = [s.sb(f"counts{n}", [P, PAD + TILES, E]) for n in range(2)]
        total = s.sb("total", [P, TILES, E])
        over = s.sb("over", [P, E, 16])
        ends = [s.sb(f"ends{n}", [P, PAD + E]) for n in range(2)]
        need, begin = s.sb("need", [P, E]), s.sb("begin", [P, E])
        base = s.sb("base", [P, TILES, E])
        slot_f, slot = s.sb("slot_f", [P, TILES]), s.sb("slot", [P, TILES], I32)
        past = s.sb("past", [P, SLOT_TILES, E])
        owner_f, owner = s.sb("owner_f", [P, SLOT_TILES]), s.sb("owner", [P, SLOT_TILES], I32)
        x_in = [s.sb(f"x_in{k}", [P, P]) for k in range(2)]
        x_t = [s.sb(f"x_t{k}", [P, P]) for k in range(2)]
        side = [s.sb(f"side{k}", [P, 256]) for k in range(2)]
        hid = [s.sb(f"hid{k}", [P, F2]) for k in range(2)]
        hid_t = [s.sb(f"hid_t{k}", [P, F2]) for k in range(2)]
        y = [s.sb(f"y{k}", [P, P]) for k in range(2)]

        loaded, zeroed, slots_zeroed, counted, d_done, placed, scattered = (s.sem(n) for n in (
            "loaded", "zeroed", "slots_zeroed", "counted", "d_done", "placed", "scattered"))
        split, bias_out = s.sem("split"), s.sem("bias_out")
        with nc.Block() as block:
            @block.sync
            def _(sp):
                sp.dma_start(b1[:, :], io[f"experts{layer}_b1"]).then_inc(loaded, 16)
                sp.dma_start(b2[:, :], io[f"experts{layer}_b2"]).then_inc(loaded, 16)
                if layer == 0:
                    sp.dma_start(row_w[:, :], io["ln2"]).then_inc(loaded, 16)
                sp.dma_start(w1[:, :, :], io[f"experts{layer}_W1"].rearrange("e d f -> d e f")).then_inc(loaded, 16)
                sp.dma_start(w2[:, :, :, :], io[f"experts{layer}_W2"].rearrange("e (c f) d -> f e c d", f=P)).then_inc(loaded, 16)
                sp.wait_ge(zeroed, 1)
                sp.dma_start(slots_in.rearrange("(t p) d -> p t d", p=P), zeros[:, :].unsqueeze(1).broadcast_to([P, SLOT_TILES, P])).then_inc(slots_zeroed, 16)
                sp.wait_ge(split, 1)
                for n in range(3):
                    sp.dma_start(b1_rows[32 * n:32 * n + 1, :], b1_parts[:, n, :]).then_inc(bias_out, 16)
                    sp.dma_start(b2_rows[32 * n:32 * n + 1, :], b2_parts[:, n, :]).then_inc(bias_out, 16)
                sp.wait_ge(bias_out, 6 * 16)

            @block.tensor
            def _(pe):
                nc.tensor.matmul(banks[0][:, 0:TILES * E], c("before"), pick_all[:, :, :], start=True, stop=True).then_inc(counted, 1)
                nc.tensor.matmul(banks[1][:, 0:TILES * E], c("ones"), pick_all[:, :, :], start=True, stop=True).then_inc(counted, 1)

            @block.gpsimd
            def _(pool):
                nc.gpsimd.memset(zeros[:, :], 0.0).then_inc(zeroed, 1)
                nc.gpsimd.memset(ones16[:, :], 1.0)
                for t in (b1_rows, b2_rows):
                    nc.gpsimd.memset(t[:, :], 0.0)
                for t in counts:
                    nc.gpsimd.memset(t[:, 0:PAD, :], 0.0)
                for t in ends:
                    last = nc.gpsimd.memset(t[:, 0:PAD], 0.0)
                last.then_inc(zeroed, 1)
                pool.wait_ge(slots_zeroed, 16)
                pool.wait_ge(placed, 1)
                for t in range(TILES):
                    nc.gpsimd.indirect_dma_start(slots_in, bass.IndirectOffsetOnAxis(ap=slot[:, t:t + 1], axis=0), h_all[:, t, :], None).then_inc(scattered, 16)
                pool.wait_ge(scattered, 16 * TILES)

            @block.vector
            def _(dve):
                ch = Chain(dve, d_done)
                dve.wait_ge(zeroed, 2)
                dve.wait_ge(counted, 2)
                tile_e = lambda t: t.rearrange("p (t e) -> p t e", e=E)
                nc.vector.tensor_copy(total[:, :, :], tile_e(banks[1][:, 0:TILES * E]))
                ch.link(nc.vector.tensor_copy(counts[0][:, PAD:, :], tile_e(banks[1][:, 0:TILES * E])))
                for n, step in enumerate((1, 2, 4, 8)):
                    a, b = counts[n % 2], counts[(n + 1) % 2]
                    ch.link(nc.vector.tensor_tensor(b[:, PAD:, :], a[:, PAD:, :], a[:, PAD - step:PAD - step + TILES, :], ALU.add))
                upto = counts[0][:, PAD:, :]
                ch.link(nc.vector.tensor_tensor(over[:, :, :], upto[:, TILES - 1, :].unsqueeze(2).broadcast_to([P, E, 16]),
                                                c("tile_starts").unsqueeze(1).broadcast_to([P, E, 16]), ALU.is_gt))
                ch.link(nc.vector.tensor_reduce(need[:, :], over[:, :, :], X, ALU.add))
                ch.link(nc.vector.tensor_copy(ends[0][:, PAD:], need[:, :]))
                for n, step in enumerate((1, 2, 4)):
                    a, b = ends[n % 2], ends[(n + 1) % 2]
                    ch.link(nc.vector.tensor_tensor(b[:, PAD:], a[:, PAD:], a[:, PAD - step:PAD - step + E], ALU.add))
                end = ends[1][:, PAD:]
                ch.link(nc.vector.tensor_tensor(begin[:, :], end, need[:, :], ALU.subtract))
                ch.link(nc.vector.tensor_tensor(base[:, :, :], upto, total[:, :, :], ALU.subtract))
                ch.link(nc.vector.scalar_tensor_tensor(base[:, :, :], begin[:, :].unsqueeze(1).broadcast_to([P, TILES, E]), float(P), base[:, :, :],
                                                       ALU.mult, ALU.add))
                ch.link(nc.vector.tensor_tensor(base[:, :, :], base[:, :, :], tile_e(banks[0][:, 0:TILES * E]), ALU.add))
                ch.link(nc.vector.tensor_tensor(base[:, :, :], base[:, :, :], pick_all[:, :, :], ALU.mult))
                ch.link(nc.vector.tensor_reduce(slot_f[:, :], base[:, :, :], X, ALU.add))
                nc.vector.tensor_copy(slot[:, :], slot_f[:, :]).then_inc(placed, 1)
                ch.link(nc.vector.tensor_tensor(past[:, :, :], c("slots").unsqueeze(2).broadcast_to([P, SLOT_TILES, E]),
                                                end.unsqueeze(1).broadcast_to([P, SLOT_TILES, E]), ALU.is_ge))
                ch.link(nc.vector.tensor_reduce(owner_f[:, :], past[:, :, :], X, ALU.add))
                ch.link(nc.vector.tensor_scalar(owner_f[:, :], owner_f[:, :], float(E - 1), None, ALU.min))
                nc.vector.tensor_copy(owner[:, :], owner_f[:, :])
                dve.wait_ge(loaded, (5 if layer == 0 else 4) * 16)
                if layer == 0:
                    nc.vector.tensor_scalar(w1[:, :, :], w1[:, :, :], row_w[:, 0:1], None, ALU.mult)
                for b, parts in ((b1, b1_parts), (b2, b2_parts)):
                    for n in range(3):
                        ch.link(nc.vector.tensor_copy(parts[:, n, :], b[:, :]))
                        if n < 2:
                            ch.link(nc.vector.tensor_tensor(b[:, :], b[:, :], parts[:, n, :], ALU.subtract))
                nc.vector.tensor_scalar(need[:, :], need[:, :], 1.0, None, ALU.mult).then_inc(split, 1)
        s.clear()

        x_here, y_out = [s.sem(f"x_here{k}") for k in range(2)], [s.sem(f"y_out{k}") for k in range(2)]
        turned, x_kept, raised, sided, bent, hid_turned, hid_kept, lowered, y_kept, lent = (s.sem(n) for n in (
            "turned", "x_kept", "raised", "sided", "bent", "hid_turned", "hid_kept", "lowered", "y_kept", "lent"))
        with nc.Block() as block:
            @block.gpsimd
            def _(pool):
                for sm in (turned, x_kept, raised, sided, bent, hid_turned, hid_kept, lowered, y_kept):
                    nc.gpsimd.sem_inc(sm, 2)
                for sm in y_out:
                    nc.gpsimd.sem_inc(sm, 16)

        def after(eng, sem, i, k):
            eng.wait_ge(sem, i * 2 + (k + 3))

        def free(eng, sem, i, k):
            eng.wait_ge(sem, i * 2 + (k + 1))

        with nc.Block() as block:
            @block.sync
            def _(sp):
                with nc.sync.Fori(0, SLOT_TILES // 2) as i:
                    for k in range(2):
                        free(sp, turned, i, k)
                        sp.dma_start(x_in[k][:, :], slots_in[bass.ds(i * (2 * P) + k * P, P), :]).then_inc(x_here[k], 16)
                    for k in range(2):
                        after(sp, y_kept, i, k)
                        sp.dma_start(slots_out[bass.ds(i * (2 * P) + k * P, P), :], y[k][:, :]).then_inc(y_out[k], 16)
                for k in range(2):
                    sp.wait_ge(y_out[k], 16 + 16 * SLOT_TILES // 2)

            @block.tensor
            def _(pe):
                with nc.tensor.Fori(0, SLOT_TILES // 2) as i:
                    who = [nc.tensor.value_load(owner[0:1, bass.ds(i * 2 + k, 1)], min_val=0, max_val=E - 1) for k in range(2)]
                    for k in range(2):
                        pe.wait_ge(x_here[k], i * 16 + 16)
                        free(pe, x_kept, i, k)
                        nc.tensor.transpose(banks[k][:, 0:P], x_in[k][:, :], c("ident")).then_inc(turned, 1)
                    for k in range(2):
                        after(pe, x_kept, i, k)
                        free(pe, bent, i, k)
                        nc.tensor.matmul(banks[2 + k][:, 0:F1], x_t[k][:, :], w1[:, :, :].rearrange("p e f -> p (e f)")[:, bass.ds(who[k] * F1, F1)], start=True, stop=False)
                        nc.tensor.matmul(banks[2 + k][:, 0:F1], ones16[:, :], b1_rows[:, bass.ds(who[k] * F1, F1)], start=False, stop=True).then_inc(raised, 1)
                    for k in range(2):
                        after(pe, bent, i, k)
                        free(pe, hid_kept, i, k)
                        for n in range(CH):
                            last = nc.tensor.transpose(banks[4 + k][:, n * P:(n + 1) * P], hid[k][:, n * P:(n + 1) * P], c("ident"))
                        last.then_inc(hid_turned, 1)
                    for k in range(2):
                        after(pe, hid_kept, i, k)
                        free(pe, y_kept, i, k)
                        for n in range(CH):
                            nc.tensor.matmul(banks[6 + k][:, 0:P], hid_t[k][:, n * P:(n + 1) * P],
                                             w2[:, :, :, :].rearrange("p e c d -> p (e c d)")[:, bass.ds(who[k] * (CH * P) + n * P, P)], start=(n == 0), stop=False)
                        nc.tensor.matmul(banks[6 + k][:, 0:P], ones16[:, :], b2_rows[:, bass.ds(who[k] * P, P)], start=False, stop=True).then_inc(lowered, 1)

            @block.scalar
            def _(act):
                with nc.scalar.Fori(0, SLOT_TILES // 2) as i:
                    for k in range(2):
                        after(act, raised, i, k)
                        if layer == 0:
                            free(act, bent, i, k)
                            nc.scalar.activation(side[k][:, :], banks[2 + k][:, 256:512], ACT.Sigmoid).then_inc(sided, 1)
                        else:
                            free(act, hid_turned, i, k)
                            nc.scalar.activation(hid[k][:, :], banks[2 + k][:, 0:F2], ACT.Relu).then_inc(bent, 1)
                    for k in range(2):
                        after(act, hid_turned, i, k)
                        free(act, lowered, i, k)
                        nc.scalar.copy(hid_t[k][:, :], banks[4 + k][:, 0:F2]).then_inc(hid_kept, 1)

            @block.vector
            def _(dve):
                with nc.vector.Fori(0, SLOT_TILES // 2) as i:
                    for k in range(2):
                        after(dve, turned, i, k)
                        free(dve, raised, i, k)
                        nc.vector.tensor_copy(x_t[k][:, :], banks[k][:, 0:P]).then_inc(x_kept, 1)
                    if layer == 0:
                        for k in range(2):
                            after(dve, sided, i, k)
                            free(dve, hid_turned, i, k)
                            nc.vector.tensor_tensor(hid[k][:, :], banks[2 + k][:, 0:256], side[k][:, :], ALU.mult).then_inc(bent, 1)
                    for k in range(2):
                        after(dve, lowered, i, k)
                        dve.wait_ge(y_out[k], i * 16 + 16)
                        nc.vector.tensor_copy(y[k][:, :], banks[6 + k][:, 0:P]).then_inc(y_kept, 1)
        gathered = s.sem("gathered")
        with nc.Block() as block:
            @block.gpsimd
            def _(pool):
                for t in range(TILES):
                    nc.gpsimd.indirect_dma_start(y_all[:, t, :], None, slots_out, bass.IndirectOffsetOnAxis(ap=slot[:, t:t + 1], axis=0)).then_inc(gathered, 16)
                pool.wait_ge(gathered, 16 * TILES)
        s.clear()


def layer1_attention(nc, io, m, x_all, x4_all, h_all, pick_all, prob_all):
    banks, c, psum = m.banks, m.c, m.psum
    SETS = H1 // 4
    VA = HD1 + 1
    SC = 3 * P
    with ExitStack() as ctx:
        s = Memory(nc, ctx, "attn1_")
        w_in = s.sb("w_in", [P, 2, P])
        w_q, w_k, w_v = s.sb("w_q", [P, SETS, 4, 32]), s.sb("w_k", [P, SETS, 4, 32]), s.sb("w_v", [P, P])
        wo, wo_g, wr = s.sb("wo", [P, P]), s.sb("wo_g", [P, P]), s.sb("wr", [P, E])
        gamma, beta, beta_rep = s.sb("gamma", [P, 1]), s.sb("beta", [P, 1]), s.sb("beta_rep", [P, P])
        bo, br, ln_g, ln_b = s.sb("bo", [P, P]), s.sb("br", [P, E]), s.sb("ln_g", [P, P]), s.sb("ln_b", [P, P])
        theta = s.sb("theta", [P, H1])
        powers, decay = s.sb("powers", [P, H1, SC]), s.sb("decay", [P, SC])
        id16, neg16 = s.sb("id16", [P, P], BF16), s.sb("neg16", [P, P], BF16)
        x_in, x_t = s.sb("x_in", [P, GT, P]), s.sb("x_t", [P, GTOK])
        q_t, k_t = s.sb("q_t", [P, SETS, GTOK]), s.sb("k_t", [P, SETS, GTOK])
        v_one = s.sb("v_one", [P, GT, H1, VA])
        scores = [s.sb(f"scores{b}", [P, H1, SC]) for b in range(GB)]
        top = s.sb("top", [P, GB, 2, H1])
        probs_t = s.sb("probs_t", [P, 3, 2, SC])
        inv = s.sb("inv", [P, GT, H1])
        out, out_n, out_t, scratch = s.sb("out", [P, GT, P]), s.sb("out_n", [P, GT, P]), s.sb("out_t", [P, GTOK]), s.sb("scratch", [P, GT, P])
        x4, z = s.sb("x4", [P, GT, P]), s.sb("z", [P, GT, P])
        var, sd = s.sb("var", [P, 3, GT * H1]), s.sb("sd", [P, 3, GT * H1])
        logits, best = s.sb("logits", [P, GT, E]), s.sb("best", [P, GT])
        exps, total = s.sb("exps", [P, GT, E]), s.sb("total", [P, GT])
        loaded, done0, decayed, negated, biased, beta_up, zeroed = (s.sem(n) for n in (
            "loaded", "done0", "decayed", "negated", "biased", "beta_up", "zeroed"))
        with nc.Block() as block:
            @block.sync
            def _(sp):
                for dst, src in ((w_in[:, 0, :], "L1_Wq"), (w_in[:, 1, :], "L1_Wk"), (w_v[:, :], "L1_Wv"), (wo[:, :], "L1_Wo"), (wr[:, :], "L1_Wr"),
                                 (gamma[:, :], "L1_gamma"), (beta[:, :], "L1_beta")):
                    sp.dma_start(dst, io[src]).then_inc(loaded, 16)
                for dst, src, n in ((bo, "L1_bo", P), (br, "L1_br", E), (ln_g, "L1_ln_g", P), (ln_b, "L1_ln_b", P), (theta, "L1_theta", H1)):
                    sp.dma_start(dst[:, :], rows(io[src], n)).then_inc(loaded, 16)

            @block.gpsimd
            def _(pool):
                nc.gpsimd.memset(v_one[:, :, :, HD1:], 1.0)
                nc.gpsimd.memset(w_q[:, :, :, :], 0.0)
                nc.gpsimd.memset(w_k[:, :, :, :], 0.0).then_inc(zeroed, 1)

            @block.scalar
            def _(act):
                act.wait_ge(negated, 1)
                for h in range(H1):
                    last = nc.scalar.activation(powers[:, h, :], c("lag"), ACT.Exp, scale=theta[:, h:h + 1])
                last.then_inc(decayed, 1)

            @block.tensor
            def _(pe):
                pe.wait_ge(beta_up, 1)
                nc.tensor.matmul(banks[0][:, 0:P], beta_rep[:, :], wo[:, :], start=True, stop=True).then_inc(biased, 1)

            @block.vector
            def _(dve):
                ch = Chain(dve, done0)
                dve.wait_ge(loaded, 12 * 16)
                dve.wait_ge(zeroed, 1)
                nc.vector.tensor_scalar(theta[:, :], theta[:, :], -1.0, None, ALU.mult).then_inc(negated, 1)
                for n, w in enumerate((w_q, w_k)):
                    nc.vector.tensor_copy(w[:, :, :, 0:HD1], w_in[:, n, :].rearrange("p (s i d) -> p s i d", s=SETS, d=HD1))
                nc.vector.tensor_copy(beta_rep[:, :], beta[:, 0:1].broadcast_to([P, P])).then_inc(beta_up, 1)
                nc.vector.tensor_scalar(wo_g[:, :], wo[:, :], gamma[:, 0:1], None, ALU.mult)
                nc.vector.tensor_copy(id16[:, :], c("ident"))
                nc.vector.tensor_copy(neg16[:, :], c("neg_ts"))
                dve.wait_ge(biased, 1)
                nc.vector.tensor_tensor(bo[:, :], bo[:, :], banks[0][:, 0:P], ALU.add)
                dve.wait_ge(decayed, 1)
                ch.link(nc.vector.tensor_reduce(decay[:, :], powers[:, :, :].rearrange("p h n -> p n h"), X, ALU.add))
                ch.link(nc.vector.tensor_scalar(decay[:, :], decay[:, :], float(HD1) ** -0.5 / H1, -1.0, ALU.mult, ALU.add))
                ch.link(nc.vector.tensor_tensor(decay[:, :], decay[:, :], c("lag_ok"), ALU.mult))
                nc.vector.tensor_scalar(decay[:, :], decay[:, :], 1.0, None, ALU.add)
        s.clear()

        with nc.Fori(0, GROUPS) as g:
            x_copied, turned, kept, projected = s.sem("x_copied"), s.sem("turned"), s.sem("kept"), s.sem("projected")
            x_now = lambda: x_all[:, bass.ds(g * GT, GT), :]
            with nc.Block() as block:
                @block.tensor
                def _(pe):
                    pe.wait_ge(x_copied, 1)
                    for t in range(GT):
                        last = nc.tensor.transpose(banks[0][:, t * P:(t + 1) * P], x_in[:, t, :], c("ident"))
                    last.then_inc(turned, 1)
                    pe.wait_ge(kept, 1)
                    for n, w in enumerate((w_q, w_k)):
                        for st in range(SETS):
                            nc.tensor.matmul(banks[1 + 2 * n + st], w[:, st, :, :].rearrange("p i d -> p (i d)"), x_t[:, :], start=True, stop=True).then_inc(projected, 1)
                    for t in range(GT):
                        last = nc.tensor.matmul(banks[5][:, t * P:(t + 1) * P], x_t[:, t * P:(t + 1) * P], w_v[:, :], start=True, stop=True)
                    last.then_inc(projected, 1)

                @block.vector
                def _(dve):
                    nc.vector.tensor_copy(x_in[:, :, :], x_now()).then_inc(x_copied, 1)
                    for st in range(SETS):
                        dve.wait_ge(projected, SETS + st + 1)
                        nc.vector.tensor_copy(k_t[:, st, :], banks[1 + SETS + st])
                    dve.wait_ge(projected, 2 * SETS + 1)
                    nc.vector.tensor_copy(v_one[:, :, :, 0:HD1], banks[5].rearrange("p (t h d) -> p t h d", t=GT, d=HD1))

                @block.scalar
                def _(act):
                    act.wait_ge(turned, 1)
                    nc.scalar.copy(x_t[:, :], banks[0]).then_inc(kept, 1)
                    for st in range(SETS):
                        act.wait_ge(projected, st + 1)
                        nc.scalar.copy(q_t[:, st, :], banks[1 + st])

            scored, scaled, centred, exped, flipped, moved, weighed, c_done = (s.sem(n) for n in (
                "scored", "scaled", "centred", "exped", "flipped", "moved", "weighed", "c_done"))
            turns = [(b, h) for b in range(GB) for h in range(0, H1, 2)]
            N = len(turns)
            with nc.Block() as block:
                @block.tensor
                def _(pe):
                    def free(n):
                        if n - 3 >= N:
                            pe.wait_ge(moved, n - 3 - N + 1)
                        elif n >= 3:
                            pe.wait_ge(scaled, n - 3 + 1)

                    for n, (b, h0) in enumerate(turns):
                        free(n)
                        for a in range(2):
                            st, i = divmod(h0 + a, 4)
                            at, dst = slice(32 * i, 32 * i + 32), banks[2 * (n % 3) + a]
                            t0, t1 = b * SEQ, b * SEQ + P
                            nc.tensor.matmul(dst[:, 0:P], q_t[at, st, t0:t0 + P], k_t[at, st, t0:t0 + P], start=True, stop=False, skip_group_check=True)
                            nc.tensor.matmul(dst[:, P:SC], q_t[at, st, t1:t1 + P], k_t[at, st, t0:t0 + SEQ], start=False, stop=False, skip_group_check=True)
                            nc.tensor.matmul(dst[:, 0:P], id16[:, :], neg16[:, :], start=False, stop=False, skip_group_check=True)
                            last = nc.tensor.matmul(dst[:, 2 * P:SC], id16[:, :], neg16[:, :], start=False, stop=True, skip_group_check=True)
                        last.then_inc(scored, 1)

                    def weigh(n):
                        b, h0 = turns[n]
                        pe.wait_ge(moved, n + 1)
                        for a in range(2):
                            h, pr = h0 + a, probs_t[:, n % 3, a, :]
                            dst = lambda t: banks[6 + b][:, (t * H1 + h) * VA:(t * H1 + h + 1) * VA]
                            nc.tensor.matmul(dst(0), pr[:, 0:P], v_one[:, 2 * b, h, :], start=True, stop=True)
                            nc.tensor.matmul(dst(1), pr[:, P:2 * P], v_one[:, 2 * b, h, :], start=True, stop=False)
                            last = nc.tensor.matmul(dst(1), pr[:, 2 * P:SC], v_one[:, 2 * b + 1, h, :], start=False, stop=True)
                        last.then_inc(weighed, 1)

                    for n, (b, h0) in enumerate(turns):
                        free(n + N)
                        pe.wait_ge(exped, b + 1)
                        for a in range(2):
                            for q in range(3):
                                last = nc.tensor.transpose(banks[2 * ((n + N) % 3) + a][:, q * P:(q + 1) * P], scores[b][:, h0 + a, q * P:(q + 1) * P], c("ident"))
                        last.then_inc(flipped, 1)
                        if n:
                            weigh(n - 1)
                    weigh(N - 1)

                @block.scalar
                def _(act):
                    def exps(b):
                        act.wait_ge(centred, b + 1)
                        nc.scalar.activation(scores[b][:, :, :], scores[b][:, :, :], ACT.Exp).then_inc(exped, 1)

                    exps(0)
                    for n in range(N):
                        if n == N // 2:
                            exps(1)
                        act.wait_ge(flipped, n + 1)
                        if n >= 3:
                            act.wait_ge(weighed, n - 2)
                        k = 2 * ((n + N) % 3)
                        nc.scalar.copy(probs_t[:, n % 3, :, :], psum[:, k:k + 2, 0:SC]).then_inc(moved, 1)

                @block.vector
                def _(dve):
                    ch = Chain(dve, c_done)
                    for n, (b, h0) in enumerate(turns):
                        dve.wait_ge(scored, n + 1)
                        k = 2 * (n % 3)
                        nc.vector.tensor_tensor(scores[b][:, h0:h0 + 2, :], psum[:, k:k + 2, 0:SC],
                                                decay[:, :].unsqueeze(1).broadcast_to([P, 2, SC]), ALU.mult).then_inc(scaled, 1)
                        if h0 == H1 - 2:
                            dve.wait_ge(scaled, n + 1)
                            parts = (scores[b][:, :, 0:P], scores[b][:, :, P:SC])
                            for q in range(2):
                                last = nc.vector.tensor_reduce(top[:, b, q, :], parts[q], X, ALU.max)
                            ch.link(last)
                            for q in range(2):
                                last = nc.vector.tensor_tensor(parts[q], parts[q], top[:, b, q, :].unsqueeze(2).broadcast_to([P, H1, parts[q].shape[2]]), ALU.subtract)
                            last.then_inc(centred, 1)
                    for b in range(GB):
                        dve.wait_ge(weighed, N // GB * (b + 1))
                        o = banks[6 + b][:, 0:2 * H1 * VA].rearrange("p (t h d) -> p t h d", t=2, d=VA)
                        ch.link(nc.vector.reciprocal(inv[:, 2 * b:2 * b + 2, :].unsqueeze(3), o[:, :, :, HD1:]))
                        nc.vector.tensor_tensor(out[:, 2 * b:2 * b + 2, :].rearrange("p t (h d) -> p t h d", d=HD1), o[:, :, :, 0:HD1],
                                                inv[:, 2 * b:2 * b + 2, :].unsqueeze(3).broadcast_to([P, 2, H1, HD1]), ALU.mult)

            var_ready, sd_ready, head_normed, out_turned, out_kept, out_ready = (s.sem(n) for n in (
                "var_ready", "sd_ready", "head_normed", "out_turned", "out_kept", "out_ready"))
            x4_up, z_up, x4_turned, x4_kept, routed, shifted, raised, f_done, p_done = (s.sem(n) for n in (
                "x4_up", "z_up", "x4_turned", "x4_kept", "routed", "shifted", "raised", "f_done", "p_done"))
            with nc.Block() as block:
                @block.tensor
                def _(pe):
                    pe.wait_ge(head_normed, 1)
                    for t in range(GT):
                        last = nc.tensor.transpose(banks[0][:, t * P:(t + 1) * P], out_n[:, t, :], c("ident"))
                    last.then_inc(out_turned, 1)
                    pe.wait_ge(out_kept, 1)
                    for t in range(GT):
                        last = nc.tensor.matmul(banks[1][:, t * P:(t + 1) * P], out_t[:, t * P:(t + 1) * P], wo_g[:, :], start=True, stop=True)
                    last.then_inc(out_ready, 1)
                    pe.wait_ge(x4_up, 1)
                    for t in range(GT):
                        last = nc.tensor.transpose(banks[2][:, t * P:(t + 1) * P], x4[:, t, :], c("ident"))
                    last.then_inc(x4_turned, 1)
                    pe.wait_ge(x4_kept, 1)
                    for t in range(GT):
                        last = nc.tensor.matmul(banks[3][:, t * E:(t + 1) * E], x_t[:, t * P:(t + 1) * P], wr[:, :], start=True, stop=True)
                    last.then_inc(routed, 1)

                @block.scalar
                def _(act):
                    act.wait_ge(var_ready, 1)
                    nc.scalar.activation(sd[:, 0, :], var[:, 0, :], ACT.Sqrt).then_inc(sd_ready, 1)
                    act.wait_ge(out_turned, 1)
                    nc.scalar.copy(out_t[:, :], banks[0]).then_inc(out_kept, 1)
                    act.wait_ge(var_ready, 2)
                    nc.scalar.activation(sd[:, 1, 0:GT], var[:, 1, 0:GT], ACT.Sqrt).then_inc(sd_ready, 1)
                    act.wait_ge(x4_turned, 1)
                    nc.scalar.copy(x_t[:, :], banks[2]).then_inc(x4_kept, 1)
                    act.wait_ge(var_ready, 3)
                    nc.scalar.activation(sd[:, 2, 0:GT], var[:, 2, 0:GT], ACT.Sqrt).then_inc(sd_ready, 1)
                    act.wait_ge(shifted, 1)
                    nc.scalar.activation(exps[:, :, :], exps[:, :, :], ACT.Exp).then_inc(raised, 1)

                @block.gpsimd
                def _(pool):
                    pool.wait_ge(x4_up, 1)
                    nc.gpsimd.tensor_copy(x4_all[:, bass.ds(g * GT, GT), :], x4[:, :, :])
                    pool.wait_ge(z_up, 1)
                    row = lambda t: t[:, :].unsqueeze(1).broadcast_to([P, GT, P])
                    nc.gpsimd.tensor_tensor(scratch[:, :, :], z[:, :, :], row(ln_g), ALU.mult).then_inc(p_done, 1)
                    pool.wait_ge(p_done, 1)
                    nc.gpsimd.tensor_tensor(h_all[:, bass.ds(g * GT, GT), :], scratch[:, :, :], row(ln_b), ALU.add)

                @block.vector
                def _(dve):
                    ch = Chain(dve, f_done)
                    by_head = lambda t: t[:, :, :].rearrange("p t (h d) -> p (t h) d", d=HD1)
                    layer_norm(nc, dve, ch, by_head(out), by_head(scratch), by_head(out_n), var[:, 0, :], sd[:, 0, :], var_ready, sd_ready, 1)
                    nc.vector.tensor_scalar(total[:, :], sd[:, 0, 0:GT], 1.0, None, ALU.mult).then_inc(head_normed, 1)
                    dve.wait_ge(out_ready, 1)
                    ch.link(nc.vector.tensor_tensor(x4[:, :, :], banks[1].rearrange("p (t c) -> p t c", t=GT), bo[:, :].unsqueeze(1).broadcast_to([P, GT, P]), ALU.add))
                    ch.link(nc.vector.tensor_tensor(z[:, :, :], x4[:, :, :], x_now(), ALU.add))
                    layer_norm(nc, dve, ch, z[:, :, :], scratch[:, :, :], x4[:, :, :], var[:, 1, 0:GT], sd[:, 1, 0:GT], var_ready, sd_ready, 2)
                    ch.link(nc.vector.tensor_copy(out[:, :, :], x4[:, :, :]))
                    nc.vector.tensor_scalar(total[:, :], sd[:, 1, 0:GT], 1.0, None, ALU.mult).then_inc(x4_up, 1)
                    layer_norm(nc, dve, ch, out[:, :, :], scratch[:, :, :], z[:, :, :], var[:, 2, 0:GT], sd[:, 2, 0:GT], var_ready, sd_ready, 3)
                    ch.link(nc.vector.tensor_scalar(total[:, :], sd[:, 2, 0:GT], 1.0, None, ALU.mult))
                    nc.vector.tensor_copy(best[:, :], total[:, :]).then_inc(z_up, 1)
                    dve.wait_ge(routed, 1)
                    ch.link(nc.vector.tensor_tensor(logits[:, :, :], banks[3][:, 0:GT * E].rearrange("p (t e) -> p t e", t=GT),
                                                    br[:, :].unsqueeze(1).broadcast_to([P, GT, E]), ALU.add))
                    ch.link(nc.vector.tensor_reduce(total[:, :], logits[:, :, :], X, ALU.max))
                    nc.vector.tensor_tensor(exps[:, :, :], logits[:, :, :], total[:, :].unsqueeze(2).broadcast_to([P, GT, E]), ALU.subtract).then_inc(shifted, 1)
                    dve.wait_ge(raised, 1)
                    ch.link(nc.vector.tensor_reduce(total[:, :], exps[:, :, :], X, ALU.add))
                    nc.vector.reciprocal(prob_all[:, bass.ds(g * GT, GT)], total[:, :])
                    pick_first(nc, ch, m, logits, best, pick_all[:, bass.ds(g * GT, GT), :])
            s.clear()


def norm_all(nc, io, m, stage, a, y, out, scale, scratch, store=None):
    STEPS = 4
    n = TILES // STEPS
    with ExitStack() as ctx:
        s = Memory(nc, ctx, stage)
        var, sd = s.sb("var", [P, TILES]), s.sb("sd", [P, TILES])
        var_ready, sd_ready, done, normed, stored = (s.sem(x) for x in ("var_ready", "sd_ready", "done", "normed", "stored"))
        with nc.Block() as block:
            @block.scalar
            def _(act):
                for k in range(STEPS):
                    act.wait_ge(var_ready, k + 1)
                    nc.scalar.activation(sd[:, n * k:n * k + n], var[:, n * k:n * k + n], ACT.Sqrt).then_inc(sd_ready, 1)

            @block.vector
            def _(dve):
                ch = Chain(dve, done)
                for k in range(STEPS):
                    at = slice(n * k, n * k + n)
                    if scale is not None:
                        ch.link(nc.vector.tensor_tensor(y[:, at, :], y[:, at, :], scale[:, at].unsqueeze(2).broadcast_to([P, n, P]), ALU.mult))
                    ch.link(nc.vector.tensor_tensor(y[:, at, :], y[:, at, :], a[:, at, :], ALU.add))
                    layer_norm(nc, dve, ch, y[:, at, :], scratch[:, at, :], out[:, at, :], var[:, at], sd[:, at], var_ready, sd_ready, k + 1)
                    nc.vector.tensor_copy(var[:, at], sd[:, at]).then_inc(normed, 1)

            @block.sync
            def _(sp):
                if store is not None:
                    for k in range(STEPS):
                        sp.wait_ge(normed, k + 1)
                        sp.dma_start(store.rearrange("(t p) d -> p t d", p=P)[:, n * k:n * k + n, :], out[:, n * k:n * k + n, :]).then_inc(stored, 16)
                    sp.wait_ge(stored, 16 * STEPS)
        s.clear()


def laid_out(i):
    a = {"consts": constants(), "x": i["L0_attn_hidden_states"].reshape(TOKENS, D)}
    for n in ("q", "k", "v"):
        a[f"W{n}_t"] = i[f"L0_attn_W{n}"].T
        a[f"conv_{n}_t"] = i[f"L0_attn_conv_{n}_w"].T.reshape(-1)
    a["Wb_t"] = i["L0_attn_Wb"].T
    a["w_qkv"] = np.concatenate([i[f"L0_ffn_W{n}"] for n in "qkv"], 1)
    a["b_qkv"] = np.concatenate([i[f"L0_ffn_b{n}"] for n in "qkv"])
    a["qk_w"] = np.concatenate([np.tile(i["L0_ffn_qn_w"], NQ), np.tile(i["L0_ffn_kn_w"], NKV)])
    a["ffn_Wo"], a["ffn_bo"], a["ffn_Wr"], a["ffn_br"] = (i[f"L0_ffn_{n}"] for n in ("Wo", "bo", "Wr", "br"))
    a["Wg_tiled"] = np.tile(i["L0_ffn_Wg"], (NQ, NQ))
    a["bg_tiled"] = np.tile(i["L0_ffn_bg"], NQ).reshape(P, 1)
    a["ln1"], a["ln2"] = i["L0_ffn_ln1_w"].reshape(P, 1), i["L0_ffn_ln2_w"].reshape(P, 1)
    for n in range(2):
        a[f"experts{n}_W1"], a[f"experts{n}_W2"] = i[f"L{n}_ffn_W1"], i[f"L{n}_ffn_W2"]
        a[f"experts{n}_b1"], a[f"experts{n}_b2"] = i[f"L{n}_ffn_b1"].reshape(P, -1), i[f"L{n}_ffn_b2"].reshape(P, -1)
    for n in ("Wq", "Wk", "Wv", "Wo", "bo", "theta"):
        a[f"L1_{n}"] = i[f"L1_attn_{n}"]
    a["L1_gamma"], a["L1_beta"] = i["L1_attn_gamma"].reshape(P, 1), i["L1_attn_beta"].reshape(P, 1)
    for n in ("Wr", "br", "ln_g", "ln_b"):
        a[f"L1_{n}"] = i[f"L1_ffn_{n}"]
    a["gate_w1x_t"] = i["L0_attn_gate_W1"][:, :D].T
    a["gate_w1s_t"] = i["L0_attn_gate_W1"][:, D:].T
    a["gate_w2_t"] = i["L0_attn_gate_W2"].T
    a["gate_b1"] = i["L0_attn_gate_b1"].reshape(P, 1)
    a["gate_b2"] = i["L0_attn_gate_b2"]
    a["copy_bias"] = i["L0_attn_gate_copy_bias"]
    a["log_temp"] = i["L0_attn_gate_log_temp"]
    a["o_norm"] = i["L0_attn_o_norm_w"].reshape(DK, 1)
    a["Wo_t"] = i["L0_attn_Wo"].T
    a["fir_short"] = i["L0_attn_fir_short_filt"].reshape(P, FIRS)
    a["fir_long_rev"] = i["L0_attn_fir_long_filt"].reshape(P, FIRL)[:, ::-1]
    return a


def kernel(**inputs):
    import concourse.bacc as bacc
    from concourse.bass_utils import run_bass_kernel_spmd

    nc = bacc.Bacc("TRN2", target_bir_lowering=False, num_devices=1)
    arrays = {k: np.ascontiguousarray(v) for k, v in laid_out(inputs).items()}
    io = {k: nc.dram_tensor(k, v.shape, mybir.dt.from_np(v.dtype), kind="ExternalInput").ap() for k, v in arrays.items()}
    for name, shape in SCRATCH.items():
        io[name] = nc.dram_tensor(name, shape, F32, kind="Internal").ap()
    out = nc.dram_tensor("out", (TOKENS, D), F32, kind="ExternalOutput").ap()
    build_program(nc, io, out)
    got = run_bass_kernel_spmd(nc, [arrays], core_ids=[0]).results[0]["out"]
    return got.reshape(BATCH, SEQ, D)
```

```python
from contextlib import ExitStack

import numpy as np
import concourse.bass as bass
from concourse import mybir

F32 = mybir.dt.float32
BF16 = mybir.dt.bfloat16
I32 = mybir.dt.int32
U32 = mybir.dt.uint32
ALU = mybir.AluOpType
ACT = mybir.ActivationFunctionType
X = mybir.AxisListType.X

P = 128
BATCH, SEQ, D = 8, 256, 128
TOKENS = BATCH * SEQ
TILES = TOKENS // P
GT = 4
GTOK = GT * P
GB = GTOK // SEQ
GROUPS = TOKENS // GTOK
H0, DK = 4, 32
CHUNK = 32
GCH = GTOK // CHUNK
SCH = SEQ // CHUNK
CONV, FIRS, FIRL = 4, 5, 64
FBLK = TOKENS // FIRL
NBR, NSTAT = 4, 4
DECAY = 1.0 - 1.0 / 3000.0
EPS_FLOOR = 0.08 * DECAY
NQ, NKV, HD0 = 16, 4, 8
REP = NQ // NKV
H1, HD1 = 8, 16
E = 8
SLOT_TILES = TILES + E
NEG = -30000.0

CONST_PARTS = [("ident", 128), ("block_ones", 128), ("before", 128), ("ones", 128), ("neg_st", 128), ("neg_ts", 128),
               ("minus_lower", 32), ("causal_t", 32), ("cos", 8), ("sin", 8), ("lag", 384), ("lag_ok", 384),
               ("tile_starts", 16), ("experts", 8), ("slots", SLOT_TILES), ("head_ones", 128),
               ("minus_upper", 32), ("sum_rows", 64), ("pick_rows", 32), ("eps6", 1), ("eps5", 1)]
CONST_AT, _n = {}, 0
for _name, _w in CONST_PARTS:
    CONST_AT[_name] = (_n, _n + _w)
    _n += _w
CONST_W = _n


def constants():
    c = np.zeros((P, CONST_W), np.float32)

    def put(name, a):
        lo, hi = CONST_AT[name]
        c[:, lo:hi] = a

    i, j = np.arange(P)[:, None], np.arange(P)[None, :]
    put("ident", i == j)
    put("block_ones", i // DK == j // DK)
    put("before", i < j)
    put("head_ones", i // HD0 == j // HD0)
    put("ones", 1.0)
    put("neg_st", np.where(i > j, NEG, 0.0))
    put("neg_ts", np.where(j > i, NEG, 0.0))
    r, k = i % CHUNK, np.arange(CHUNK)[None, :]
    put("minus_lower", np.where(k < r, -1.0, 0.0))
    put("causal_t", k >= r)
    put("minus_upper", np.where(k > r, -1.0, 0.0))
    col = np.arange(2 * 32)[None, :]
    put("sum_rows", col % 32 == H0 * (col // 32) + i // DK)
    col = np.arange(GT * 2 * H0)[None, :]
    put("pick_rows", i == 32 * (col // (2 * H0)) + col % (2 * H0))
    put("eps6", 1e-6)
    put("eps5", 1e-5)
    half = HD0 // 2
    freq = (np.float32(1.0) / np.float32(10000.0) ** (np.arange(0, HD0, 2, dtype=np.float32) / np.float32(HD0))).astype(np.float32)
    ang = np.arange(SEQ, dtype=np.float32)[:, None] * freq[None, :]
    put("cos", np.cos(ang).reshape(2, P, half).transpose(1, 0, 2).reshape(P, 8))
    put("sin", np.sin(ang).reshape(2, P, half).transpose(1, 0, 2).reshape(P, 8))
    lag = np.concatenate([i - j, i + P - np.arange(SEQ)[None, :]], 1)
    put("lag", np.maximum(lag, 0))
    put("lag_ok", lag >= 0)
    put("tile_starts", np.arange(16)[None, :] * P)
    put("experts", np.arange(E)[None, :])
    put("slots", np.arange(SLOT_TILES)[None, :])
    return c


SCRATCH = {"taps_padded": (2 * P, P), "sorted0": (SLOT_TILES * P, P), "sorted1": (SLOT_TILES * P, P),
           "expert_out0": (SLOT_TILES * P, P), "expert_out1": (SLOT_TILES * P, P)}


def dump(nc, io, m, name, t):
    if "dump_" + name in io:
        s = m.nc.alloc_semaphore("dump_" + name)
        with nc.Block() as block:
            @block.sync
            def _(sp):
                sp.dma_start(io["dump_" + name], t).then_inc(s, 16)
                sp.wait_ge(s, 16)


def rows(ap, n):
    return bass.AP(ap.tensor, 0, [[0, P], [1, n]])


def last_first(ap):
    *outer, (step, n) = [list(d) for d in ap.ap]
    return bass.AP(ap.tensor, ap.offset + step * (n - 1), [*outer, [-step, n]])


class Chain:

    def __init__(self, eng, done):
        self.eng, self.done, self.n = eng, done, 0

    def link(self, ins):
        self.n += 1
        ins.then_inc(self.done, 1)
        self.eng.wait_ge(self.done, self.n)


class Memory:

    def __init__(self, nc, ctx, stage=""):
        self.nc, self.ctx, self.stage, self.sems = nc, ctx, stage, []

    def sb(self, name, shape, dt=F32):
        return self.ctx.enter_context(self.nc.sbuf_tensor(self.stage + name, list(shape), dt))

    def sem(self, name):
        s = self.nc.alloc_semaphore(self.stage + name)
        self.sems.append(s)
        return s

    def clear(self):
        nums = sorted(s.num for s in self.sems)
        for lo in [n for n in nums if n - 1 not in nums]:
            hi = lo
            while hi in nums:
                hi += 1
            self.nc.sync.sem_clear(range(lo, hi))
        self.nc.all_engine_barrier()
        for s in self.sems:
            self.nc.release_semaphore(s)
        self.sems = []


def build_program(nc, io, out):
    ctx = ExitStack()
    with ctx:
        shared = Memory(nc, ctx)
        psum = ctx.enter_context(nc.psum_tensor("psum", [P, 8, 512], F32))
        banks = [psum[:, i, :] for i in range(8)]
        shared.psum = psum
        cst = shared.sb("cst", [P, CONST_W])
        shared.banks, shared.cst = banks, cst
        shared.c = lambda name: cst[:, CONST_AT[name][0]:CONST_AT[name][1]]
        const_loaded = nc.alloc_semaphore("const_loaded")
        with nc.Block() as block:
            @block.sync
            def _(sp):
                sp.dma_start(cst[:, :], io["consts"]).then_inc(const_loaded, 16)
                sp.wait_ge(const_loaded, 16)
        x1_all = shared.sb("x1_all", [P, TILES, P])
        layer0_mixer(nc, io, shared, x1_all)
        dump(nc, io, shared, "x1", x1_all[:, :, :])
        res_all = shared.sb("res_all", [P, TILES, P])
        h_all = shared.sb("h_all", [P, TILES, P])
        pick_all = shared.sb("pick_all", [P, TILES, E])
        with ExitStack() as weights_ctx:
            weights = ExpertWeights(nc, io, shared, weights_ctx, 0)
            layer0_attention(nc, io, shared, x1_all, res_all, h_all, pick_all)
            experts(nc, io, shared, 0, weights, h_all, pick_all, x1_all, Norm(res_all, x1_all, res_all, None, h_all))
        dump(nc, io, shared, "x2", res_all[:, :, :])
        prob_all = shared.sb("prob_all", [P, TILES])
        x4_all = x1_all
        with ExitStack() as weights_ctx:
            weights = ExpertWeights(nc, io, shared, weights_ctx, 1)
            layer1_attention(nc, io, shared, res_all, x4_all, h_all, pick_all, prob_all)
            dump(nc, io, shared, "x3", x4_all[:, :, :])
            experts(nc, io, shared, 1, weights, h_all, pick_all, res_all, Norm(x4_all, res_all, h_all, prob_all, x4_all, out))


def layer0_mixer(nc, io, m, x1_all):
    banks, c = m.banks, m.c
    with ExitStack() as ctx:
        lay = Memory(nc, ctx)
        x_t = lay.sb("x_t", [P, GROUPS * GB, CONV - 1 + SEQ])
        q_t = lay.sb("q_t", [P, GROUPS, GTOK])
        k_t = lay.sb("k_t", [P, GROUPS, GTOK])
        v_t = lay.sb("v_t", [P, GROUPS * GB, FIRL + SEQ])
        beta_t = lay.sb("beta_t", [P, GROUPS, GTOK])
        fir_long = lay.sb("fir_long", [P, TILES, P])
        project(nc, io, m, x_t, q_t, k_t, v_t, beta_t)
        long_filter(nc, io, m, v_t, fir_long)
        dump(nc, io, m, "q_t", q_t[:, :, :])
        dump(nc, io, m, "v_t", v_t[:, :, :])
        dump(nc, io, m, "fir", fir_long[:, :, :])
        delta_and_gate(nc, io, m, x_t, q_t, k_t, v_t, beta_t, fir_long, x1_all)


def project(nc, io, m, x_t, q_t, k_t, v_t, beta_t):
    banks, c = m.banks, m.c
    with ExitStack() as ctx:
        s = Memory(nc, ctx, "project_")
        w_t = s.sb("w_t", [P, 3, P])
        taps = s.sb("taps", [P, 3, CONV, P])
        w_conv = s.sb("w_conv", [P, 3, CONV, P])
        wb = s.sb("wb", [P, H0])
        wb_rep = s.sb("wb_rep", [P, H0, DK])
        x_in = s.sb("x_in", [P, GT, P])
        loaded, scaled, zeroed = s.sem("weights_loaded"), s.sem("weights_scaled"), s.sem("pads_zeroed")
        with nc.Block() as block:
            @block.sync
            def _(sp):
                for n, name in enumerate(("q", "k", "v")):
                    sp.dma_start(w_t[:, n, :], io[f"W{name}_t"]).then_inc(loaded, 16)
                    sp.dma_start(taps[:, n, :, :], rows(io[f"conv_{name}_t"], CONV * P)).then_inc(loaded, 16)
                sp.dma_start(wb[:, :], io["Wb_t"]).then_inc(loaded, 16)

            @block.gpsimd
            def _(pool):
                nc.gpsimd.memset(x_t[:, :, 0:CONV - 1], 0.0)
                nc.gpsimd.memset(v_t[:, :, 0:FIRL], 0.0).then_inc(zeroed, 1)

            @block.vector
            def _(dve):
                dve.wait_ge(loaded, 7 * 16)
                for n in range(3):
                    nc.vector.tensor_tensor(w_conv[:, n, :, :], w_t[:, n, :].unsqueeze(1).broadcast_to([P, CONV, P]),
                                            taps[:, n, :, :], ALU.mult)
                nc.vector.tensor_copy(wb_rep[:, :, :], wb[:, :].unsqueeze(2).broadcast_to([P, H0, DK])).then_inc(scaled, 1)
        s.clear()
        with nc.Fori(0, GROUPS) as g:
            x_here, x_turned, x_kept = s.sem("x_here"), s.sem("x_turned"), s.sem("x_kept")
            projected = s.sem("projected")
            with nc.Block() as block:
                @block.sync
                def _(sp):
                    sp.dma_start(x_in[:, :, :], io["x"][bass.ds(g * GTOK, GTOK), :].rearrange("(n p) d -> p n d", p=P)).then_inc(x_here, 16)

                @block.tensor
                def _(pe):
                    pe.wait_ge(x_here, 16)
                    for t in range(GT):
                        last = nc.tensor.transpose(banks[0][:, t * P:(t + 1) * P], x_in[:, t, :], c("ident"))
                    last.then_inc(x_turned, 1)
                    pe.wait_ge(x_kept, 1)
                    for n in range(3):
                        for j in range(CONV):
                            last = nc.tensor.matmul(banks[1 + n][:, :], w_conv[:, n, j, :], x_t[:, bass.ds(g * GB, GB), j:j + SEQ],
                                                    start=(j == 0), stop=(j == CONV - 1))
                        last.then_inc(projected, 1)
                    nc.tensor.matmul(banks[4][:, :], wb_rep[:, :, :], x_t[:, bass.ds(g * GB, GB), CONV - 1:CONV - 1 + SEQ],
                                     start=True, stop=True).then_inc(projected, 1)

                @block.scalar
                def _(act):
                    act.wait_ge(x_turned, 1)
                    nc.scalar.copy(x_t[:, bass.ds(g * GB, GB), CONV - 1:], banks[0][:, :].rearrange("p (b t) -> p b t", b=GB)).then_inc(x_kept, 1)
                    act.wait_ge(projected, 1)
                    nc.scalar.activation(q_t[:, bass.ds(g, 1), :], banks[1][:, :].unsqueeze(1), ACT.Silu)
                    act.wait_ge(projected, 2)
                    nc.scalar.activation(k_t[:, bass.ds(g, 1), :], banks[2][:, :].unsqueeze(1), ACT.Silu)
                    act.wait_ge(projected, 3)
                    nc.scalar.activation(v_t[:, bass.ds(g * GB, GB), FIRL:], banks[3][:, :].rearrange("p (b t) -> p b t", b=GB), ACT.Silu)
                    act.wait_ge(projected, 4)
                    nc.scalar.activation(beta_t[:, bass.ds(g, 1), :], banks[4][:, :].unsqueeze(1), ACT.Sigmoid)
            s.clear()


def long_filter(nc, io, m, v_t, fir_long):
    banks, c = m.banks, m.c
    with ExitStack() as ctx:
        s = Memory(nc, ctx, "filter_")
        tri = s.sb("tri", [P, P, FIRL])
        win = s.sb("win", [P, P, FBLK])
        taps = s.sb("taps", [P, P])
        taps_here, taps_zeroed, taps_out = s.sem("taps_here"), s.sem("taps_zeroed"), s.sem("taps_out")
        tri_here = s.sem("tri_here")
        turned, kept, filtered, used = s.sem("turned"), s.sem("kept"), s.sem("filtered"), s.sem("used")
        reversed_ = s.sem("reversed")
        v_back = s.sb("v_back", [P, (TOKENS // SEQ) * (FIRL + SEQ)])
        pad = io["taps_padded"]

        def unload(eng, copy, first):
            for k in range(first, 8, 2):
                eng.wait_ge(filtered, k + 1)
                for half in range(2):
                    copy(fir_long[64 * half:64 * half + 64, :, 16 * k:16 * k + 16],
                         banks[k][0:64, :].rearrange("p (c t h) -> p t c h", c=16, h=2)[:, :, :, half])

        with nc.Block() as block:
            @block.sync
            def _(sp):
                sp.wait_ge(taps_zeroed, 1)
                sp.dma_start(taps[:, 0:FIRL], io["fir_long_rev"]).then_inc(taps_here, 16)
                sp.wait_ge(taps_here, 16)
                sp.dma_start(pad[P:2 * P, :], taps[:, :]).then_inc(taps_out, 16)
                sp.dma_start(pad[0:P, FIRL:P], taps[:, FIRL:P]).then_inc(taps_out, 16)
                sp.wait_ge(taps_out, 32)
                for q in range(4):
                    sp.dma_start(tri[32 * q:32 * q + 32, :, :],
                                 bass.AP(pad.tensor, P * P + 1 - FIRL + 32 * q, [[1, 32], [P, P], [1, FIRL]])).then_inc(tri_here, 16)

            @block.vector
            def _(dve):
                nc.vector.memset(taps[:, :], 0.0).then_inc(taps_zeroed, 1)
                nc.vector.tensor_copy(v_back[:, :], last_first(v_t[:, :, :].rearrange("p b t -> p (b t)"))).then_inc(reversed_, 1)
                for w in range(0, FBLK, 8):
                    dve.wait_ge(turned, w // 4 + 2)
                    for k in range(2):
                        b = (w // 4 + k) % 4
                        nc.vector.tensor_copy(win[:, :, w + 4 * k:w + 4 * k + 4],
                                              banks[b][:, :].rearrange("p (w c) -> p c w", w=4)).then_inc(kept, 1)
                unload(dve, nc.vector.tensor_copy, 0)

            @block.scalar
            def _(act):
                unload(act, nc.scalar.copy, 1)

            @block.tensor
            def _(pe):
                pe.wait_ge(reversed_, 1)
                for w in range(FBLK):
                    if w >= 16 and w % 4 == 0:
                        pe.wait_ge(kept, w // 4 - 3)
                    end, at = (TOKENS // SEQ) * (FIRL + SEQ), (w // 4) * (FIRL + SEQ) + FIRL * (w % 4)
                    last = nc.tensor.transpose(banks[(w // 4) % 4][:, (w % 4) * P:(w % 4 + 1) * P], v_back[:, end - at - P:end - at], c("ident"))
                    if w % 4 == 3:
                        last.then_inc(turned, 1)
                pe.wait_ge(kept, 8)
                pe.wait_ge(tri_here, 64)
                for ch in range(P):
                    last = nc.tensor.matmul(banks[ch // 16][0:64, (ch % 16) * FBLK:(ch % 16 + 1) * FBLK],
                                            tri[:, ch, :], win[:, ch, :], start=True, stop=True)
                    if ch % 16 == 15:
                        last.then_inc(filtered, 1)
        s.clear()


def head_block(t, h, width=CHUNK):
    return t[h * width:(h + 1) * width, :, h * width:(h + 1) * width]


def delta_and_gate(nc, io, m, x_t, q_t, k_t, v_t, beta_t, fir_long, x1_all):
    banks, c = m.banks, m.c
    with ExitStack() as ctx:
        s = Memory(nc, ctx, "mixer_")
        w1_x, w1_s, w2_t = s.sb("w1_x", [P, P]), s.sb("w1_s", [P, P]), s.sb("w2_t", [P, NBR])
        b1, wo, o_norm = s.sb("b1", [P, 1]), s.sb("wo", [P, P]), s.sb("o_norm", [P, 1])
        taps, tap_diag = s.sb("taps", [P, FIRS]), s.sb("tap_diag", [P, FIRS, P])
        b2, copy_bias, log_temp = s.sb("b2", [P, NBR]), s.sb("copy_bias", [P, H0]), s.sb("log_temp", [P, H0])
        logit_bias, inv_temp = s.sb("logit_bias", [P, H0, NBR]), s.sb("inv_temp", [P, H0])
        sq_q, sq_k, norm_rows = s.sb("sq_q", [P, GTOK]), s.sb("sq_k", [P, GTOK]), s.sb("norm_rows", [P, P])
        unit = s.sb("unit", [P, 3, GTOK])
        vb_n, k_tok, w_t = s.sb("vb_n", [P, GTOK]), s.sb("k_tok", [P, GTOK]), s.sb("w_t", [P, GTOK])
        below = s.sb("below", [P, GTOK])
        attn = s.sb("attn", [P, GTOK])
        bd_pow = [s.sb(f"bd_pow{n}", [P, GCH, P]) for n in range(2)]
        solve = s.sb("solve", [P, GCH, 3 * DK])
        state = s.sb("state", [P, SCH, GB, DK])
        od_t = s.sb("od_t", [P, GTOK])
        pick_wide = s.sb("pick_wide", [P, GT * 2 * H0, DK])
        v_s = s.sb("v_s", [P, GB, FIRL + SEQ])
        branch, branch_sq = s.sb("branch", [P, NBR, GTOK]), s.sb("branch_sq", [P, NBR, GTOK])
        sums = s.sb("sums", [P, 6, NBR * GT * H0])
        stats = s.sb("stats", [P, GT, H0, 8, NSTAT])
        stats_t = s.sb("stats_t", [P, GTOK])
        hidden = s.sb("hidden", [P, H0, GTOK])
        gate = [s.sb(f"gate{n}", [P, GT * H0, NBR]) for n in range(2)]
        small = s.sb("small", [P, 8, GT * H0])
        mixed, mixed_t = s.sb("mixed", [P, GTOK]), s.sb("mixed_t", [P, GTOK])
        x_in = s.sb("x_in", [P, GT, P])
        loaded, cleared, dve_done, temp_done = s.sem("loaded"), s.sem("cleared"), s.sem("dve_done"), s.sem("temp_done")
        w1s_zeroed = s.sem("w1s_zeroed")
        with nc.Block() as block:
            @block.sync
            def _(sp):
                sp.wait_ge(w1s_zeroed, 1)
                for dst, src in ((w1_x, "gate_w1x_t"), (w2_t, "gate_w2_t"), (wo, "Wo_t"), (taps, "fir_short"), (b1, "gate_b1")):
                    sp.dma_start(dst[:, :], io[src]).then_inc(loaded, 16)
                for h in range(H0):
                    sp.dma_start(w1_s[32 * h:32 * h + 16, :], io["gate_w1s_t"]).then_inc(loaded, 16)
                    sp.dma_start(o_norm[32 * h:32 * h + 32, :], io["o_norm"]).then_inc(loaded, 16)
                for dst, src, n in ((b2, "gate_b2", NBR), (copy_bias, "copy_bias", H0), (log_temp, "log_temp", H0)):
                    sp.dma_start(dst[:, :], rows(io[src], n)).then_inc(loaded, 16)

            @block.gpsimd
            def _(pool):
                nc.gpsimd.memset(w1_s[:, :], 0.0).then_inc(w1s_zeroed, 1)
                for t in bd_pow:
                    nc.gpsimd.memset(t[:, :, :], 0.0)
                nc.gpsimd.memset(stats[:, :, :, :, :], 0.0)

            @block.scalar
            def _(act):
                act.wait_ge(loaded, 16 * 16)
                nc.scalar.activation(inv_temp[:, :], log_temp[:, :], ACT.Exp, scale=-1.0)

            @block.vector
            def _(dve):
                dve.wait_ge(loaded, 16 * 16)
                ch = Chain(dve, dve_done)
                nc.vector.tensor_copy(pick_wide[:, :, :], c("pick_rows").unsqueeze(2).broadcast_to([P, GT * 2 * H0, DK]))
                for j in range(FIRS):
                    nc.vector.tensor_scalar(tap_diag[:, j, :], c("ident"), taps[:, j:j + 1], None, ALU.mult)
                ch.link(nc.vector.tensor_copy(logit_bias[:, :, :], b2[:, :].unsqueeze(1).broadcast_to([P, H0, NBR])))
                nc.vector.scalar_tensor_tensor(logit_bias[:, :, 3], copy_bias[:, :], DECAY, logit_bias[:, :, 3], ALU.mult, ALU.add)
                nc.vector.tensor_scalar(wo[:, :], wo[:, :], o_norm[:, 0:1], None, ALU.mult)
        s.clear()

        with nc.Fori(0, GROUPS) as g:
            squared, summed, rooted, inverted, spread = s.sem("squared"), s.sem("summed"), s.sem("rooted"), s.sem("inverted"), s.sem("spread")
            v_copied, keyed, x_here, d_done = s.sem("v_copied"), s.sem("keyed"), s.sem("x_here"), s.sem("d_done")
            produced, masked, placed = s.sem("produced"), s.sem("masked"), s.sem("placed")
            kept, applied, powered, added = ([s.sem(f"{n}{b}") for b in range(GB)] for n in ("kept", "applied", "powered", "added"))
            chunk = lambda t, h, n: t[32 * h:32 * h + 32, n * CHUNK:(n + 1) * CHUNK]
            with nc.Block() as block:
                @block.sync
                def _(sp):
                    sp.dma_start(x_in[:, :, :], io["x"][bass.ds(g * GTOK, GTOK), :].rearrange("(n p) d -> p n d", p=P)).then_inc(x_here, 16)
                    sp.wait_ge(x_here, 16)

                level_out = lambda b: m.psum[:, 2 + 2 * b:4 + 2 * b, :].rearrange("p k (n c) -> p (k n) c", c=P)

                @block.tensor
                def _(pe):
                    for n, t in enumerate((sq_q, sq_k)):
                        pe.wait_ge(squared, n + 1)
                    for t in range(GT):
                        for n, sq in enumerate((sq_q, sq_k)):
                            last = nc.tensor.matmul(banks[0][32 * t:32 * t + 32, 0:P], c("sum_rows")[:, 32 * n:32 * n + 32], sq[:, t * P:(t + 1) * P],
                                                    start=(n == 0), stop=(n == 1))
                    last.then_inc(summed, 1)
                    pe.wait_ge(inverted, 1)
                    for n in range(2):
                        for t in range(GT):
                            at = (t * 2 + 1 - n) * H0
                            last = nc.tensor.matmul(banks[6 + n][:, t * P:(t + 1) * P], pick_wide[:, at:at + H0, :],
                                                    norm_rows[:, :], start=True, stop=True)
                        last.then_inc(spread, 1)
                    pe.wait_ge(d_done, 3)
                    for b in range(GB):
                        for n in range(SCH):
                            for h in range(H0):
                                last = nc.tensor.matmul(banks[b][32 * h:32 * h + 32, n * 2 * CHUNK:(n + 1) * 2 * CHUNK], chunk(unit[:, 2, :], h, b * SCH + n),
                                                        unit[32 * h:32 * h + 32, 0:2, (b * SCH + n) * CHUNK:(b * SCH + n + 1) * CHUNK], start=True, stop=True)
                        last.then_inc(produced, 1)
                    pe.wait_ge(keyed, 1)
                    for lv in range(5):
                        for b in range(GB):
                            pe.wait_ge(kept[b], lv + 1)
                            if lv:
                                pe.wait_ge(powered[b], min(lv, 4))
                                pe.wait_ge(added[b], lv)
                            else:
                                pe.wait_ge(placed, b + 1)
                            for n in range(SCH):
                                last = nc.tensor.matmul(level_out(b)[:, n, 0:3 * DK], bd_pow[lv % 2][:, b * SCH + n, :],
                                                        solve[:, b * SCH + n, :], start=True, stop=True)
                            last.then_inc(applied[b], 1)

                @block.scalar
                def _(act):
                    nc.scalar.activation(sq_q[:, :].unsqueeze(1), q_t[:, bass.ds(g, 1), :], ACT.Square).then_inc(squared, 1)
                    nc.scalar.activation(sq_k[:, :].unsqueeze(1), k_t[:, bass.ds(g, 1), :], ACT.Square).then_inc(squared, 1)
                    act.wait_ge(summed, 1)
                    nc.scalar.activation(norm_rows[:, :], banks[0][:, 0:P], ACT.Sqrt, bias=c("eps6")).then_inc(rooted, 1)
                    nc.scalar.copy(v_s[:, :, :], v_t[:, bass.ds(g * GB, GB), :]).then_inc(v_copied, 1)
                    for b in range(GB):
                        act.wait_ge(masked, b + 1)
                        for h in range(2):
                            last = nc.scalar.copy(head_block(bd_pow[0][:, b * SCH:(b + 1) * SCH, :], h),
                                                  below[32 * h:32 * h + 32, b * SEQ:(b + 1) * SEQ].rearrange("p (n t) -> p n t", n=SCH))
                        last.then_inc(placed, 1)
                    for lv in range(4):
                        for b in range(GB):
                            act.wait_ge(applied[b], lv + 1)
                            nc.scalar.copy(solve[:, b * SCH:(b + 1) * SCH, 0:DK], level_out(b)[:, :, 0:DK]).then_inc(powered[b], 1)

                @block.vector
                def _(dve):
                    ch = Chain(dve, d_done)
                    dve.wait_ge(rooted, 1)
                    nc.vector.reciprocal(norm_rows[:, :], norm_rows[:, :]).then_inc(inverted, 1)
                    dve.wait_ge(spread, 1)
                    ch.link(nc.vector.tensor_tensor(unit[:, 2:3, :], banks[6][:, :].unsqueeze(1), k_t[:, bass.ds(g, 1), :], ALU.mult))
                    ch.link(nc.vector.tensor_tensor(unit[:, 0:1, :], unit[:, 2:3, :], beta_t[:, bass.ds(g, 1), :], ALU.mult))
                    dve.wait_ge(spread, 2)
                    ch.link(nc.vector.tensor_tensor(unit[:, 1:2, :], banks[7][:, :].unsqueeze(1), q_t[:, bass.ds(g, 1), :], ALU.mult))
                    ch.link(nc.vector.tensor_tensor(vb_n[:, :].rearrange("p (b t) -> p b t", b=GB), v_t[:, bass.ds(g * GB, GB), FIRL:],
                                                    beta_t[:, bass.ds(g, 1), :].rearrange("p o (b t) -> p (o b) t", b=GB), ALU.mult))
                    nc.vector.transpose(solve[:, :, DK:2 * DK], vb_n[:, :])
                    nc.vector.transpose(solve[:, :, 2 * DK:], unit[:, 0, :])
                    nc.vector.transpose(k_tok[:, :], unit[:, 2, :]).then_inc(keyed, 1)
                    for b in range(GB):
                        cols = slice(b * SEQ, (b + 1) * SEQ)
                        products = banks[b][:, :].rearrange("p (n k t) -> p n k t", n=SCH, k=2)
                        mask = lambda name: c(name).unsqueeze(1).broadcast_to([P, SCH, CHUNK])
                        by_chunk = lambda t: t[:, cols].rearrange("p (n t) -> p n t", n=SCH)
                        dve.wait_ge(produced, b + 1)
                        nc.vector.tensor_tensor(by_chunk(below), products[:, :, 0, :], mask("minus_upper"), ALU.mult).then_inc(masked, 1)
                        dve.wait_ge(masked, b + 1)
                        for h in (2, 3):
                            nc.vector.tensor_copy(head_block(bd_pow[0][:, b * SCH:(b + 1) * SCH, :], h),
                                                  below[32 * h:32 * h + 32, cols].rearrange("p (n t) -> p n t", n=SCH))
                        nc.vector.transpose(solve[:, b * SCH:(b + 1) * SCH, 0:DK], below[:, cols]).then_inc(kept[b], 1)
                        nc.vector.tensor_tensor(by_chunk(attn), products[:, :, 1, :], mask("causal_t"), ALU.mult)
                    for lv in range(5):
                        for b in range(GB):
                            dve.wait_ge(applied[b], lv + 1)
                            half = slice(b * SCH, (b + 1) * SCH)
                            if lv < 4:
                                dve.wait_ge(powered[b], lv + 1)
                                for h in range(H0):
                                    last = nc.vector.transpose(head_block(bd_pow[(lv + 1) % 2][:, half, :], h), solve[32 * h:32 * h + 32, half, 0:DK])
                                last.then_inc(kept[b], 1)
                            if lv:
                                dve.wait_ge(added[b], lv)
                            nc.vector.tensor_tensor(solve[:, half, DK:], solve[:, half, DK:], level_out(b)[:, :, DK:3 * DK], ALU.add).then_inc(added[b], 1)
                    for b in range(GB):
                        dve.wait_ge(added[b], 5)
                    nc.vector.transpose(w_t[:, :], solve[:, :, 2 * DK:])

            corrected, fixed, stepped, advanced, scanned = s.sem("corrected"), s.sem("fixed"), s.sem("stepped"), s.sem("advanced"), s.sem("scanned")
            filtered, turned, fir_copied, evacuated, squares = s.sem("filtered"), s.sem("turned"), s.sem("fir_copied"), s.sem("evacuated"), s.sem("squares")
            by_head = lambda t, b: t[:, b, :].rearrange("p (th d) -> p th d", d=DK)
            sum_of = lambda n, b: sums[:, n, b * GT * H0:(b + 1) * GT * H0]
            with nc.Block() as block:
                @block.tensor
                def _(pe):
                    def each(i):
                        return [(b, h, b * SCH + i) for b in range(GB) for h in range(H0)]

                    def outputs(i):
                        for b, h, n in each(i):
                            hs = slice(32 * h, 32 * h + 32)
                            if i:
                                nc.tensor.matmul(chunk(banks[2], h, n), state[hs, i, b, :], chunk(unit[:, 1, :], h, n), start=True, stop=False)
                            last = nc.tensor.matmul(chunk(banks[2], h, n), solve[hs, n, DK:2 * DK], chunk(attn, h, n), start=(i == 0), stop=True)
                        return last

                    for i in range(SCH):
                        if i:
                            pe.wait_ge(advanced, i)
                            for b, h, n in each(i):
                                last = nc.tensor.matmul(chunk(banks[0], h, b), chunk(w_t, h, n), state[32 * h:32 * h + 32, i, b, :], start=True, stop=True)
                            last.then_inc(corrected, 1)
                            outputs(i - 1)
                            pe.wait_ge(fixed, i)
                        if i < SCH - 1:
                            for b, h, n in each(i):
                                last = nc.tensor.matmul(chunk(banks[1], h, b), chunk(k_tok, h, n), solve[32 * h:32 * h + 32, n, DK:2 * DK], start=True, stop=True)
                            last.then_inc(stepped, 1)
                        if i < GT:
                            for j in range(FIRS):
                                at = FIRL + (i % 2) * P - (FIRS - 1) + j
                                last = nc.tensor.matmul(banks[4][:, i * P:(i + 1) * P], v_s[:, i // 2, at:at + P], tap_diag[:, j, :],
                                                        start=(j == 0), stop=(j == FIRS - 1))
                            last = nc.tensor.transpose(banks[3][:, i * P:(i + 1) * P], v_s[:, i // 2, FIRL + (i % 2) * P:FIRL + (i % 2 + 1) * P], c("ident"))
                            if i == GT - 1:
                                last.then_inc(filtered, 1)
                    outputs(SCH - 1).then_inc(scanned, 1)

                @block.gpsimd
                def _(pool):
                    nc.gpsimd.tensor_copy(branch[:, 1, :].rearrange("p (t c) -> p t c", t=GT), fir_long[:, bass.ds(g * GT, GT), :]).then_inc(fir_copied, 1)

                @block.scalar
                def _(act):
                    act.wait_ge(fir_copied, 1)
                    nc.scalar.activation(branch_sq[:, 1, :], branch[:, 1, :], ACT.Square).then_inc(squares, 1)
                    act.wait_ge(filtered, 1)
                    for n, br in enumerate((3, 0)):
                        nc.scalar.copy(branch[:, br, :], banks[3 + n][:, :]).then_inc(evacuated, 1)
                        nc.scalar.activation(branch_sq[:, br, :], banks[3 + n][:, :], ACT.Square).then_inc(squares, 1)

                @block.vector
                def _(dve):
                    for i in range(SCH):
                        values = solve[:, i::SCH, DK:2 * DK]
                        if i:
                            dve.wait_ge(corrected, i)
                            nc.vector.tensor_tensor(values, values, banks[0][:, 0:GB * DK].rearrange("p (b d) -> p b d", b=GB),
                                                    ALU.subtract).then_inc(fixed, 1)
                        if i < SCH - 1:
                            dve.wait_ge(stepped, i + 1)
                            new = banks[1][:, 0:GB * DK].rearrange("p (b d) -> p b d", b=GB)
                            if i:
                                dve.wait_ge(advanced, i)
                                nc.vector.tensor_tensor(state[:, i + 1, :, :], state[:, i, :, :], new, ALU.add).then_inc(advanced, 1)
                            else:
                                nc.vector.tensor_copy(state[:, 1, :, :], new).then_inc(advanced, 1)
                        if i >= SCH - 3:
                            n = i - (SCH - 3)
                            br = (1, 3, 0)[n]
                            dve.wait_ge(*((fir_copied, 1) if n == 0 else (evacuated, n)))
                            dve.wait_ge(squares, n + 1)
                            nc.vector.tensor_reduce(sum_of(0, br), by_head(branch, br), X, ALU.add)
                            nc.vector.tensor_reduce(sum_of(2, br), by_head(branch, br), X, ALU.add, apply_absolute_value=True)
                            nc.vector.tensor_reduce(sum_of(1, br), by_head(branch_sq, br), X, ALU.add)

            means, norms, listed, listed_t, od_kept, b_done = (s.sem(n) for n in ("means", "norms", "listed", "listed_t", "od_kept", "b_done"))
            od_evac, od_square = s.sem("od_evac"), s.sem("od_square")
            with nc.Block() as block:
                @block.tensor
                def _(pe):
                    pe.wait_ge(od_kept, 1)
                    for t in range(GT):
                        last = nc.tensor.transpose(banks[3][:, t * P:(t + 1) * P], od_t[:, t * P:(t + 1) * P], c("ident"))
                    last.then_inc(turned, 1)
                    pe.wait_ge(listed, 1)
                    for t in range(GT):
                        last = nc.tensor.transpose(banks[4][:, t * P:(t + 1) * P], stats[:, t, :, :, :].rearrange("p h b s -> p (h b s)"), c("ident"))
                    last.then_inc(listed_t, 1)

                @block.scalar
                def _(act):
                    nc.scalar.copy(od_t[:, :], banks[2][:, :]).then_inc(od_kept, 1)
                    act.wait_ge(turned, 1)
                    nc.scalar.activation(branch_sq[:, 2, :], banks[3][:, :], ACT.Square).then_inc(od_square, 1)
                    nc.scalar.copy(branch[:, 2, :], banks[3][:, :]).then_inc(od_evac, 1)
                    act.wait_ge(means, 1)
                    nc.scalar.activation(sums[:, 4, :], sums[:, 1, :], ACT.Sqrt).then_inc(norms, 1)
                    act.wait_ge(listed_t, 1)
                    nc.scalar.copy(stats_t[:, :], banks[4][:, :])

                @block.vector
                def _(dve):
                    ch = Chain(dve, b_done)
                    slot = lambda n: stats[:, :, :, 0:NBR, n].rearrange("p t h b -> p b (t h)")
                    row = lambda n: sums[:, n, :].rearrange("p (b th) -> p b th", b=NBR)
                    dve.wait_ge(od_square, 1)
                    nc.vector.tensor_reduce(sum_of(1, 2), by_head(branch_sq, 2), X, ALU.add).then_inc(means, 1)
                    dve.wait_ge(od_evac, 1)
                    nc.vector.tensor_reduce(sum_of(0, 2), by_head(branch, 2), X, ALU.add)
                    ch.link(nc.vector.tensor_reduce(sum_of(2, 2), by_head(branch, 2), X, ALU.add, apply_absolute_value=True))
                    nc.vector.tensor_scalar(slot(0), row(0), 1.0 / DK, None, ALU.mult)
                    nc.vector.tensor_scalar(slot(2), row(2), 1.0 / DK, None, ALU.mult)
                    ch.link(nc.vector.tensor_tensor(sums[:, 3, :], sums[:, 0, :], sums[:, 0, :], ALU.mult))
                    dve.wait_ge(means, 1)
                    ch.link(nc.vector.scalar_tensor_tensor(sums[:, 5, :], sums[:, 3, :], -1.0 / DK, sums[:, 1, :], ALU.mult, ALU.add))
                    nc.vector.tensor_scalar(slot(1), row(5), 1.0 / DK, None, ALU.mult)
                    dve.wait_ge(norms, 1)
                    nc.vector.tensor_copy(slot(3), row(4)).then_inc(listed, 1)

            raised, bent, scored, centred, exped, weighed = s.sem("raised"), s.sem("bent"), s.sem("scored"), s.sem("centred"), s.sem("exped"), s.sem("weighed")
            mixing, mean_sq, rms, mixed_up, mixed_turned, mixed_kept, projected = (s.sem(n) for n in (
                "mixing", "mean_sq", "rms", "mixed_up", "mixed_turned", "mixed_kept", "projected"))
            var_ready, sd_ready, g_done = s.sem("var_ready"), s.sem("sd_ready"), s.sem("g_done")
            with nc.Block() as block:
                @block.tensor
                def _(pe):
                    for h in range(H0):
                        nc.tensor.matmul(banks[h][:, :], w1_x[:, :], x_t[:, bass.ds(g * GB, GB), CONV - 1:], start=True, stop=False)
                        nc.tensor.matmul(banks[h][:, :], w1_s[32 * h:32 * h + 32, :], stats_t[32 * h:32 * h + 32, :], start=False, stop=True).then_inc(raised, 1)
                    for h in range(H0):
                        pe.wait_ge(bent, h + 1)
                        for t in range(GT):
                            at = (t * H0 + h) * NBR
                            last = nc.tensor.matmul(banks[4][:, at:at + NBR], hidden[:, h, t * P:(t + 1) * P], w2_t[:, :], start=True, stop=True)
                    last.then_inc(scored, 1)
                    pe.wait_ge(mixed_up, 1)
                    for t in range(GT):
                        last = nc.tensor.transpose(banks[5][:, t * P:(t + 1) * P], mixed[:, t * P:(t + 1) * P], c("ident"))
                    last.then_inc(mixed_turned, 1)
                    pe.wait_ge(mixed_kept, 1)
                    for t in range(GT):
                        last = nc.tensor.matmul(banks[6][:, t * P:(t + 1) * P], mixed_t[:, t * P:(t + 1) * P], wo[:, :], start=True, stop=True)
                    last.then_inc(projected, 1)

                @block.scalar
                def _(act):
                    for h in range(H0):
                        act.wait_ge(raised, h + 1)
                        nc.scalar.activation(hidden[:, h, :], banks[h][:, :], ACT.Gelu_apprx_tanh, bias=b1[:, 0:1]).then_inc(bent, 1)
                    act.wait_ge(centred, 1)
                    nc.scalar.activation(gate[1][:, :, :], gate[0][:, :, :], ACT.Exp).then_inc(exped, 1)
                    act.wait_ge(mean_sq, 1)
                    nc.scalar.activation(small[:, 4, :], small[:, 3, :], ACT.Sqrt).then_inc(rms, 1)
                    act.wait_ge(mixed_turned, 1)
                    nc.scalar.copy(mixed_t[:, :], banks[5][:, :]).then_inc(mixed_kept, 1)
                    act.wait_ge(var_ready, 1)
                    nc.scalar.activation(small[:, 7, 0:GT], small[:, 6, 0:GT], ACT.Sqrt).then_inc(sd_ready, 1)

                @block.vector
                def _(dve):
                    ch = Chain(dve, g_done)
                    per_tile = lambda t: t.unsqueeze(1).broadcast_to([P, GT, H0 * NBR])
                    by_tile = gate[0][:, :, :].rearrange("p (t h) n -> p t (h n)", t=GT)
                    over = lambda n: small[:, n, :].unsqueeze(2).broadcast_to([P, GT * H0, NBR])
                    dve.wait_ge(scored, 1)
                    ch.link(nc.vector.tensor_tensor(by_tile, banks[4][:, 0:GT * H0 * NBR].rearrange("p (t n) -> p t n", t=GT),
                                                    per_tile(logit_bias[:, :, :].rearrange("p h n -> p (h n)")), ALU.add))
                    ch.link(nc.vector.tensor_tensor(gate[0][:, :, :].rearrange("p (t h) n -> p t h n", t=GT),
                                                    gate[0][:, :, :].rearrange("p (t h) n -> p t h n", t=GT),
                                                    inv_temp[:, :].unsqueeze(1).unsqueeze(3).broadcast_to([P, GT, H0, NBR]), ALU.mult))
                    ch.link(nc.vector.tensor_reduce(small[:, 0, :], gate[0][:, :, :], X, ALU.max))
                    nc.vector.tensor_tensor(gate[0][:, :, :], gate[0][:, :, :], over(0), ALU.subtract).then_inc(centred, 1)
                    dve.wait_ge(exped, 1)
                    ch.link(nc.vector.tensor_reduce(small[:, 1, :], gate[1][:, :, :], X, ALU.add))
                    ch.link(nc.vector.reciprocal(small[:, 1, :], small[:, 1, :]))
                    ch.link(nc.vector.tensor_tensor(gate[0][:, :, :], gate[1][:, :, :], over(1), ALU.mult))
                    ch.link(nc.vector.tensor_scalar(gate[0][:, :, :], gate[0][:, :, :], 1.0 - 4.0 * EPS_FLOOR, EPS_FLOOR, ALU.mult, ALU.add))
                    ch.link(nc.vector.tensor_tensor(branch_sq[:, :, :].rearrange("p b (th d) -> p b th d", d=DK),
                                                    branch[:, :, :].rearrange("p b (th d) -> p b th d", d=DK),
                                                    gate[0][:, :, :].rearrange("p th b -> p b th").unsqueeze(3).broadcast_to([P, NBR, GT * H0, DK]), ALU.mult))
                    ch.link(nc.vector.tensor_tensor(branch[:, 0:2, :], branch_sq[:, 0:2, :], branch_sq[:, 2:4, :], ALU.add))
                    ch.link(nc.vector.tensor_tensor(mixed[:, :], branch[:, 0, :], branch[:, 1, :], ALU.add))
                    ch.link(nc.vector.tensor_tensor(branch[:, 2, :], mixed[:, :], mixed[:, :], ALU.mult))
                    ch.link(nc.vector.tensor_reduce(small[:, 2, :], branch[:, 2, :].rearrange("p (th d) -> p th d", d=DK), X, ALU.add))
                    nc.vector.tensor_scalar(small[:, 3, :], small[:, 2, :], 1.0 / DK, 1e-5, ALU.mult, ALU.add).then_inc(mean_sq, 1)
                    dve.wait_ge(rms, 1)
                    ch.link(nc.vector.reciprocal(small[:, 5, :], small[:, 4, :]))
                    nc.vector.tensor_tensor(mixed[:, :].rearrange("p (th d) -> p th d", d=DK), mixed[:, :].rearrange("p (th d) -> p th d", d=DK),
                                            small[:, 5, :].unsqueeze(2).broadcast_to([P, GT * H0, DK]), ALU.mult).then_inc(mixed_up, 1)
                    dve.wait_ge(projected, 1)
                    ch.link(nc.vector.tensor_tensor(x_in[:, :, :], x_in[:, :, :], banks[6][:, :].rearrange("p (t c) -> p t c", t=GT), ALU.add))
                    layer_norm(nc, dve, ch, x_in[:, :, :], branch[:, 3, :].rearrange("p (t c) -> p t c", t=GT), x1_all[:, bass.ds(g * GT, GT), :],
                               small[:, 6, 0:GT], small[:, 7, 0:GT], var_ready, sd_ready, 1)
            s.clear()


def layer_norm(nc, dve, ch, x, scratch, out, var, sd, var_ready, sd_ready, turn):
    tiles, width = x.shape[1], x.shape[2]
    wide = lambda t: t.unsqueeze(2).broadcast_to([P, tiles, width])
    ch.link(nc.vector.tensor_reduce(var, x, X, ALU.add))
    ch.link(nc.vector.tensor_scalar(var, var, -1.0 / width, None, ALU.mult))
    ch.link(nc.vector.tensor_tensor(x, x, wide(var), ALU.add))
    ch.link(nc.vector.tensor_tensor(scratch, x, x, ALU.mult))
    ch.link(nc.vector.tensor_reduce(var, scratch, X, ALU.add))
    nc.vector.tensor_scalar(var, var, 1.0 / width, 1e-5, ALU.mult, ALU.add).then_inc(var_ready, 1)
    dve.wait_ge(sd_ready, turn)
    ch.link(nc.vector.reciprocal(sd, sd))
    ch.link(nc.vector.tensor_tensor(out, x, wide(sd), ALU.mult))


def layer0_attention(nc, io, m, x1_all, res_all, h_all, pick_all):
    banks, c, psum = m.banks, m.c, m.psum
    QKV, QK, HEADS = (NQ + 2 * NKV) * HD0, (NQ + NKV) * HD0, NQ + NKV
    SC = 3 * P
    with ExitStack() as ctx:
        s = Memory(nc, ctx, "attn0_")
        w_qkv, wo, wg = s.sb("w_qkv", [P, QKV]), s.sb("wo", [P, P]), s.sb("wg", [P, P])
        wr, ln1, ln2, bg = s.sb("wr", [P, E]), s.sb("ln1", [P, 1]), s.sb("ln2", [P, 1]), s.sb("bg", [P, 1])
        b_qkv, qk_w, bo, br = s.sb("b_qkv", [P, QKV]), s.sb("qk_w", [P, QK]), s.sb("bo", [P, P]), s.sb("br", [P, E])
        bound = s.sb("bound", [P, 3])
        id16, neg16 = s.sb("id16", [P, P], BF16), s.sb("neg16", [P, P], BF16)
        h, h_t, sq = s.sb("h", [P, GT, P]), s.sb("h_t", [P, GTOK]), s.sb("sq", [P, GT, P])
        qkv = s.sb("qkv", [P, GT, QKV])
        rot = [s.sb(f"rot{n}", [P, GT, QK]) for n in range(2)]
        small = s.sb("small", [P, 4, GT])
        head_ms = s.sb("head_ms", [P, GT, HEADS])
        q_pad, k_pad = s.sb("q_pad", [P, GT, REP, NKV, 32]), s.sb("k_pad", [P, GT, NKV, 32])
        q_t, k_t = s.sb("q_t", [P, REP, GTOK]), s.sb("k_t", [P, NKV, GTOK])
        v_one = s.sb("v_one", [P, GT, NKV, 32])
        out_t = s.sb("out_t", [P, GB, REP, SEQ])
        probs = s.sb("probs", [P, 3, 2, SC])
        inv = s.sb("inv", [P, GT, NQ])
        att, att_t, gate_t = s.sb("att", [P, GT, P]), s.sb("att_t", [P, GTOK]), s.sb("gate_t", [P, GTOK])
        x2 = s.sb("x2", [P, GT, P])
        logits, best = s.sb("logits", [P, GT, E]), s.sb("best", [P, GT])
        loaded, done0 = s.sem("loaded"), s.sem("done0")
        with nc.Block() as block:
            @block.sync
            def _(sp):
                for dst, src in ((w_qkv, "w_qkv"), (wo, "ffn_Wo"), (wg, "Wg_tiled"), (wr, "ffn_Wr"), (ln1, "ln1"), (ln2, "ln2"), (bg, "bg_tiled")):
                    sp.dma_start(dst[:, :], io[src]).then_inc(loaded, 16)
                for dst, src, n in ((b_qkv, "b_qkv", QKV), (qk_w, "qk_w", QK), (bo, "ffn_bo", P), (br, "ffn_br", E)):
                    sp.dma_start(dst[:, :], rows(io[src], n)).then_inc(loaded, 16)

            @block.gpsimd
            def _(pool):
                nc.gpsimd.memset(q_pad[:, :, :, :, :], 0.0)
                nc.gpsimd.memset(k_pad[:, :, :, :], 0.0)
                nc.gpsimd.memset(k_t[:, :, :], 0.0)
                nc.gpsimd.memset(v_one[:, :, :, HD0 + 1:], 0.0)
                nc.gpsimd.memset(v_one[:, :, :, HD0:HD0 + 1], 1.0)

            @block.vector
            def _(dve):
                ch = Chain(dve, done0)
                dve.wait_ge(loaded, 11 * 16)
                nc.vector.tensor_scalar(w_qkv[:, :], w_qkv[:, :], ln1[:, 0:1], None, ALU.mult)
                nc.vector.tensor_scalar(wr[:, :], wr[:, :], ln2[:, 0:1], None, ALU.mult)
                nc.vector.tensor_tensor(wg[:, :], wg[:, :], c("head_ones"), ALU.mult)
                nc.vector.tensor_copy(id16[:, :], c("ident"))
                nc.vector.tensor_copy(neg16[:, :], c("neg_st"))
                nc.vector.tensor_reduce(bound[:, 0:1], qk_w[:, 0:NQ * HD0], X, ALU.max, apply_absolute_value=True)
                ch.link(nc.vector.tensor_reduce(bound[:, 1:2], qk_w[:, NQ * HD0:], X, ALU.max, apply_absolute_value=True))
                ch.link(nc.vector.tensor_tensor(bound[:, 2:3], bound[:, 0:1], bound[:, 1:2], ALU.mult))
                nc.vector.tensor_scalar(bound[:, 2:3], bound[:, 2:3], -float(HD0) ** 0.5, None, ALU.mult)
        s.clear()

        with nc.Fori(0, GROUPS) as g:
            squared, ms_ready, root_ready, turned, kept, projected, d_done = (s.sem(n) for n in (
                "squared", "ms_ready", "root_ready", "turned", "kept", "projected", "d_done"))
            padded, q_turned, q_kept = s.sem("padded"), s.sem("q_turned"), s.sem("q_kept")
            x1 = lambda: x1_all[:, bass.ds(g * GT, GT), :]
            wide = lambda t: t.unsqueeze(2).broadcast_to([P, GT, P])
            with nc.Block() as block:
                @block.scalar
                def _(act):
                    nc.scalar.activation(sq[:, :, :], x1(), ACT.Square).then_inc(squared, 1)
                    act.wait_ge(ms_ready, 1)
                    nc.scalar.activation(small[:, 1, :], small[:, 0, :], ACT.Sqrt).then_inc(root_ready, 1)
                    act.wait_ge(turned, 1)
                    nc.scalar.copy(h_t[:, :], banks[0]).then_inc(kept, 1)
                    act.wait_ge(ms_ready, 2)
                    nc.scalar.activation(head_ms[:, :, :], head_ms[:, :, :], ACT.Sqrt).then_inc(root_ready, 1)
                    for r in range(REP):
                        act.wait_ge(q_turned, r + 2)
                        nc.scalar.copy(q_t[:, r, :], banks[3 + r])

                @block.tensor
                def _(pe):
                    pe.wait_ge(d_done, 3)
                    for t in range(GT):
                        last = nc.tensor.transpose(banks[0][:, t * P:(t + 1) * P], h[:, t, :], c("ident"))
                    last.then_inc(turned, 1)
                    pe.wait_ge(kept, 1)
                    for t in range(GT):
                        last = nc.tensor.matmul(psum[:, 1 + t // 2, (t % 2) * 256:(t % 2) * 256 + QKV], h_t[:, t * P:(t + 1) * P], w_qkv[:, :],
                                                start=True, stop=True)
                    last.then_inc(projected, 1)
                    pe.wait_ge(padded, 1)
                    for r in (REP, *range(REP)):
                        for t in range(GT):
                            src = q_pad[:, t, r, :, :] if r < REP else k_pad[:, t, :, :]
                            last = nc.tensor.transpose(banks[3 + r][:, t * P:(t + 1) * P], src.rearrange("p i d -> p (i d)"), c("ident"))
                        last.then_inc(q_turned, 1)

                @block.vector
                def _(dve):
                    ch = Chain(dve, d_done)
                    dve.wait_ge(squared, 1)
                    ch.link(nc.vector.tensor_reduce(small[:, 0, :], sq[:, :, :], X, ALU.add))
                    nc.vector.tensor_scalar(small[:, 0, :], small[:, 0, :], 1.0 / D, 1e-6, ALU.mult, ALU.add).then_inc(ms_ready, 1)
                    dve.wait_ge(root_ready, 1)
                    ch.link(nc.vector.reciprocal(small[:, 2, :], small[:, 1, :]))
                    ch.link(nc.vector.tensor_tensor(h[:, :, :], x1(), wide(small[:, 2, :]), ALU.mult))
                    dve.wait_ge(projected, 1)
                    ch.link(nc.vector.tensor_tensor(qkv[:, :, :].rearrange("p (a b) n -> p a b n", b=2),
                                                    psum[:, 1:3, :].rearrange("p a (b n) -> p a b n", b=2)[:, :, :, 0:QKV],
                                                    b_qkv[:, :].unsqueeze(1).unsqueeze(1).broadcast_to([P, 2, 2, QKV]), ALU.add))
                    half = HD0 // 2
                    halves = lambda t: t.rearrange("p t (h d) -> p t h d", d=half)
                    for t in range(GT):
                        for n, name in enumerate(("cos", "sin")):
                            table = c(name)[:, (t % 2) * half:(t % 2 + 1) * half].unsqueeze(1).broadcast_to([P, 2 * HEADS, half])
                            last = nc.vector.tensor_tensor(rot[n][:, t, :].rearrange("p (h d) -> p h d", d=half),
                                                           qkv[:, t, 0:QK].rearrange("p (h d) -> p h d", d=half), table, ALU.mult)
                    ch.link(last)
                    lo = lambda t: halves(t)[:, :, 0::2, :]
                    hi = lambda t: halves(t)[:, :, 1::2, :]
                    nc.vector.tensor_tensor(lo(qkv[:, :, 0:QK]), lo(rot[0][:, :, :]), hi(rot[1][:, :, :]), ALU.subtract)
                    ch.link(nc.vector.tensor_tensor(hi(qkv[:, :, 0:QK]), lo(rot[1][:, :, :]), hi(rot[0][:, :, :]), ALU.add))
                    ch.link(nc.vector.tensor_tensor(rot[0][:, :, :], qkv[:, :, 0:QK], qkv[:, :, 0:QK], ALU.mult))
                    ch.link(nc.vector.tensor_reduce(head_ms[:, :, :], rot[0][:, :, :].rearrange("p t (h d) -> p t h d", d=HD0), X, ALU.add))
                    nc.vector.tensor_scalar(head_ms[:, :, :], head_ms[:, :, :], 1.0 / HD0, 1e-6, ALU.mult, ALU.add).then_inc(ms_ready, 1)
                    nc.vector.tensor_copy(v_one[:, :, :, 0:HD0], qkv[:, :, QK:].rearrange("p t (i d) -> p t i d", d=HD0))
                    dve.wait_ge(root_ready, 2)
                    ch.link(nc.vector.reciprocal(head_ms[:, :, :], head_ms[:, :, :]))
                    ch.link(nc.vector.tensor_tensor(rot[1][:, :, :].rearrange("p t (h d) -> p t h d", d=HD0),
                                                    qkv[:, :, 0:QK].rearrange("p t (h d) -> p t h d", d=HD0),
                                                    head_ms[:, :, :].unsqueeze(3).broadcast_to([P, GT, HEADS, HD0]), ALU.mult))
                    for t in range(GT):
                        for r in range(REP):
                            nc.vector.tensor_tensor(q_pad[:, t, r, :, 0:HD0],
                                                    rot[1][:, t, 0:NQ * HD0].rearrange("p (i r d) -> p r i d", r=REP, d=HD0)[:, r, :, :],
                                                    qk_w[:, 0:NQ * HD0].rearrange("p (i r d) -> p r i d", r=REP, d=HD0)[:, r, :, :], ALU.mult)
                        last = nc.vector.tensor_tensor(k_pad[:, t, :, 0:HD0], rot[1][:, t, NQ * HD0:].rearrange("p (i d) -> p i d", d=HD0),
                                                       qk_w[:, NQ * HD0:].rearrange("p (i d) -> p i d", d=HD0), ALU.mult)
                    last.then_inc(padded, 1)
                    dve.wait_ge(q_turned, 1)
                    for i in range(NKV):
                        nc.vector.tensor_copy(k_t[32 * i:32 * i + 32, i, :], banks[7][32 * i:32 * i + 32, :])

            scored, exped, used, summed = s.sem("scored"), s.sem("exped"), s.sem("used"), s.sem("summed")
            turns = [(b, r, i2) for b in range(GB) for r in range(REP) for i2 in range(2)]
            with nc.Block() as block:
                @block.tensor
                def _(pe):
                    def score(n):
                        b, r, i2 = turns[n]
                        if n >= 3:
                            pe.wait_ge(exped, n - 2)
                        for a in range(2):
                            i = 2 * i2 + a
                            dst, k0, k1 = banks[2 * (n % 3) + a], b * SEQ, b * SEQ + P
                            nc.tensor.matmul(dst[:, 0:2 * P], k_t[:, i, k0:k0 + P], q_t[:, r, k0:k0 + SEQ], start=True, stop=False, skip_group_check=True)
                            nc.tensor.matmul(dst[:, 2 * P:SC], k_t[:, i, k1:k1 + P], q_t[:, r, k1:k1 + P], start=False, stop=False, skip_group_check=True)
                            nc.tensor.matmul(dst[:, 0:P], id16[:, :], neg16[:, :], start=False, stop=False, skip_group_check=True)
                            last = nc.tensor.matmul(dst[:, 2 * P:SC], id16[:, :], neg16[:, :], start=False, stop=True, skip_group_check=True)
                        last.then_inc(scored, 1)

                    def weigh(n):
                        b, r, i2 = turns[n]
                        pe.wait_ge(exped, n + 1)
                        if b and i2 == 0 and r % 2 == 0:
                            pe.wait_ge(summed, r // 2 + 1)
                        for a in range(2):
                            i = 2 * i2 + a
                            pr, dst = probs[:, n % 3, a, :], banks[6 + r // 2][32 * i:32 * i + 32, (r % 2) * SEQ:(r % 2 + 1) * SEQ]
                            nc.tensor.matmul(dst, v_one[:, 2 * b, i, :], pr[:, 0:2 * P], start=True, stop=False, skip_group_check=True)
                            last = nc.tensor.matmul(dst[:, P:], v_one[:, 2 * b + 1, i, :], pr[:, 2 * P:SC], start=False, stop=True, skip_group_check=True)
                        last.then_inc(used, 1)

                    for n in range(len(turns)):
                        score(n)
                        if n:
                            weigh(n - 1)
                    weigh(len(turns) - 1)

                @block.scalar
                def _(act):
                    for n in range(len(turns)):
                        act.wait_ge(scored, n + 1)
                        if n >= 3:
                            act.wait_ge(used, n - 2)
                        nc.scalar.activation(probs[:, n % 3, :, :], psum[:, 2 * (n % 3):2 * (n % 3) + 2, 0:SC], ACT.Exp,
                                             bias=bound[:, 2:3], scale=float(HD0) ** -0.5).then_inc(exped, 1)

                @block.vector
                def _(dve):
                    for b in range(GB):
                        for k in range(2):
                            dve.wait_ge(used, len(turns) // GB * b + 4 * (k + 1))
                            nc.vector.tensor_copy(out_t[:, b, 2 * k:2 * k + 2, :], banks[6 + k].rearrange("p (r t) -> p r t", r=2)).then_inc(summed, 1)

            by_token, att_ready, inverted = s.sem("by_token"), s.sem("att_ready"), s.sem("inverted")
            att_turned, att_kept, gated, gate_up, multiplied, out_ready = (s.sem(n) for n in (
                "att_turned", "att_kept", "gated", "gate_up", "multiplied", "out_ready"))
            x2_sq, r_ready, r_root, h_turned, h_kept, routed, e_done = (s.sem(n) for n in (
                "x2_sq", "r_ready", "r_root", "h_turned", "h_kept", "routed", "e_done"))
            with nc.Block() as block:
                @block.tensor
                def _(pe):
                    for b in range(GB):
                        for r in range(REP):
                            for t in range(2):
                                at = ((r % 2) * 2 + t) * P
                                last = nc.tensor.transpose(banks[4 + 2 * b + r // 2][:, at:at + P], out_t[:, b, r, t * P:(t + 1) * P], c("ident"))
                        last.then_inc(by_token, 1)
                    for t in range(GT):
                        if t % 2 == 0:
                            pe.wait_ge(att_ready, t // 2 + 1)
                        last = nc.tensor.transpose(banks[0][:, t * P:(t + 1) * P], att[:, t, :], c("ident"))
                    last.then_inc(att_turned, 1)
                    pe.wait_ge(att_kept, 1)
                    nc.tensor.matmul(banks[1], wg[:, :], att_t[:, :], start=True, stop=True).then_inc(gated, 1)
                    pe.wait_ge(multiplied, 1)
                    for t in range(GT):
                        last = nc.tensor.matmul(banks[2][:, t * P:(t + 1) * P], att_t[:, t * P:(t + 1) * P], wo[:, :], start=True, stop=True)
                    last.then_inc(out_ready, 1)
                    pe.wait_ge(e_done, 4)
                    for t in range(GT):
                        last = nc.tensor.transpose(banks[3][:, t * P:(t + 1) * P], h[:, t, :], c("ident"))
                    last.then_inc(h_turned, 1)
                    pe.wait_ge(h_kept, 1)
                    for t in range(GT):
                        last = nc.tensor.matmul(banks[4][:, t * E:(t + 1) * E], h_t[:, t * P:(t + 1) * P], wr[:, :], start=True, stop=True)
                    last.then_inc(routed, 1)

                @block.scalar
                def _(act):
                    act.wait_ge(att_turned, 1)
                    nc.scalar.copy(att_t[:, :], banks[0]).then_inc(att_kept, 1)
                    act.wait_ge(gated, 1)
                    nc.scalar.activation(gate_t[:, :], banks[1], ACT.Sigmoid, bias=bg[:, 0:1]).then_inc(gate_up, 1)
                    act.wait_ge(e_done, 2)
                    nc.scalar.activation(sq[:, :, :], x2[:, :, :], ACT.Square).then_inc(x2_sq, 1)
                    act.wait_ge(r_ready, 1)
                    nc.scalar.activation(small[:, 1, :], small[:, 0, :], ACT.Sqrt).then_inc(r_root, 1)
                    act.wait_ge(h_turned, 1)
                    nc.scalar.copy(h_t[:, :], banks[3]).then_inc(h_kept, 1)

                @block.gpsimd
                def _(pool):
                    pool.wait_ge(e_done, 2)
                    nc.gpsimd.tensor_tensor(res_all[:, bass.ds(g * GT, GT), :], x2[:, :, :], x1(), ALU.add)
                    pool.wait_ge(e_done, 5)
                    nc.gpsimd.tensor_copy(h_all[:, bass.ds(g * GT, GT), :], h[:, :, :])

                @block.vector
                def _(dve):
                    ch = Chain(dve, e_done)
                    for b in range(GB):
                        dve.wait_ge(by_token, b + 1)
                        sums = psum[:, 4 + 2 * b:6 + 2 * b, :].rearrange("p k (r t i d) -> p t (k r) i d", r=2, t=2, i=NKV)
                        for t in range(2):
                            last = nc.vector.reciprocal(inv[:, 2 * b + t, :].rearrange("p (i r) -> p r i", r=REP).unsqueeze(3), sums[:, t, :, :, HD0:HD0 + 1])
                        last.then_inc(inverted, 1)
                        dve.wait_ge(inverted, b + 1)
                        for t in range(2):
                            last = nc.vector.tensor_tensor(att[:, 2 * b + t, :].rearrange("p (i r d) -> p r i d", r=REP, d=HD0), sums[:, t, :, :, 0:HD0],
                                                           inv[:, 2 * b + t, :].rearrange("p (i r) -> p r i", r=REP).unsqueeze(3).broadcast_to([P, REP, NKV, HD0]), ALU.mult)
                        last.then_inc(att_ready, 1)
                    dve.wait_ge(gate_up, 1)
                    nc.vector.tensor_tensor(att_t[:, :], att_t[:, :], gate_t[:, :], ALU.mult).then_inc(multiplied, 1)
                    dve.wait_ge(out_ready, 1)
                    ch.link(nc.vector.tensor_tensor(x2[:, :, :], banks[2].rearrange("p (t c) -> p t c", t=GT),
                                                    bo[:, :].unsqueeze(1).broadcast_to([P, GT, P]), ALU.add))
                    ch.link(nc.vector.tensor_tensor(x2[:, :, :], x2[:, :, :], x1(), ALU.add))
                    dve.wait_ge(x2_sq, 1)
                    ch.link(nc.vector.tensor_reduce(small[:, 0, :], sq[:, :, :], X, ALU.add))
                    nc.vector.tensor_scalar(small[:, 0, :], small[:, 0, :], 1.0 / D, 1e-6, ALU.mult, ALU.add).then_inc(r_ready, 1)
                    dve.wait_ge(r_root, 1)
                    nc.vector.reciprocal(small[:, 2, :], small[:, 1, :]).then_inc(r_ready, 1)
                    dve.wait_ge(r_ready, 2)
                    ch.link(nc.vector.tensor_tensor(h[:, :, :], x2[:, :, :], wide(small[:, 2, :]), ALU.mult))
                    dve.wait_ge(routed, 1)
                    ch.link(nc.vector.tensor_tensor(logits[:, :, :], banks[4][:, 0:GT * E].rearrange("p (t e) -> p t e", t=GT),
                                                    br[:, :].unsqueeze(1).broadcast_to([P, GT, E]), ALU.add))
                    pick_first(nc, ch, m, logits, best, pick_all[:, bass.ds(g * GT, GT), :])
            s.clear()


def pick_first(nc, ch, m, logits, best, out):
    wide = best[:, :].unsqueeze(2).broadcast_to([P, GT, E])
    ch.link(nc.vector.tensor_reduce(best[:, :], logits[:, :, :], X, ALU.max))
    ch.link(nc.vector.tensor_tensor(logits[:, :, :], logits[:, :, :], wide, ALU.is_ge))
    ch.link(nc.vector.scalar_tensor_tensor(logits[:, :, :], logits[:, :, :], -float(E), m.c("experts").unsqueeze(1).broadcast_to([P, GT, E]),
                                           ALU.mult, ALU.add))
    ch.link(nc.vector.tensor_reduce(best[:, :], logits[:, :, :], X, ALU.min))
    ch.link(nc.vector.tensor_tensor(out, logits[:, :, :], wide, ALU.is_equal))


class ExpertWeights:

    def __init__(self, nc, io, m, ctx, layer):
        s = self.memory = Memory(nc, ctx, f"weights{layer}_")
        self.F1 = 512
        self.F2 = 256 if layer == 0 else 512
        self.w1, self.w2 = s.sb("w1", [P, E, self.F1]), s.sb("w2", [P, E, self.F2 // P, P])
        self.b1, self.b2 = s.sb("b1", [P, E * self.F1 // P]), s.sb("b2", [P, E])
        self.row_w = s.sb("row_w", [P, 1])
        zeros = s.sb("zeros", [P, P])
        self.loaded, self.slots_zeroed = s.sem("loaded"), s.sem("slots_zeroed")
        self.loads = 4
        zeroed = nc.alloc_semaphore(f"zeroed{layer}")
        with nc.Block() as block:
            @block.vector
            def _(dve):
                nc.vector.memset(zeros[:, :], 0.0).then_inc(zeroed, 1)

            @block.sync
            def _(sp):
                sp.dma_start(self.b1[:, :], io[f"experts{layer}_b1"]).then_inc(self.loaded, 16)
                sp.dma_start(self.b2[:, :], io[f"experts{layer}_b2"]).then_inc(self.loaded, 16)
                sp.dma_start(self.w1[:, :, :], io[f"experts{layer}_W1"].rearrange("e d f -> d e f")).then_inc(self.loaded, 16)
                sp.dma_start(self.w2[:, :, :, :], io[f"experts{layer}_W2"].rearrange("e (c f) d -> f e c d", f=P)).then_inc(self.loaded, 16)
                if layer == 0:
                    self.loads = 5
                    sp.dma_start(self.row_w[:, :], io["ln2"]).then_inc(self.loaded, 16)
                sp.wait_ge(zeroed, 1)
                sp.dma_start(io[f"sorted{layer}"].rearrange("(t p) d -> p t d", p=P),
                             zeros[:, :].unsqueeze(1).broadcast_to([P, SLOT_TILES, P])).then_inc(self.slots_zeroed, 16)


def experts(nc, io, m, layer, weights, h_all, pick_all, y_all, norm):
    banks, c = m.banks, m.c
    F1, F2, w1, w2, b1, b2, row_w = weights.F1, weights.F2, weights.w1, weights.w2, weights.b1, weights.b2, weights.row_w
    CH = F2 // P
    slots_in, slots_out = io[f"sorted{layer}"], io[f"expert_out{layer}"]
    with ExitStack() as ctx:
        s = Memory(nc, ctx, f"moe{layer}_")
        b1_parts, b2_parts = s.sb("b1_parts", [P, 3, E * F1 // P], BF16), s.sb("b2_parts", [P, 3, E], BF16)
        b1_rows, b2_rows = s.sb("b1_rows", [P, E * F1], BF16), s.sb("b2_rows", [P, E * P], BF16)
        ones16 = s.sb("ones16", [P, P], BF16)
        PAD = 8
        counts = [s.sb(f"counts{n}", [P, PAD + TILES, E]) for n in range(2)]
        total = s.sb("total", [P, TILES, E])
        over = s.sb("over", [P, E, 16])
        ends = [s.sb(f"ends{n}", [P, PAD + E]) for n in range(2)]
        need, begin = s.sb("need", [P, E]), s.sb("begin", [P, E])
        base = s.sb("base", [P, TILES, E])
        slot_f, slot = s.sb("slot_f", [P, TILES]), s.sb("slot", [P, TILES], I32)
        past = s.sb("past", [P, SLOT_TILES, E])
        owner_f, owner = s.sb("owner_f", [P, SLOT_TILES]), s.sb("owner", [P, SLOT_TILES], I32)
        TURN = 4
        x_in = [s.sb(f"x_in{k}", [P, P]) for k in range(TURN)]
        x_t = [s.sb(f"x_t{k}", [P, P]) for k in range(2)]
        side = [s.sb(f"side{k}", [P, 256]) for k in range(2)]
        hid = [s.sb(f"hid{k}", [P, F2]) for k in range(2)]
        hid_t = [s.sb(f"hid_t{k}", [P, F2]) for k in range(2)]
        y = [s.sb(f"y{k}", [P, P]) for k in range(TURN)]

        zeroed, counted, d_done, placed, scattered = (s.sem(n) for n in ("zeroed", "counted", "d_done", "placed", "scattered"))
        split, bias_out = s.sem("split"), s.sem("bias_out")
        with nc.Block() as block:
            @block.sync
            def _(sp):
                sp.wait_ge(split, 1)
                for n in range(3):
                    sp.dma_start(b1_rows[32 * n:32 * n + 1, :], b1_parts[:, n, :]).then_inc(bias_out, 16)
                    sp.dma_start(b2_rows[32 * n:32 * n + 1, :], b2_parts[:, n, :]).then_inc(bias_out, 16)
                sp.wait_ge(bias_out, 6 * 16)

            @block.tensor
            def _(pe):
                nc.tensor.matmul(banks[0][:, 0:TILES * E], c("before"), pick_all[:, :, :], start=True, stop=True).then_inc(counted, 1)
                nc.tensor.matmul(banks[1][:, 0:TILES * E], c("ones"), pick_all[:, :, :], start=True, stop=True).then_inc(counted, 1)

            @block.gpsimd
            def _(pool):
                for t in counts:
                    nc.gpsimd.memset(t[:, 0:PAD, :], 0.0)
                for t in ends:
                    last = nc.gpsimd.memset(t[:, 0:PAD], 0.0)
                last.then_inc(zeroed, 1)
                pool.wait_ge(weights.slots_zeroed, 16)
                pool.wait_ge(placed, 1)
                for t in range(TILES):
                    nc.gpsimd.indirect_dma_start(slots_in, bass.IndirectOffsetOnAxis(ap=slot[:, t:t + 1], axis=0), h_all[:, t, :], None).then_inc(scattered, 16)
                pool.wait_ge(scattered, 16 * TILES)

            @block.vector
            def _(dve):
                ch = Chain(dve, d_done)
                dve.wait_ge(zeroed, 1)
                dve.wait_ge(counted, 2)
                tile_e = lambda t: t.rearrange("p (t e) -> p t e", e=E)
                nc.vector.tensor_copy(total[:, :, :], tile_e(banks[1][:, 0:TILES * E]))
                ch.link(nc.vector.tensor_copy(counts[0][:, PAD:, :], tile_e(banks[1][:, 0:TILES * E])))
                for n, step in enumerate((1, 2, 4, 8)):
                    a, b = counts[n % 2], counts[(n + 1) % 2]
                    ch.link(nc.vector.tensor_tensor(b[:, PAD:, :], a[:, PAD:, :], a[:, PAD - step:PAD - step + TILES, :], ALU.add))
                upto = counts[0][:, PAD:, :]
                ch.link(nc.vector.tensor_tensor(over[:, :, :], upto[:, TILES - 1, :].unsqueeze(2).broadcast_to([P, E, 16]),
                                                c("tile_starts").unsqueeze(1).broadcast_to([P, E, 16]), ALU.is_gt))
                ch.link(nc.vector.tensor_reduce(need[:, :], over[:, :, :], X, ALU.add))
                ch.link(nc.vector.tensor_copy(ends[0][:, PAD:], need[:, :]))
                for n, step in enumerate((1, 2, 4)):
                    a, b = ends[n % 2], ends[(n + 1) % 2]
                    ch.link(nc.vector.tensor_tensor(b[:, PAD:], a[:, PAD:], a[:, PAD - step:PAD - step + E], ALU.add))
                end = ends[1][:, PAD:]
                ch.link(nc.vector.tensor_tensor(begin[:, :], end, need[:, :], ALU.subtract))
                ch.link(nc.vector.tensor_tensor(base[:, :, :], upto, total[:, :, :], ALU.subtract))
                ch.link(nc.vector.scalar_tensor_tensor(base[:, :, :], begin[:, :].unsqueeze(1).broadcast_to([P, TILES, E]), float(P), base[:, :, :],
                                                       ALU.mult, ALU.add))
                ch.link(nc.vector.tensor_tensor(base[:, :, :], base[:, :, :], tile_e(banks[0][:, 0:TILES * E]), ALU.add))
                ch.link(nc.vector.tensor_tensor(base[:, :, :], base[:, :, :], pick_all[:, :, :], ALU.mult))
                ch.link(nc.vector.tensor_reduce(slot_f[:, :], base[:, :, :], X, ALU.add))
                nc.vector.tensor_copy(slot[:, :], slot_f[:, :]).then_inc(placed, 1)
                ch.link(nc.vector.tensor_tensor(past[:, :, :], c("slots").unsqueeze(2).broadcast_to([P, SLOT_TILES, E]),
                                                end.unsqueeze(1).broadcast_to([P, SLOT_TILES, E]), ALU.is_ge))
                ch.link(nc.vector.tensor_reduce(owner_f[:, :], past[:, :, :], X, ALU.add))
                ch.link(nc.vector.tensor_scalar(owner_f[:, :], owner_f[:, :], float(E - 1), None, ALU.min))
                nc.vector.tensor_copy(owner[:, :], owner_f[:, :])
                nc.vector.memset(ones16[:, :], 1.0)
                nc.vector.memset(b1_rows[:, :], 0.0)
                nc.vector.memset(b2_rows[:, :], 0.0)
                dve.wait_ge(weights.loaded, weights.loads * 16)
                if layer == 0:
                    nc.vector.tensor_scalar(w1[:, :, :], w1[:, :, :], row_w[:, 0:1], None, ALU.mult)
                for b, parts in ((b1, b1_parts), (b2, b2_parts)):
                    for n in range(3):
                        ch.link(nc.vector.tensor_copy(parts[:, n, :], b[:, :]))
                        if n < 2:
                            ch.link(nc.vector.tensor_tensor(b[:, :], b[:, :], parts[:, n, :], ALU.subtract))
                nc.vector.tensor_scalar(need[:, :], need[:, :], 1.0, None, ALU.mult).then_inc(split, 1)
        s.clear()

        x_here, y_out = [s.sem(f"x_here{k}") for k in range(TURN)], [s.sem(f"y_out{k}") for k in range(TURN)]
        turned, x_kept, raised, sided, bent, hid_turned, hid_kept, lowered, y_kept = (s.sem(n) for n in (
            "turned", "x_kept", "raised", "sided", "bent", "hid_turned", "hid_kept", "lowered", "y_kept"))
        with nc.Block() as block:
            @block.gpsimd
            def _(pool):
                for sm in y_out:
                    nc.gpsimd.sem_inc(sm, 16)

        def passed(eng, sem, j, back=0):
            if not (isinstance(j, int) and j - back < 0):
                eng.wait_ge(sem, j + (1 - back))

        def is_tile(j, back=0):
            return not isinstance(j, int) or 0 <= j - back < SLOT_TILES

        def steps(eng_fori, step):
            turns = SLOT_TILES // TURN
            for k in range(TURN):
                step(k, 0, k)
            with eng_fori(1, turns - 1) as i:
                for k in range(TURN):
                    step(i * TURN + k, i, k)
            for j in range(SLOT_TILES - TURN, SLOT_TILES + 3):
                step(j, j // TURN, j % TURN)

        with nc.Block() as block:
            @block.sync
            def _(sp):
                def load(j, k):
                    sp.dma_start(x_in[k][:, :], slots_in[bass.ds(j * P, P), :]).then_inc(x_here[k], 16)

                def step(j, i, k):
                    if is_tile(j, -TURN) and not (isinstance(j, int) and j >= SLOT_TILES - TURN):
                        passed(sp, turned, j)
                        load(j + TURN, k)
                    if is_tile(j, 3):
                        passed(sp, y_kept, j, 3)
                        sp.dma_start(slots_out[bass.ds((j - 3) * P, P), :], y[(k - 3) % TURN][:, :]).then_inc(y_out[(k - 3) % TURN], 16)

                for k in range(TURN):
                    load(k, k)
                steps(nc.sync.Fori, step)
                for k in range(TURN):
                    sp.wait_ge(y_out[k], 16 + 16 * SLOT_TILES // TURN)

            @block.tensor
            def _(pe):
                def turn_tokens(j, i, k):
                    pe.wait_ge(x_here[k], i * 16 + 16)
                    passed(pe, x_kept, j, 2)
                    nc.tensor.transpose(banks[k % 2][:, 0:P], x_in[k][:, :], c("ident")).then_inc(turned, 1)

                def step(j, i, k):
                    if is_tile(j, -1):
                        turn_tokens(j + 1, i + (k + 1) // TURN, (k + 1) % TURN)
                    if is_tile(j):
                        who = nc.tensor.value_load(owner[0:1, bass.ds(j, 1)], min_val=0, max_val=E - 1)
                        passed(pe, x_kept, j)
                        passed(pe, bent, j, 2)
                        up = banks[2 + k % 2][:, 0:F1]
                        nc.tensor.matmul(up, x_t[k % 2][:, :], w1[:, :, :].rearrange("p e f -> p (e f)")[:, bass.ds(who * F1, F1)], start=True, stop=False)
                        nc.tensor.matmul(up, ones16[:, :], b1_rows[:, bass.ds(who * F1, F1)], start=False, stop=True).then_inc(raised, 1)
                    if is_tile(j, 1):
                        passed(pe, bent, j, 1)
                        passed(pe, hid_kept, j, 3)
                        for n in range(CH):
                            last = nc.tensor.transpose(banks[4 + (k + 1) % 2][:, n * P:(n + 1) * P], hid[(k + 1) % 2][:, n * P:(n + 1) * P], c("ident"))
                        last.then_inc(hid_turned, 1)
                    if is_tile(j, 2):
                        who = nc.tensor.value_load(owner[0:1, bass.ds(j - 2, 1)], min_val=0, max_val=E - 1)
                        passed(pe, hid_kept, j, 2)
                        passed(pe, y_kept, j, 4)
                        down = banks[6 + k % 2][:, 0:P]
                        for n in range(CH):
                            nc.tensor.matmul(down, hid_t[k % 2][:, n * P:(n + 1) * P],
                                             w2[:, :, :, :].rearrange("p e c d -> p (e c d)")[:, bass.ds(who * (CH * P) + n * P, P)], start=(n == 0), stop=False)
                        nc.tensor.matmul(down, ones16[:, :], b2_rows[:, bass.ds(who * P, P)], start=False, stop=True).then_inc(lowered, 1)

                turn_tokens(0, 0, 0)
                steps(nc.tensor.Fori, step)

            @block.scalar
            def _(act):
                def step(j, i, k):
                    if is_tile(j):
                        passed(act, raised, j)
                        if layer == 0:
                            passed(act, bent, j, 2)
                            nc.scalar.activation(side[k % 2][:, :], banks[2 + k % 2][:, 256:512], ACT.Sigmoid).then_inc(sided, 1)
                        else:
                            passed(act, hid_turned, j, 2)
                            nc.scalar.activation(hid[k % 2][:, :], banks[2 + k % 2][:, 0:F2], ACT.Relu).then_inc(bent, 1)
                    if is_tile(j, 1):
                        passed(act, hid_turned, j, 1)
                        passed(act, lowered, j, 3)
                        nc.scalar.copy(hid_t[(k + 1) % 2][:, :], banks[4 + (k + 1) % 2][:, 0:F2]).then_inc(hid_kept, 1)

                steps(nc.scalar.Fori, step)

            @block.vector
            def _(dve):
                def keep_tokens(j, k):
                    passed(dve, turned, j)
                    passed(dve, raised, j, 2)
                    nc.vector.tensor_copy(x_t[k % 2][:, :], banks[k % 2][:, 0:P]).then_inc(x_kept, 1)

                def step(j, i, k):
                    if is_tile(j, -1):
                        keep_tokens(j + 1, k + 1)
                    if layer == 0 and is_tile(j):
                        passed(dve, sided, j)
                        passed(dve, hid_turned, j, 2)
                        nc.vector.tensor_tensor(hid[k % 2][:, :], banks[2 + k % 2][:, 0:256], side[k % 2][:, :], ALU.mult).then_inc(bent, 1)
                    if is_tile(j, 2):
                        passed(dve, lowered, j, 2)
                        dve.wait_ge(y_out[(k - 2) % TURN], (i + (k - 2) // TURN) * 16 + 16)
                        nc.vector.tensor_copy(y[(k - 2) % TURN][:, :], banks[6 + k % 2][:, 0:P]).then_inc(y_kept, 1)

                keep_tokens(0, 0)
                steps(nc.vector.Fori, step)
        norm_all(nc, s, slots_out, slot, norm)
        s.clear()
    weights.memory.clear()


def layer1_attention(nc, io, m, x_all, x4_all, h_all, pick_all, prob_all):
    banks, c, psum = m.banks, m.c, m.psum
    SETS = H1 // 4
    SC = 3 * P
    with ExitStack() as ctx:
        s = Memory(nc, ctx, "attn1_")
        w_in = s.sb("w_in", [P, 2, P])
        w_q, w_k, w_v = s.sb("w_q", [P, SETS, 4, 32]), s.sb("w_k", [P, SETS, 4, 32]), s.sb("w_v", [P, P])
        wo, wo_g, wr = s.sb("wo", [P, P]), s.sb("wo_g", [P, P]), s.sb("wr", [P, E])
        gamma, beta, beta_rep = s.sb("gamma", [P, 1]), s.sb("beta", [P, 1]), s.sb("beta_rep", [P, P])
        bo, br, ln_g, ln_b = s.sb("bo", [P, P]), s.sb("br", [P, E]), s.sb("ln_g", [P, P]), s.sb("ln_b", [P, P])
        theta = s.sb("theta", [P, H1])
        powers, decay = s.sb("powers", [P, H1, SC]), s.sb("decay", [P, SC])
        id16, neg16 = s.sb("id16", [P, P], BF16), s.sb("neg16", [P, P], BF16)
        x_in, x_t = s.sb("x_in", [P, GT, P]), s.sb("x_t", [P, GTOK])
        q_t, k_t = s.sb("q_t", [P, SETS, GTOK]), s.sb("k_t", [P, SETS, 4, GTOK])
        v_one = s.sb("v_one", [P, GT, H1, 32])
        sums_t = s.sb("sums_t", [P, GB, SETS, SEQ])
        scores = [s.sb(f"scores{b}", [P, H1, SC]) for b in range(GB)]
        top = s.sb("top", [P, GB, 2, H1])
        probs_t = s.sb("probs_t", [P, 3, 2, SC])
        inv = s.sb("inv", [P, GT, H1])
        out, out_n, out_t, scratch = s.sb("out", [P, GT, P]), s.sb("out_n", [P, GT, P]), s.sb("out_t", [P, GTOK]), s.sb("scratch", [P, GT, P])
        x4, z = s.sb("x4", [P, GT, P]), s.sb("z", [P, GT, P])
        var, sd = s.sb("var", [P, 3, GT * H1]), s.sb("sd", [P, 3, GT * H1])
        logits, best = s.sb("logits", [P, GT, E]), s.sb("best", [P, GT])
        exps, total = s.sb("exps", [P, GT, E]), s.sb("total", [P, GT])
        loaded, done0, decayed, negated, biased, beta_up, zeroed = (s.sem(n) for n in (
            "loaded", "done0", "decayed", "negated", "biased", "beta_up", "zeroed"))
        with nc.Block() as block:
            @block.sync
            def _(sp):
                for dst, src in ((w_in[:, 0, :], "L1_Wq"), (w_in[:, 1, :], "L1_Wk"), (w_v[:, :], "L1_Wv"), (wo[:, :], "L1_Wo"), (wr[:, :], "L1_Wr"),
                                 (gamma[:, :], "L1_gamma"), (beta[:, :], "L1_beta")):
                    sp.dma_start(dst, io[src]).then_inc(loaded, 16)
                for dst, src, n in ((bo, "L1_bo", P), (br, "L1_br", E), (ln_g, "L1_ln_g", P), (ln_b, "L1_ln_b", P), (theta, "L1_theta", H1)):
                    sp.dma_start(dst[:, :], rows(io[src], n)).then_inc(loaded, 16)

            @block.gpsimd
            def _(pool):
                nc.gpsimd.memset(v_one[:, :, :, HD1 + 1:], 0.0)
                nc.gpsimd.memset(v_one[:, :, :, HD1:HD1 + 1], 1.0)
                nc.gpsimd.memset(k_t[:, :, :, :], 0.0)
                nc.gpsimd.memset(w_q[:, :, :, :], 0.0)
                nc.gpsimd.memset(w_k[:, :, :, :], 0.0).then_inc(zeroed, 1)

            @block.scalar
            def _(act):
                act.wait_ge(negated, 1)
                for h in range(H1):
                    last = nc.scalar.activation(powers[:, h, :], c("lag"), ACT.Exp, scale=theta[:, h:h + 1])
                last.then_inc(decayed, 1)

            @block.tensor
            def _(pe):
                pe.wait_ge(beta_up, 1)
                nc.tensor.matmul(banks[0][:, 0:P], beta_rep[:, :], wo[:, :], start=True, stop=True).then_inc(biased, 1)

            @block.vector
            def _(dve):
                ch = Chain(dve, done0)
                dve.wait_ge(loaded, 12 * 16)
                dve.wait_ge(zeroed, 1)
                nc.vector.tensor_scalar(theta[:, :], theta[:, :], -1.0, None, ALU.mult).then_inc(negated, 1)
                for n, w in enumerate((w_q, w_k)):
                    nc.vector.tensor_copy(w[:, :, :, 0:HD1], w_in[:, n, :].rearrange("p (s i d) -> p s i d", s=SETS, d=HD1))
                nc.vector.tensor_copy(beta_rep[:, :], beta[:, 0:1].broadcast_to([P, P])).then_inc(beta_up, 1)
                nc.vector.tensor_scalar(wo_g[:, :], wo[:, :], gamma[:, 0:1], None, ALU.mult)
                nc.vector.tensor_copy(id16[:, :], c("ident"))
                nc.vector.tensor_copy(neg16[:, :], c("neg_ts"))
                dve.wait_ge(biased, 1)
                nc.vector.tensor_tensor(bo[:, :], bo[:, :], banks[0][:, 0:P], ALU.add)
                dve.wait_ge(decayed, 1)
                ch.link(nc.vector.tensor_reduce(decay[:, :], powers[:, :, :].rearrange("p h n -> p n h"), X, ALU.add))
                ch.link(nc.vector.tensor_scalar(decay[:, :], decay[:, :], float(HD1) ** -0.5 / H1, -1.0, ALU.mult, ALU.add))
                ch.link(nc.vector.tensor_tensor(decay[:, :], decay[:, :], c("lag_ok"), ALU.mult))
                nc.vector.tensor_scalar(decay[:, :], decay[:, :], 1.0, None, ALU.add)
        s.clear()

        with nc.Fori(0, GROUPS) as g:
            x_copied, turned, kept, projected = s.sem("x_copied"), s.sem("turned"), s.sem("kept"), s.sem("projected")
            x_now = lambda: x_all[:, bass.ds(g * GT, GT), :]
            with nc.Block() as block:
                @block.tensor
                def _(pe):
                    pe.wait_ge(x_copied, 1)
                    for t in range(GT):
                        last = nc.tensor.transpose(banks[0][:, t * P:(t + 1) * P], x_in[:, t, :], c("ident"))
                    last.then_inc(turned, 1)
                    pe.wait_ge(kept, 1)
                    for n, w in enumerate((w_q, w_k)):
                        for st in range(SETS):
                            nc.tensor.matmul(banks[1 + 2 * n + st], w[:, st, :, :].rearrange("p i d -> p (i d)"), x_t[:, :], start=True, stop=True).then_inc(projected, 1)
                    for t in range(GT):
                        last = nc.tensor.matmul(banks[5][:, t * P:(t + 1) * P], x_t[:, t * P:(t + 1) * P], w_v[:, :], start=True, stop=True)
                    last.then_inc(projected, 1)

                @block.vector
                def _(dve):
                    nc.vector.tensor_copy(x_in[:, :, :], x_now()).then_inc(x_copied, 1)
                    for st in range(SETS):
                        dve.wait_ge(projected, SETS + st + 1)
                        for i in range(4):
                            nc.vector.tensor_copy(k_t[32 * i:32 * i + 32, st, i, :], banks[1 + SETS + st][32 * i:32 * i + 32, :])
                    dve.wait_ge(projected, 2 * SETS + 1)
                    nc.vector.tensor_copy(v_one[:, :, :, 0:HD1], banks[5].rearrange("p (t h d) -> p t h d", t=GT, d=HD1))

                @block.scalar
                def _(act):
                    act.wait_ge(turned, 1)
                    nc.scalar.copy(x_t[:, :], banks[0]).then_inc(kept, 1)
                    for st in range(SETS):
                        act.wait_ge(projected, st + 1)
                        nc.scalar.copy(q_t[:, st, :], banks[1 + st])

            scored, scaled, centred, exped, flipped, moved, weighed, c_done = (s.sem(n) for n in (
                "scored", "scaled", "centred", "exped", "flipped", "moved", "weighed", "c_done"))
            copied, by_token = s.sem("copied"), s.sem("by_token")
            turns = [(b, h) for b in range(GB) for h in range(0, H1, 2)]
            N = len(turns)
            with nc.Block() as block:
                @block.tensor
                def _(pe):
                    def free(n):
                        if n - 3 >= N:
                            pe.wait_ge(moved, n - 3 - N + 1)
                        elif n >= 3:
                            pe.wait_ge(scaled, n - 3 + 1)

                    for n, (b, h0) in enumerate(turns):
                        free(n)
                        for a in range(2):
                            st, i = divmod(h0 + a, 4)
                            dst = banks[2 * (n % 3) + a]
                            t0, t1 = b * SEQ, b * SEQ + P
                            nc.tensor.matmul(dst[:, 0:P], q_t[:, st, t0:t0 + P], k_t[:, st, i, t0:t0 + P], start=True, stop=False, skip_group_check=True)
                            nc.tensor.matmul(dst[:, P:SC], q_t[:, st, t1:t1 + P], k_t[:, st, i, t0:t0 + SEQ], start=False, stop=False, skip_group_check=True)
                            nc.tensor.matmul(dst[:, 0:P], id16[:, :], neg16[:, :], start=False, stop=False, skip_group_check=True)
                            last = nc.tensor.matmul(dst[:, 2 * P:SC], id16[:, :], neg16[:, :], start=False, stop=True, skip_group_check=True)
                        last.then_inc(scored, 1)

                    def weigh(n):
                        b, h0 = turns[n]
                        pe.wait_ge(moved, n + 1)
                        for a in range(2):
                            (st, i), pr = divmod(h0 + a, 4), probs_t[:, n % 3, a, :]
                            dst = banks[6 + b][32 * i:32 * i + 32, st * SEQ:(st + 1) * SEQ]
                            nc.tensor.matmul(dst, v_one[:, 2 * b, h0 + a, :], pr[:, 0:2 * P], start=True, stop=False, skip_group_check=True)
                            last = nc.tensor.matmul(dst[:, P:], v_one[:, 2 * b + 1, h0 + a, :], pr[:, 2 * P:SC], start=False, stop=True, skip_group_check=True)
                        last.then_inc(weighed, 1)

                    for n, (b, h0) in enumerate(turns):
                        free(n + N)
                        pe.wait_ge(exped, b + 1)
                        for a in range(2):
                            for q in range(3):
                                last = nc.tensor.transpose(banks[2 * ((n + N) % 3) + a][:, q * P:(q + 1) * P], scores[b][:, h0 + a, q * P:(q + 1) * P], c("ident"))
                        last.then_inc(flipped, 1)
                        if n:
                            weigh(n - 1)
                    weigh(N - 1)
                    for b in range(GB):
                        pe.wait_ge(copied, b + 1)
                        for t in range(2):
                            for st in range(SETS):
                                last = nc.tensor.transpose(banks[b][:, (t * SETS + st) * P:(t * SETS + st + 1) * P], sums_t[:, b, st, t * P:(t + 1) * P], c("ident"))
                        last.then_inc(by_token, 1)

                @block.scalar
                def _(act):
                    def exps(b):
                        act.wait_ge(centred, b + 1)
                        nc.scalar.activation(scores[b][:, :, :], scores[b][:, :, :], ACT.Exp).then_inc(exped, 1)

                    exps(0)
                    for n in range(N):
                        if n == N // 2:
                            exps(1)
                        act.wait_ge(flipped, n + 1)
                        if n >= 3:
                            act.wait_ge(weighed, n - 2)
                        k = 2 * ((n + N) % 3)
                        nc.scalar.copy(probs_t[:, n % 3, :, :], psum[:, k:k + 2, 0:SC]).then_inc(moved, 1)

                @block.vector
                def _(dve):
                    ch = Chain(dve, c_done)
                    for n, (b, h0) in enumerate(turns):
                        dve.wait_ge(scored, n + 1)
                        k = 2 * (n % 3)
                        nc.vector.tensor_tensor(scores[b][:, h0:h0 + 2, :], psum[:, k:k + 2, 0:SC],
                                                decay[:, :].unsqueeze(1).broadcast_to([P, 2, SC]), ALU.mult).then_inc(scaled, 1)
                        if h0 == H1 - 2:
                            dve.wait_ge(scaled, n + 1)
                            parts = (scores[b][:, :, 0:P], scores[b][:, :, P:SC])
                            for q in range(2):
                                last = nc.vector.tensor_reduce(top[:, b, q, :], parts[q], X, ALU.max)
                            ch.link(last)
                            for q in range(2):
                                last = nc.vector.tensor_tensor(parts[q], parts[q], top[:, b, q, :].unsqueeze(2).broadcast_to([P, H1, parts[q].shape[2]]), ALU.subtract)
                            last.then_inc(centred, 1)
                    for b in range(GB):
                        dve.wait_ge(weighed, N // GB * (b + 1))
                        nc.vector.tensor_copy(sums_t[:, b, :, :], banks[6 + b].rearrange("p (k t) -> p k t", k=SETS)).then_inc(copied, 1)
                    for b in range(GB):
                        dve.wait_ge(by_token, b + 1)
                        o = banks[b].rearrange("p (t h d) -> p t h d", t=2, d=32)
                        ch.link(nc.vector.reciprocal(inv[:, 2 * b:2 * b + 2, :].unsqueeze(3), o[:, :, :, HD1:HD1 + 1]))
                        nc.vector.tensor_tensor(out[:, 2 * b:2 * b + 2, :].rearrange("p t (h d) -> p t h d", d=HD1), o[:, :, :, 0:HD1],
                                                inv[:, 2 * b:2 * b + 2, :].unsqueeze(3).broadcast_to([P, 2, H1, HD1]), ALU.mult)

            var_ready, sd_ready, head_normed, out_turned, out_kept, out_ready = (s.sem(n) for n in (
                "var_ready", "sd_ready", "head_normed", "out_turned", "out_kept", "out_ready"))
            x4_up, z_up, x4_turned, x4_kept, routed, shifted, raised, f_done, p_done = (s.sem(n) for n in (
                "x4_up", "z_up", "x4_turned", "x4_kept", "routed", "shifted", "raised", "f_done", "p_done"))
            with nc.Block() as block:
                @block.tensor
                def _(pe):
                    pe.wait_ge(head_normed, 1)
                    for t in range(GT):
                        last = nc.tensor.transpose(banks[0][:, t * P:(t + 1) * P], out_n[:, t, :], c("ident"))
                    last.then_inc(out_turned, 1)
                    pe.wait_ge(out_kept, 1)
                    for t in range(GT):
                        last = nc.tensor.matmul(banks[1][:, t * P:(t + 1) * P], out_t[:, t * P:(t + 1) * P], wo_g[:, :], start=True, stop=True)
                    last.then_inc(out_ready, 1)
                    pe.wait_ge(x4_up, 1)
                    for t in range(GT):
                        last = nc.tensor.transpose(banks[2][:, t * P:(t + 1) * P], x4[:, t, :], c("ident"))
                    last.then_inc(x4_turned, 1)
                    pe.wait_ge(x4_kept, 1)
                    for t in range(GT):
                        last = nc.tensor.matmul(banks[3][:, t * E:(t + 1) * E], x_t[:, t * P:(t + 1) * P], wr[:, :], start=True, stop=True)
                    last.then_inc(routed, 1)

                @block.scalar
                def _(act):
                    act.wait_ge(var_ready, 1)
                    nc.scalar.activation(sd[:, 0, :], var[:, 0, :], ACT.Sqrt).then_inc(sd_ready, 1)
                    act.wait_ge(out_turned, 1)
                    nc.scalar.copy(out_t[:, :], banks[0]).then_inc(out_kept, 1)
                    act.wait_ge(var_ready, 2)
                    nc.scalar.activation(sd[:, 1, 0:GT], var[:, 1, 0:GT], ACT.Sqrt).then_inc(sd_ready, 1)
                    act.wait_ge(x4_turned, 1)
                    nc.scalar.copy(x_t[:, :], banks[2]).then_inc(x4_kept, 1)
                    act.wait_ge(var_ready, 3)
                    nc.scalar.activation(sd[:, 2, 0:GT], var[:, 2, 0:GT], ACT.Sqrt).then_inc(sd_ready, 1)
                    act.wait_ge(shifted, 1)
                    nc.scalar.activation(exps[:, :, :], exps[:, :, :], ACT.Exp).then_inc(raised, 1)

                @block.gpsimd
                def _(pool):
                    pool.wait_ge(x4_up, 1)
                    nc.gpsimd.tensor_copy(x4_all[:, bass.ds(g * GT, GT), :], x4[:, :, :])
                    pool.wait_ge(z_up, 1)
                    row = lambda t: t[:, :].unsqueeze(1).broadcast_to([P, GT, P])
                    nc.gpsimd.tensor_tensor(scratch[:, :, :], z[:, :, :], row(ln_g), ALU.mult).then_inc(p_done, 1)
                    pool.wait_ge(p_done, 1)
                    nc.gpsimd.tensor_tensor(h_all[:, bass.ds(g * GT, GT), :], scratch[:, :, :], row(ln_b), ALU.add)

                @block.vector
                def _(dve):
                    ch = Chain(dve, f_done)
                    by_head = lambda t: t[:, :, :].rearrange("p t (h d) -> p (t h) d", d=HD1)
                    layer_norm(nc, dve, ch, by_head(out), by_head(scratch), by_head(out_n), var[:, 0, :], sd[:, 0, :], var_ready, sd_ready, 1)
                    nc.vector.tensor_scalar(total[:, :], sd[:, 0, 0:GT], 1.0, None, ALU.mult).then_inc(head_normed, 1)
                    dve.wait_ge(out_ready, 1)
                    ch.link(nc.vector.tensor_tensor(x4[:, :, :], banks[1].rearrange("p (t c) -> p t c", t=GT), bo[:, :].unsqueeze(1).broadcast_to([P, GT, P]), ALU.add))
                    ch.link(nc.vector.tensor_tensor(z[:, :, :], x4[:, :, :], x_now(), ALU.add))
                    layer_norm(nc, dve, ch, z[:, :, :], scratch[:, :, :], x4[:, :, :], var[:, 1, 0:GT], sd[:, 1, 0:GT], var_ready, sd_ready, 2)
                    ch.link(nc.vector.tensor_copy(out[:, :, :], x4[:, :, :]))
                    nc.vector.tensor_scalar(total[:, :], sd[:, 1, 0:GT], 1.0, None, ALU.mult).then_inc(x4_up, 1)
                    layer_norm(nc, dve, ch, out[:, :, :], scratch[:, :, :], z[:, :, :], var[:, 2, 0:GT], sd[:, 2, 0:GT], var_ready, sd_ready, 3)
                    ch.link(nc.vector.tensor_scalar(total[:, :], sd[:, 2, 0:GT], 1.0, None, ALU.mult))
                    nc.vector.tensor_copy(best[:, :], total[:, :]).then_inc(z_up, 1)
                    dve.wait_ge(routed, 1)
                    ch.link(nc.vector.tensor_tensor(logits[:, :, :], banks[3][:, 0:GT * E].rearrange("p (t e) -> p t e", t=GT),
                                                    br[:, :].unsqueeze(1).broadcast_to([P, GT, E]), ALU.add))
                    ch.link(nc.vector.tensor_reduce(total[:, :], logits[:, :, :], X, ALU.max))
                    nc.vector.tensor_tensor(exps[:, :, :], logits[:, :, :], total[:, :].unsqueeze(2).broadcast_to([P, GT, E]), ALU.subtract).then_inc(shifted, 1)
                    dve.wait_ge(raised, 1)
                    ch.link(nc.vector.tensor_reduce(total[:, :], exps[:, :, :], X, ALU.add))
                    nc.vector.reciprocal(prob_all[:, bass.ds(g * GT, GT)], total[:, :])
                    pick_first(nc, ch, m, logits, best, pick_all[:, bass.ds(g * GT, GT), :])
            s.clear()


class Norm:

    def __init__(self, a, y, out, scale, scratch, store=None):
        self.a, self.y, self.out, self.scale, self.scratch, self.store = a, y, out, scale, scratch, store


def norm_all(nc, s, slots_out, slot, norm):
    STEPS = 4
    n = TILES // STEPS
    a, y, out, scale, scratch, store = norm.a, norm.y, norm.out, norm.scale, norm.scratch, norm.store
    var, sd = s.sb("var", [P, TILES]), s.sb("sd", [P, TILES])
    var_ready, sd_ready, done, normed, stored = (s.sem(x) for x in ("var_ready", "sd_ready", "done", "normed", "stored"))
    gathered = [s.sem(f"gathered{k}") for k in range(STEPS)]
    with nc.Block() as block:
        @block.gpsimd
        def _(pool):
            for t in range(TILES):
                nc.gpsimd.indirect_dma_start(y[:, t, :], None, slots_out, bass.IndirectOffsetOnAxis(ap=slot[:, t:t + 1], axis=0)).then_inc(gathered[t // n], 16)

        @block.scalar
        def _(act):
            for k in range(STEPS):
                act.wait_ge(var_ready, k + 1)
                nc.scalar.activation(sd[:, n * k:n * k + n], var[:, n * k:n * k + n], ACT.Sqrt).then_inc(sd_ready, 1)

        @block.vector
        def _(dve):
            ch = Chain(dve, done)
            for k in range(STEPS):
                at = slice(n * k, n * k + n)
                dve.wait_ge(gathered[k], 16 * n)
                if scale is not None:
                    ch.link(nc.vector.tensor_tensor(y[:, at, :], y[:, at, :], scale[:, at].unsqueeze(2).broadcast_to([P, n, P]), ALU.mult))
                ch.link(nc.vector.tensor_tensor(y[:, at, :], y[:, at, :], a[:, at, :], ALU.add))
                layer_norm(nc, dve, ch, y[:, at, :], scratch[:, at, :], out[:, at, :], var[:, at], sd[:, at], var_ready, sd_ready, k + 1)
                nc.vector.tensor_copy(var[:, at], sd[:, at]).then_inc(normed, 1)

        @block.sync
        def _(sp):
            if store is not None:
                for k in range(STEPS):
                    sp.wait_ge(normed, k + 1)
                    sp.dma_start(store.rearrange("(t p) d -> p t d", p=P)[:, n * k:n * k + n, :], out[:, n * k:n * k + n, :]).then_inc(stored, 16)
                sp.wait_ge(stored, 16 * STEPS)


def laid_out(i):
    a = {"consts": constants(), "x": i["L0_attn_hidden_states"].reshape(TOKENS, D)}
    for n in ("q", "k", "v"):
        a[f"W{n}_t"] = i[f"L0_attn_W{n}"].T
        a[f"conv_{n}_t"] = i[f"L0_attn_conv_{n}_w"].T.reshape(-1)
    a["Wb_t"] = i["L0_attn_Wb"].T
    a["w_qkv"] = np.concatenate([i[f"L0_ffn_W{n}"] for n in "qkv"], 1)
    a["b_qkv"] = np.concatenate([i[f"L0_ffn_b{n}"] for n in "qkv"])
    a["qk_w"] = np.concatenate([np.tile(i["L0_ffn_qn_w"], NQ), np.tile(i["L0_ffn_kn_w"], NKV)])
    a["ffn_Wo"], a["ffn_bo"], a["ffn_Wr"], a["ffn_br"] = (i[f"L0_ffn_{n}"] for n in ("Wo", "bo", "Wr", "br"))
    a["Wg_tiled"] = np.tile(i["L0_ffn_Wg"], (NQ, NQ))
    a["bg_tiled"] = np.tile(i["L0_ffn_bg"], NQ).reshape(P, 1)
    a["ln1"], a["ln2"] = i["L0_ffn_ln1_w"].reshape(P, 1), i["L0_ffn_ln2_w"].reshape(P, 1)
    for n in range(2):
        a[f"experts{n}_W1"], a[f"experts{n}_W2"] = i[f"L{n}_ffn_W1"], i[f"L{n}_ffn_W2"]
        a[f"experts{n}_b1"], a[f"experts{n}_b2"] = i[f"L{n}_ffn_b1"].reshape(P, -1), i[f"L{n}_ffn_b2"].reshape(P, -1)
    for n in ("Wq", "Wk", "Wv", "Wo", "bo", "theta"):
        a[f"L1_{n}"] = i[f"L1_attn_{n}"]
    a["L1_gamma"], a["L1_beta"] = i["L1_attn_gamma"].reshape(P, 1), i["L1_attn_beta"].reshape(P, 1)
    for n in ("Wr", "br", "ln_g", "ln_b"):
        a[f"L1_{n}"] = i[f"L1_ffn_{n}"]
    a["gate_w1x_t"] = i["L0_attn_gate_W1"][:, :D].T
    a["gate_w1s_t"] = i["L0_attn_gate_W1"][:, D:].T
    a["gate_w2_t"] = i["L0_attn_gate_W2"].T
    a["gate_b1"] = i["L0_attn_gate_b1"].reshape(P, 1)
    a["gate_b2"] = i["L0_attn_gate_b2"]
    a["copy_bias"] = i["L0_attn_gate_copy_bias"]
    a["log_temp"] = i["L0_attn_gate_log_temp"]
    a["o_norm"] = i["L0_attn_o_norm_w"].reshape(DK, 1)
    a["Wo_t"] = i["L0_attn_Wo"].T
    a["fir_short"] = i["L0_attn_fir_short_filt"].reshape(P, FIRS)
    a["fir_long_rev"] = i["L0_attn_fir_long_filt"].reshape(P, FIRL)[:, ::-1]
    return a


def kernel(**inputs):
    import concourse.bacc as bacc
    from concourse.bass_utils import run_bass_kernel_spmd

    nc = bacc.Bacc("TRN2", target_bir_lowering=False, num_devices=1)
    arrays = {k: np.ascontiguousarray(v) for k, v in laid_out(inputs).items()}
    io = {k: nc.dram_tensor(k, v.shape, mybir.dt.from_np(v.dtype), kind="ExternalInput").ap() for k, v in arrays.items()}
    for name, shape in SCRATCH.items():
        io[name] = nc.dram_tensor(name, shape, F32, kind="Internal").ap()
    out = nc.dram_tensor("out", (TOKENS, D), F32, kind="ExternalOutput").ap()
    build_program(nc, io, out)
    got = run_bass_kernel_spmd(nc, [arrays], core_ids=[0]).results[0]["out"]
    return got.reshape(BATCH, SEQ, D)
```

```python
from contextlib import ExitStack

import numpy as np
import concourse.bass as bass
from concourse import mybir

F32 = mybir.dt.float32
BF16 = mybir.dt.bfloat16
I32 = mybir.dt.int32
ALU = mybir.AluOpType
ACT = mybir.ActivationFunctionType
X = mybir.AxisListType.X

P = 128
BATCH, SEQ, D = 8, 256, 128
TOKENS = BATCH * SEQ
TILES = TOKENS // P
GT = 4
GTOK = GT * P
GB = GTOK // SEQ
GROUPS = TOKENS // GTOK
H0, DK = 4, 32
CHUNK = 32
GCH = GTOK // CHUNK
SCH = SEQ // CHUNK
CONV, FIRS, FIRL = 4, 5, 64
FBLK = TOKENS // FIRL
NBR, NSTAT = 4, 4
DECAY = 1.0 - 1.0 / 3000.0
EPS_FLOOR = 0.08 * DECAY
NQ, NKV, HD0 = 16, 4, 8
REP = NQ // NKV
H1, HD1 = 8, 16
E = 8
SLOT_TILES = TILES + E
NEG = -30000.0

CONST_PARTS = [("ident", 128), ("before", 128), ("ones", 128), ("upto", 128), ("neg_ts", 128),
               ("causal_t", 32), ("cos", 8), ("sin", 8), ("lag", 384), ("lag_ok", 384),
               ("tile_starts", 16), ("experts", 8), ("slots", SLOT_TILES), ("head_ones", 128),
               ("token_ids", TILES), ("empty_ids", SLOT_TILES),
               ("minus_upper", 32), ("sum_rows", 64), ("pick_rows", 32), ("eps6", 1), ("eps5", 1)]
CONST_AT, _n = {}, 0
for _name, _w in CONST_PARTS:
    CONST_AT[_name] = (_n, _n + _w)
    _n += _w
CONST_W = _n


def constants():
    c = np.zeros((P, CONST_W), np.float32)

    def put(name, a):
        lo, hi = CONST_AT[name]
        c[:, lo:hi] = a

    i, j = np.arange(P)[:, None], np.arange(P)[None, :]
    put("ident", i == j)
    put("before", i < j)
    put("head_ones", i // HD0 == j // HD0)
    put("ones", 1.0)
    put("upto", i <= j)
    put("neg_ts", np.where(j > i, NEG, 0.0))
    r, k = i % CHUNK, np.arange(CHUNK)[None, :]
    put("causal_t", k >= r)
    put("minus_upper", np.where(k > r, -1.0, 0.0))
    col = np.arange(2 * 32)[None, :]
    put("sum_rows", col % 32 == H0 * (col // 32) + i // DK)
    col = np.arange(GT * 2 * H0)[None, :]
    put("pick_rows", i == 32 * (col // (2 * H0)) + col % (2 * H0))
    put("eps6", 1e-6)
    put("eps5", 1e-5)
    half = HD0 // 2
    freq = (np.float32(1.0) / np.float32(10000.0) ** (np.arange(0, HD0, 2, dtype=np.float32) / np.float32(HD0))).astype(np.float32)
    ang = np.arange(SEQ, dtype=np.float32)[:, None] * freq[None, :]
    put("cos", np.cos(ang).reshape(2, P, half).transpose(1, 0, 2).reshape(P, 8))
    put("sin", np.sin(ang).reshape(2, P, half).transpose(1, 0, 2).reshape(P, 8))
    lag = np.concatenate([i - j, i + P - np.arange(SEQ)[None, :]], 1)
    put("lag", np.maximum(lag, 0))
    put("lag_ok", lag >= 0)
    put("tile_starts", np.arange(16)[None, :] * P)
    put("experts", np.arange(E)[None, :])
    put("slots", np.arange(SLOT_TILES)[None, :])
    put("token_ids", np.arange(TILES)[None, :] * P + i)
    put("empty_ids", TOKENS + np.arange(SLOT_TILES)[None, :] * P + i)
    return c


SCRATCH = {"taps_padded": (2 * P, P), "sorted0": (SLOT_TILES * P, P + 1), "sorted1": (SLOT_TILES * P, P + 1),
           "expert_out0": (TOKENS + SLOT_TILES * P, P), "expert_out1": (TOKENS + SLOT_TILES * P, P)}


def rows(ap, n):
    return bass.AP(ap.tensor, 0, [[0, P], [1, n]])


def last_first(ap):
    *outer, (step, n) = [list(d) for d in ap.ap]
    return bass.AP(ap.tensor, ap.offset + step * (n - 1), [*outer, [-step, n]])


class Chain:

    def __init__(self, eng, done):
        self.eng, self.done, self.n = eng, done, 0

    def link(self, ins):
        self.n += 1
        ins.then_inc(self.done, 1)
        self.eng.wait_ge(self.done, self.n)


class Memory:

    def __init__(self, nc, ctx, stage=""):
        self.nc, self.ctx, self.stage, self.sems = nc, ctx, stage, []

    def sb(self, name, shape, dt=F32):
        return self.ctx.enter_context(self.nc.sbuf_tensor(self.stage + name, list(shape), dt))

    def sem(self, name):
        s = self.nc.alloc_semaphore(self.stage + name)
        self.sems.append(s)
        return s

    def clear(self):
        nums = sorted(s.num for s in self.sems)
        for lo in [n for n in nums if n - 1 not in nums]:
            hi = lo
            while hi in nums:
                hi += 1
            self.nc.sync.sem_clear(range(lo, hi))
        self.nc.all_engine_barrier()
        for s in self.sems:
            self.nc.release_semaphore(s)
        self.sems = []


class MixerParameters:

    def __init__(self, nc, ctx):
        s = self.memory = Memory(nc, ctx, "mixer_params_")
        self.w1_x, self.w1_s, self.w2_t = s.sb("w1_x", [P, P]), s.sb("w1_s", [P, H0, P]), s.sb("w2_t", [P, 32])
        self.b1, self.wo, self.o_norm, self.taps = s.sb("b1", [P, 1]), s.sb("wo", [P, P]), s.sb("o_norm", [P, 1]), s.sb("taps", [P, FIRS])
        self.b2, self.copy_bias, self.log_temp = s.sb("b2", [P, NBR]), s.sb("copy_bias", [P, H0]), s.sb("log_temp", [P, H0])
        self.loaded, self.zeroed = s.sem("loaded"), s.sem("zeroed")
        self.loads = 16

    def clear_rest(self, nc, pool):
        nc.gpsimd.memset(self.w2_t[:, :], 0.0)
        nc.gpsimd.memset(self.w1_s[:, :, :], 0.0).then_inc(self.zeroed, 1)

    def fetch(self, io, sp):
        for dst, src in ((self.w1_x, "gate_w1x_t"), (self.wo, "Wo_t"), (self.taps, "fir_short"), (self.b1, "gate_b1")):
            sp.dma_start(dst[:, :], io[src]).then_inc(self.loaded, 16)
        for dst, src, n in ((self.b2, "gate_b2", NBR), (self.copy_bias, "copy_bias", H0), (self.log_temp, "log_temp", H0)):
            sp.dma_start(dst[:, :], rows(io[src], n)).then_inc(self.loaded, 16)
        sp.wait_ge(self.zeroed, 1)
        sp.dma_start(self.w2_t[:, 0:NBR], io["gate_w2_t"]).then_inc(self.loaded, 16)
        for h in range(H0):
            sp.dma_start(self.w1_s[32 * h:32 * h + 16, h, :], io["gate_w1s_t"]).then_inc(self.loaded, 16)
            sp.dma_start(self.o_norm[32 * h:32 * h + 32, :], io["o_norm"]).then_inc(self.loaded, 16)


class Attention0Parameters:

    def __init__(self, nc, ctx):
        s = self.memory = Memory(nc, ctx, "attn0_params_")
        self.w_qkv, self.wo, self.wg = s.sb("w_qkv", [P, (NQ + 2 * NKV) * HD0]), s.sb("wo", [P, P]), s.sb("wg", [P, P])
        self.wr, self.ln1, self.ln2, self.bg = s.sb("wr", [P, E]), s.sb("ln1", [P, 1]), s.sb("ln2", [P, 1]), s.sb("bg", [P, 1])
        self.b_qkv, self.qk_w = s.sb("b_qkv", [P, (NQ + 2 * NKV) * HD0]), s.sb("qk_w", [P, (NQ + NKV) * HD0])
        self.bo, self.br = s.sb("bo", [P, P]), s.sb("br", [P, E])
        self.loaded, self.loads = s.sem("loaded"), 11

    def fetch(self, io, sp):
        for dst, src in ((self.w_qkv, "w_qkv"), (self.wo, "ffn_Wo"), (self.wg, "Wg_tiled"), (self.wr, "ffn_Wr"), (self.ln1, "ln1"), (self.ln2, "ln2"),
                         (self.bg, "bg_tiled")):
            sp.dma_start(dst[:, :], io[src]).then_inc(self.loaded, 16)
        for dst, src in ((self.b_qkv, "b_qkv"), (self.qk_w, "qk_w"), (self.bo, "ffn_bo"), (self.br, "ffn_br")):
            sp.dma_start(dst[:, :], rows(io[src], dst.shape[1])).then_inc(self.loaded, 16)


class Attention1Parameters:

    def __init__(self, nc, ctx):
        s = self.memory = Memory(nc, ctx, "attn1_params_")
        self.w_in, self.w_v, self.wo, self.wr = s.sb("w_in", [P, 2, P]), s.sb("w_v", [P, P]), s.sb("wo", [P, P]), s.sb("wr", [P, E])
        self.gamma, self.beta, self.theta = s.sb("gamma", [P, 1]), s.sb("beta", [P, 1]), s.sb("theta", [P, H1])
        self.bo, self.br, self.ln_g, self.ln_b = s.sb("bo", [P, P]), s.sb("br", [P, E]), s.sb("ln_g", [P, P]), s.sb("ln_b", [P, P])
        self.loaded, self.loads = s.sem("loaded"), 12
        self.decay, self.negated, self.decayed = s.sb("decay", [P, 3 * P]), s.sem("negated"), s.sem("decayed")

    def negate(self, nc, dve):
        dve.wait_ge(self.loaded, 16 * self.loads)
        nc.vector.tensor_scalar(self.theta[:, :], self.theta[:, :], -1.0, None, ALU.mult).then_inc(self.negated, 1)

    def raise_powers(self, nc, m, act, powers):
        act.wait_ge(self.negated, 1)
        for h in range(H1):
            last = nc.scalar.activation(powers[:, h, :], m.c("lag"), ACT.Exp, scale=self.theta[:, h:h + 1])
        last.then_inc(self.decayed, 1)

    def sum_powers(self, nc, m, dve, ch, powers):
        decay = self.decay
        dve.wait_ge(self.decayed, 1)
        ch.link(nc.vector.tensor_reduce(decay[:, :], powers[:, :, :].rearrange("p h n -> p n h"), X, ALU.add))
        ch.link(nc.vector.tensor_scalar(decay[:, :], decay[:, :], float(HD1) ** -0.5 / H1, -1.0, ALU.mult, ALU.add))
        ch.link(nc.vector.tensor_tensor(decay[:, :], decay[:, :], m.c("lag_ok"), ALU.mult))
        nc.vector.tensor_scalar(decay[:, :], decay[:, :], 1.0, None, ALU.add)

    def fetch(self, io, sp):
        for dst, src in ((self.w_in[:, 0, :], "L1_Wq"), (self.w_in[:, 1, :], "L1_Wk"), (self.w_v[:, :], "L1_Wv"), (self.wo[:, :], "L1_Wo"),
                         (self.wr[:, :], "L1_Wr"), (self.gamma[:, :], "L1_gamma"), (self.beta[:, :], "L1_beta")):
            sp.dma_start(dst, io[src]).then_inc(self.loaded, 16)
        for dst, src in ((self.bo, "L1_bo"), (self.br, "L1_br"), (self.ln_g, "L1_ln_g"), (self.ln_b, "L1_ln_b"), (self.theta, "L1_theta")):
            sp.dma_start(dst[:, :], rows(io[src], dst.shape[1])).then_inc(self.loaded, 16)


def build_program(nc, io, out):
    ctx = ExitStack()
    with ctx:
        shared = Memory(nc, ctx)
        psum = ctx.enter_context(nc.psum_tensor("psum", [P, 8, 512], F32))
        banks = [psum[:, i, :] for i in range(8)]
        shared.psum = psum
        cst = shared.sb("cst", [P, CONST_W])
        shared.banks, shared.cst = banks, cst
        shared.c = lambda name: cst[:, CONST_AT[name][0]:CONST_AT[name][1]]
        x1_all = shared.sb("x1_all", [P, TILES, P])
        attention0 = Attention0Parameters(nc, ctx)
        attention1 = Attention1Parameters(nc, ctx)
        layer0_mixer(nc, io, shared, x1_all, (attention0, attention1))
        shared.empty = shared.sb("empty", [P, SLOT_TILES, P + 1])
        res_all = shared.sb("res_all", [P, TILES, P])
        h_all = shared.sb("h_all", [P, TILES, P + 1])
        pick_all = shared.sb("pick_all", [P, TILES, E])
        prob_all = shared.sb("prob_all", [P, TILES])
        with ExitStack() as weights_ctx:
            weights = ExpertWeights(nc, io, shared, weights_ctx, 0)
            layer0_attention(nc, shared, attention0, weights, x1_all, res_all, h_all, pick_all)
            experts(nc, io, shared, 0, weights, h_all, pick_all, Norm(res_all, x1_all, res_all), attention1)
        x4_all = x1_all
        with ExitStack() as weights_ctx:
            weights = ExpertWeights(nc, io, shared, weights_ctx, 1)
            layer1_attention(nc, shared, attention1, weights, res_all, x4_all, h_all, pick_all, prob_all)
            experts(nc, io, shared, 1, weights, h_all, pick_all, Norm(x4_all, res_all, x4_all, prob_all, out))


def layer0_mixer(nc, io, m, x1_all, next_params):
    with ExitStack() as ctx:
        lay = Memory(nc, ctx)
        x_t = lay.sb("x_t", [P, GROUPS * GB, CONV - 1 + SEQ])
        q_t = lay.sb("q_t", [P, GROUPS, GTOK])
        k_t = lay.sb("k_t", [P, GROUPS, GTOK])
        v_t = lay.sb("v_t", [P, GROUPS * GB, FIRL + SEQ])
        beta_t = lay.sb("beta_t", [P, GROUPS, GTOK])
        fir_long = lay.sb("fir_long", [P, TILES, P])
        x_all = lay.sb("x_all", [P, TILES, P])
        params = MixerParameters(nc, ctx)
        with ExitStack() as filter_ctx:
            fir = Memory(nc, filter_ctx, "fir_")
            tri = fir.sb("tri", [P, P, FIRL])
            tri_here = fir.sem("tri_here")
            project(nc, io, m, x_all, x_t, q_t, k_t, v_t, beta_t, tri, tri_here)
            long_filter(nc, io, m, v_t, fir_long, tri, tri_here, params, next_params)
            fir.clear()
        delta_and_gate(nc, m, params, x_all, x_t, q_t, k_t, v_t, beta_t, fir_long, x1_all)


def project(nc, io, m, x_all, x_t, q_t, k_t, v_t, beta_t, tri, tri_here):
    banks, c = m.banks, m.c
    with ExitStack() as ctx:
        s = Memory(nc, ctx, "project_")
        w_t = s.sb("w_t", [P, 3, P])
        taps = s.sb("taps", [P, 3, CONV, P])
        w_conv = s.sb("w_conv", [P, 3, CONV, P])
        wb = s.sb("wb", [P, H0])
        wb_rep = s.sb("wb_rep", [P, H0, DK])
        half = s.sb("half", [P, 6, GTOK])
        x_here = s.sb("x_here", [P, 2 * GT, P])
        long_taps = s.sb("long_taps", [P, P])
        loaded, scaled, zeroed, x_loaded = s.sem("weights_loaded"), s.sem("weights_scaled"), s.sem("pads_zeroed"), s.sem("x_loaded")
        const_loaded = s.sem("const_loaded")
        taps_here, taps_zeroed, taps_out = s.sem("taps_here"), s.sem("taps_zeroed"), s.sem("taps_out")
        pad = io["taps_padded"]
        with nc.Block() as block:
            @block.sync
            def _(sp):
                sp.wait_ge(taps_zeroed, 1)
                sp.dma_start(long_taps[:, 0:FIRL], io["fir_long_rev"]).then_inc(taps_here, 16)
                sp.dma_start(x_all[:, :, :], io["x"].rearrange("(n p) d -> p n d", p=P)).then_inc(x_loaded, 16)
                sp.wait_ge(taps_here, 16)
                sp.dma_start(pad[P:2 * P, :], long_taps[:, :]).then_inc(taps_out, 16)
                sp.dma_start(pad[0:P, FIRL:P], long_taps[:, FIRL:P]).then_inc(taps_out, 16)
                sp.wait_ge(x_loaded, 16)
                sp.wait_ge(taps_out, 32)
                for q in range(4):
                    sp.dma_start(tri[32 * q:32 * q + 32, :, :],
                                 bass.AP(pad.tensor, P * P + 1 - FIRL + 32 * q, [[1, 32], [P, P], [1, FIRL]])).then_inc(tri_here, 16)

            @block.scalar
            def _(act):
                for n, name in enumerate(("q", "k", "v")):
                    act.dma_start(w_t[:, n, :], io[f"W{name}_t"]).then_inc(loaded, 16)
                    act.dma_start(taps[:, n, :, :], rows(io[f"conv_{name}_t"], CONV * P)).then_inc(loaded, 16)
                act.dma_start(wb[:, :], io["Wb_t"]).then_inc(loaded, 16)
                act.dma_start(m.cst[:, :], io["consts"]).then_inc(const_loaded, 16)
                act.wait_ge(const_loaded, 16)

            @block.gpsimd
            def _(pool):
                nc.gpsimd.memset(long_taps[:, :], 0.0).then_inc(taps_zeroed, 1)
                nc.gpsimd.memset(x_t[:, :, 0:CONV - 1], 0.0)
                nc.gpsimd.memset(v_t[:, :, 0:FIRL], 0.0).then_inc(zeroed, 1)

            @block.vector
            def _(dve):
                dve.wait_ge(loaded, 7 * 16)
                for n in range(3):
                    nc.vector.tensor_tensor(w_conv[:, n, :, :], w_t[:, n, :].unsqueeze(1).broadcast_to([P, CONV, P]),
                                            taps[:, n, :, :], ALU.mult)
                nc.vector.tensor_copy(wb_rep[:, :, :], wb[:, :].unsqueeze(2).broadcast_to([P, H0, DK])).then_inc(scaled, 1)
        s.clear()
        with nc.Fori(0, GROUPS // 2) as pair:
            x_copied, x_turned, x_kept, projected, sigmoid = s.sem("x_copied"), s.sem("x_turned"), s.sem("x_kept"), s.sem("projected"), s.sem("sigmoid")
            sequences = lambda k: bass.ds(pair * (2 * GB) + k * GB, GB)
            with nc.Block() as block:
                @block.tensor
                def _(pe):
                    for k in range(2):
                        pe.wait_ge(x_copied, k + 1)
                        for t in range(GT):
                            last = nc.tensor.transpose(banks[4 * k][:, t * P:(t + 1) * P], x_here[:, k * GT + t, :], c("ident"))
                        last.then_inc(x_turned, 1)
                    for k in range(2):
                        pe.wait_ge(x_kept, k + 1)
                        nc.tensor.matmul(banks[4 * k][:, :], wb_rep[:, :, :], x_t[:, sequences(k), CONV - 1:CONV - 1 + SEQ],
                                         start=True, stop=True).then_inc(projected, 1)
                        for n in range(3):
                            for j in range(CONV):
                                last = nc.tensor.matmul(banks[4 * k + 1 + n][:, :], w_conv[:, n, j, :], x_t[:, sequences(k), j:j + SEQ],
                                                        start=(j == 0), stop=(j == CONV - 1))
                            last.then_inc(projected, 1)

                @block.scalar
                def _(act):
                    for k in range(2):
                        act.wait_ge(projected, 4 * k + 1)
                        nc.scalar.activation(beta_t[:, bass.ds(pair * 2 + k, 1), :], banks[4 * k][:, :].unsqueeze(1), ACT.Sigmoid)
                        for n in range(3):
                            act.wait_ge(projected, 4 * k + n + 2)
                            nc.scalar.activation(half[:, 3 * k + n, :], banks[4 * k + 1 + n][:, :], ACT.Sigmoid).then_inc(sigmoid, 1)

                @block.vector
                def _(dve):
                    by_sequence = lambda t: t.rearrange("p (b t) -> p b t", b=GB)
                    for k in range(2):
                        nc.vector.tensor_copy(x_here[:, k * GT:(k + 1) * GT, :], x_all[:, bass.ds(pair * (2 * GT) + k * GT, GT), :]).then_inc(x_copied, 1)
                    for k in range(2):
                        dve.wait_ge(x_turned, k + 1)
                        nc.vector.tensor_copy(x_t[:, sequences(k), CONV - 1:], by_sequence(banks[4 * k][:, :])).then_inc(x_kept, 1)
                    for k in range(2):
                        for n, dst in enumerate((q_t, k_t)):
                            dve.wait_ge(sigmoid, 3 * k + n + 1)
                            nc.vector.tensor_tensor(dst[:, bass.ds(pair * 2 + k, 1), :], half[:, 3 * k + n:3 * k + n + 1, :], banks[4 * k + 1 + n][:, :].unsqueeze(1), ALU.mult)
                        dve.wait_ge(sigmoid, 3 * k + 3)
                        nc.vector.tensor_tensor(v_t[:, sequences(k), FIRL:], by_sequence(half[:, 3 * k + 2, :]), by_sequence(banks[4 * k + 3][:, :]), ALU.mult)
            s.clear()


def long_filter(nc, io, m, v_t, fir_long, tri, tri_here, params, next_params):
    banks, c = m.banks, m.c
    with ExitStack() as ctx:
        s = Memory(nc, ctx, "filter_")
        win = s.sb("win", [P, P, FBLK])
        turned, kept, filtered, reversed_ = s.sem("turned"), s.sem("kept"), s.sem("filtered"), s.sem("reversed")
        v_back = s.sb("v_back", [P, (TOKENS // SEQ) * (FIRL + SEQ)])

        def unload(eng, copy, first):
            for k in range(first, 8, 2):
                eng.wait_ge(filtered, k + 1)
                for half in range(2):
                    copy(fir_long[64 * half:64 * half + 64, :, 16 * k:16 * k + 16],
                         banks[k][0:64, :].rearrange("p (c t h) -> p t c h", c=16, h=2)[:, :, :, half])

        with nc.Block() as block:
            @block.gpsimd
            def _(pool):
                params.clear_rest(nc, pool)

            @block.sync
            def _(sp):
                params.fetch(io, sp)
                for later in next_params:
                    later.fetch(io, sp)

            @block.vector
            def _(dve):
                width, parts = v_back.shape[1], 4
                backwards = last_first(v_t[:, :, :].rearrange("p b t -> p (b t)"))
                for n in range(parts - 1, -1, -1):
                    at = slice(n * width // parts, (n + 1) * width // parts)
                    nc.vector.tensor_copy(v_back[:, at], backwards[:, at]).then_inc(reversed_, 1)
                for w in range(0, FBLK, 8):
                    dve.wait_ge(turned, w // 4 + 2)
                    for k in range(2):
                        b = (w // 4 + k) % 4
                        nc.vector.tensor_copy(win[:, :, w + 4 * k:w + 4 * k + 4],
                                              banks[b][:, :].rearrange("p (w c) -> p c w", w=4)).then_inc(kept, 1)
                unload(dve, nc.vector.tensor_copy, 0)

            @block.scalar
            def _(act):
                unload(act, nc.scalar.copy, 1)

            @block.tensor
            def _(pe):
                for w in range(FBLK):
                    if w % 8 == 0:
                        pe.wait_ge(reversed_, w // 8 + 1)
                    if w >= 16 and w % 4 == 0:
                        pe.wait_ge(kept, w // 4 - 3)
                    end, at = (TOKENS // SEQ) * (FIRL + SEQ), (w // 4) * (FIRL + SEQ) + FIRL * (w % 4)
                    last = nc.tensor.transpose(banks[(w // 4) % 4][:, (w % 4) * P:(w % 4 + 1) * P], v_back[:, end - at - P:end - at], c("ident"))
                    if w % 4 == 3:
                        last.then_inc(turned, 1)
                pe.wait_ge(kept, 8)
                pe.wait_ge(tri_here, 64)
                for ch in range(P):
                    last = nc.tensor.matmul(banks[ch // 16][0:64, (ch % 16) * FBLK:(ch % 16 + 1) * FBLK],
                                            tri[:, ch, :], win[:, ch, :], start=True, stop=True)
                    if ch % 16 == 15:
                        last.then_inc(filtered, 1)
        s.clear()


def head_block(t, h, width=CHUNK):
    return t[h * width:(h + 1) * width, :, h * width:(h + 1) * width]


def delta_and_gate(nc, m, params, x_all, x_t, q_t, k_t, v_t, beta_t, fir_long, x1_all):
    banks, c = m.banks, m.c
    with ExitStack() as ctx:
        s = Memory(nc, ctx, "mixer_")
        w1_x, w1_s, w2_t, b1, wo, o_norm, taps = params.w1_x, params.w1_s, params.w2_t, params.b1, params.wo, params.o_norm, params.taps
        b2, copy_bias, log_temp, loaded = params.b2, params.copy_bias, params.log_temp, params.loaded
        norm = LayerNorm(s, "norm", GT)
        logit_bias, inv_temp = s.sb("logit_bias", [P, H0, NBR]), s.sb("inv_temp", [P, H0])
        sq_q, sq_k, norm_rows = s.sb("sq_q", [P, GTOK]), s.sb("sq_k", [P, GTOK]), s.sb("norm_rows", [P, P])
        unit = s.sb("unit", [P, 3, GTOK])
        vb_n, k_tok, w_t = s.sb("vb_n", [P, GTOK]), s.sb("k_tok", [P, GTOK]), s.sb("w_t", [P, GTOK])
        below = s.sb("below", [P, GTOK])
        attn = s.sb("attn", [P, GTOK])
        bd_pow = [s.sb(f"bd_pow{n}", [P, GCH, P]) for n in range(2)]
        solve = s.sb("solve", [P, GCH, 3 * DK])
        state = s.sb("state", [P, SCH, GB, DK])
        od_t = s.sb("od_t", [P, GTOK])
        pick_wide = s.sb("pick_wide", [P, GT * 2 * H0, DK])
        v_s = s.sb("v_s", [P, GB, FIRS - 1 + SEQ])
        v_tap = s.sb("v_tap", [P, GB, SEQ])
        short = [s.sb(f"short{n}", [P, GB, SEQ]) for n in range(2)]
        branch, branch_sq = s.sb("branch", [P, NBR, GTOK]), s.sb("branch_sq", [P, NBR, GTOK])
        sums = s.sb("sums", [P, 6, NBR * GT * H0])
        stats = s.sb("stats", [P, GT, H0, 8, NSTAT])
        stats_t = s.sb("stats_t", [P, GTOK])
        logits_t = s.sb("logits_t", [P, GTOK])
        hidden = s.sb("hidden", [P, H0, GTOK])
        gate = [s.sb(f"gate{n}", [P, GT * H0, NBR]) for n in range(2)]
        small = s.sb("small", [P, 8, GT * H0])
        mixed, mixed_t = s.sb("mixed", [P, GTOK]), s.sb("mixed_t", [P, GTOK])
        x_res = s.sb("x_res", [P, GT, P])
        dve_done = s.sem("dve_done")
        with nc.Block() as block:
            @block.gpsimd
            def _(pool):
                for t in bd_pow:
                    nc.gpsimd.memset(t[:, :, :], 0.0)
                nc.gpsimd.memset(stats[:, :, :, :, :], 0.0)

            @block.scalar
            def _(act):
                act.wait_ge(loaded, 16 * params.loads)
                nc.scalar.activation(inv_temp[:, :], log_temp[:, :], ACT.Exp, scale=-1.0)

            @block.vector
            def _(dve):
                dve.wait_ge(loaded, 16 * params.loads)
                ch = Chain(dve, dve_done)
                nc.vector.tensor_copy(pick_wide[:, :, :], c("pick_rows").unsqueeze(2).broadcast_to([P, GT * 2 * H0, DK]))
                ch.link(nc.vector.tensor_copy(logit_bias[:, :, :], b2[:, :].unsqueeze(1).broadcast_to([P, H0, NBR])))
                nc.vector.scalar_tensor_tensor(logit_bias[:, :, 3], copy_bias[:, :], DECAY, logit_bias[:, :, 3], ALU.mult, ALU.add)
                nc.vector.tensor_scalar(wo[:, :], wo[:, :], o_norm[:, 0:1], None, ALU.mult)
        s.clear()

        chunk = lambda t, h, n: t[32 * h:32 * h + 32, n * CHUNK:(n + 1) * CHUNK]
        by_head = lambda t, b: t[:, b, :].rearrange("p (th d) -> p th d", d=DK)
        sum_of = lambda n, b: sums[:, n, b * GT * H0:(b + 1) * GT * H0]

        class Solve:
            LEVELS = 5

            def __init__(self, g):
                self.g = g
                self.squared, self.summed, self.rooted, self.inverted, self.spread = (s.sem(n) for n in ("squared", "summed", "rooted", "inverted", "spread"))
                self.v_copied, self.tapped, self.keyed, self.d_done = (s.sem(n) for n in ("v_copied", "tapped", "keyed", "d_done"))
                self.produced, self.masked, self.placed = (s.sem(n) for n in ("produced", "masked", "placed"))
                self.kept, self.applied, self.powered, self.added = ([s.sem(f"{n}{b}") for b in range(GB)] for n in ("kept", "applied", "powered", "added"))

            def level_out(self, b):
                return m.psum[:, 2 + 2 * b:4 + 2 * b, :].rearrange("p k (n c) -> p (k n) c", c=P)

            def filter_short(self, pool):
                nc.gpsimd.tensor_copy(v_s[:, :, :], v_t[:, bass.ds(self.g * GB, GB), FIRL - (FIRS - 1):]).then_inc(self.v_copied, 1)
                pool.wait_ge(self.v_copied, 1)
                nc.gpsimd.tensor_scalar(short[0][:, :, :], v_s[:, :, 0:SEQ], taps[:, 0:1], None, ALU.mult)
                for j in range(1, FIRS):
                    nc.gpsimd.tensor_scalar(v_tap[:, :, :], v_s[:, :, j:j + SEQ], taps[:, j:j + 1], None, ALU.mult).then_inc(self.tapped, 1)
                    pool.wait_ge(self.tapped, 2 * j - 1)
                    nc.gpsimd.tensor_tensor(short[j % 2][:, :, :], short[(j - 1) % 2][:, :, :], v_tap[:, :, :], ALU.add).then_inc(self.tapped, 1)
                    pool.wait_ge(self.tapped, 2 * j)

            def sum_squares(self, pe):
                pe.wait_ge(self.squared, 2)
                for t in range(GT):
                    for n, sq in enumerate((sq_q, sq_k)):
                        last = nc.tensor.matmul(banks[0][32 * t:32 * t + 32, 0:P], c("sum_rows")[:, 32 * n:32 * n + 32], sq[:, t * P:(t + 1) * P],
                                                start=(n == 0), stop=(n == 1))
                last.then_inc(self.summed, 1)

            def spread_norms(self, pe):
                pe.wait_ge(self.inverted, 1)
                for n in range(2):
                    for t in range(GT):
                        at = (t * 2 + 1 - n) * H0
                        last = nc.tensor.matmul(banks[6 + n][:, t * P:(t + 1) * P], pick_wide[:, at:at + H0, :],
                                                norm_rows[:, :], start=True, stop=True)
                    last.then_inc(self.spread, 1)

            def products(self, pe):
                pe.wait_ge(self.d_done, 3)
                for b in range(GB):
                    for n in range(SCH):
                        for h in range(H0):
                            last = nc.tensor.matmul(banks[b][32 * h:32 * h + 32, n * 2 * CHUNK:(n + 1) * 2 * CHUNK], chunk(unit[:, 2, :], h, b * SCH + n),
                                                    unit[32 * h:32 * h + 32, 0:2, (b * SCH + n) * CHUNK:(b * SCH + n + 1) * CHUNK], start=True, stop=True)
                    last.then_inc(self.produced, 1)
                pe.wait_ge(self.keyed, 1)

            def apply(self, pe, lv, sequences=range(GB)):
                for b in sequences:
                    pe.wait_ge(self.kept[b], lv + 1)
                    if lv:
                        pe.wait_ge(self.powered[b], min(lv, 4))
                        pe.wait_ge(self.added[b], lv)
                    else:
                        pe.wait_ge(self.placed, b + 1)
                    for n in range(SCH):
                        last = nc.tensor.matmul(self.level_out(b)[:, n, 0:3 * DK], bd_pow[lv % 2][:, b * SCH + n, :],
                                                solve[:, b * SCH + n, :], start=True, stop=True)
                    last.then_inc(self.applied[b], 1)

            def root(self, act):
                act.wait_ge(self.summed, 1)
                nc.scalar.activation(norm_rows[:, :], banks[0][:, 0:P], ACT.Sqrt, bias=c("eps6")).then_inc(self.rooted, 1)

            def place(self, act):
                for b in range(GB):
                    act.wait_ge(self.masked, b + 1)
                    for h in range(2):
                        last = nc.scalar.copy(head_block(bd_pow[0][:, b * SCH:(b + 1) * SCH, :], h),
                                              below[32 * h:32 * h + 32, b * SEQ:(b + 1) * SEQ].rearrange("p (n t) -> p n t", n=SCH))
                    last.then_inc(self.placed, 1)

            def power(self, act, lv, sequences=range(GB)):
                for b in sequences:
                    act.wait_ge(self.applied[b], lv + 1)
                    nc.scalar.copy(solve[:, b * SCH:(b + 1) * SCH, 0:DK], self.level_out(b)[:, :, 0:DK]).then_inc(self.powered[b], 1)

            def square(self, dve):
                for sq, t in ((sq_q, q_t), (sq_k, k_t)):
                    nc.vector.tensor_tensor(sq[:, :].unsqueeze(1), t[:, bass.ds(self.g, 1), :], t[:, bass.ds(self.g, 1), :], ALU.mult).then_inc(self.squared, 1)

            def invert(self, dve):
                dve.wait_ge(self.rooted, 1)
                nc.vector.reciprocal(norm_rows[:, :], norm_rows[:, :]).then_inc(self.inverted, 1)

            def scale(self, dve):
                g, ch = self.g, Chain(dve, self.d_done)
                dve.wait_ge(self.spread, 1)
                ch.link(nc.vector.tensor_tensor(unit[:, 2:3, :], banks[6][:, :].unsqueeze(1), k_t[:, bass.ds(g, 1), :], ALU.mult))
                ch.link(nc.vector.tensor_tensor(unit[:, 0:1, :], unit[:, 2:3, :], beta_t[:, bass.ds(g, 1), :], ALU.mult))
                dve.wait_ge(self.spread, 2)
                ch.link(nc.vector.tensor_tensor(unit[:, 1:2, :], banks[7][:, :].unsqueeze(1), q_t[:, bass.ds(g, 1), :], ALU.mult))
                ch.link(nc.vector.tensor_tensor(vb_n[:, :].rearrange("p (b t) -> p b t", b=GB), v_t[:, bass.ds(g * GB, GB), FIRL:],
                                                beta_t[:, bass.ds(g, 1), :].rearrange("p o (b t) -> p (o b) t", b=GB), ALU.mult))
                nc.vector.transpose(solve[:, :, DK:2 * DK], vb_n[:, :])
                nc.vector.transpose(solve[:, :, 2 * DK:], unit[:, 0, :])
                nc.vector.transpose(k_tok[:, :], unit[:, 2, :]).then_inc(self.keyed, 1)

            def mask(self, dve):
                for b in range(GB):
                    cols = slice(b * SEQ, (b + 1) * SEQ)
                    products = banks[b][:, :].rearrange("p (n k t) -> p n k t", n=SCH, k=2)
                    mask = lambda name: c(name).unsqueeze(1).broadcast_to([P, SCH, CHUNK])
                    by_chunk = lambda t: t[:, cols].rearrange("p (n t) -> p n t", n=SCH)
                    dve.wait_ge(self.produced, b + 1)
                    nc.vector.tensor_tensor(by_chunk(below), products[:, :, 0, :], mask("minus_upper"), ALU.mult).then_inc(self.masked, 1)
                    dve.wait_ge(self.masked, b + 1)
                    for h in (2, 3):
                        nc.vector.tensor_copy(head_block(bd_pow[0][:, b * SCH:(b + 1) * SCH, :], h),
                                              below[32 * h:32 * h + 32, cols].rearrange("p (n t) -> p n t", n=SCH))
                    nc.vector.transpose(solve[:, b * SCH:(b + 1) * SCH, 0:DK], below[:, cols]).then_inc(self.kept[b], 1)
                    nc.vector.tensor_tensor(by_chunk(attn), products[:, :, 1, :], mask("causal_t"), ALU.mult)

            def add(self, dve, lv):
                for b in range(GB):
                    dve.wait_ge(self.applied[b], lv + 1)
                    half = slice(b * SCH, (b + 1) * SCH)
                    if lv < self.LEVELS - 1:
                        dve.wait_ge(self.powered[b], lv + 1)
                        for h in range(H0):
                            last = nc.vector.transpose(head_block(bd_pow[(lv + 1) % 2][:, half, :], h), solve[32 * h:32 * h + 32, half, 0:DK])
                        last.then_inc(self.kept[b], 1)
                    if lv:
                        dve.wait_ge(self.added[b], lv)
                    nc.vector.tensor_tensor(solve[:, half, DK:], solve[:, half, DK:], self.level_out(b)[:, :, DK:3 * DK], ALU.add).then_inc(self.added[b], 1)

            def turn_keys(self, dve):
                for b in range(GB):
                    dve.wait_ge(self.added[b], self.LEVELS)
                nc.vector.transpose(w_t[:, :], solve[:, :, 2 * DK:])

        class Gate:
            UP = (6, 7, 0, 1)

            def __init__(self, g):
                self.g = g
                (self.means, self.norms, self.listed, self.listed_t, self.turned, self.od_evac, self.od_square, self.stats_kept, self.raised, self.bent,
                 self.scored, self.logits_kept, self.by_token, self.centred, self.exped, self.mean_sq, self.rms, self.mixed_up, self.mixed_turned,
                 self.mixed_kept, self.projected, self.var_ready, self.sd_ready, self.g_done) = (s.sem("gate_" + n) for n in (
                    "means", "norms", "listed", "listed_t", "turned", "od_evac", "od_square", "stats_kept", "raised", "bent",
                    "scored", "logits_kept", "by_token", "centred", "exped", "mean_sq", "rms", "mixed_up", "mixed_turned",
                    "mixed_kept", "projected", "var_ready", "sd_ready", "g_done"))

            def turn_outputs(self, pe):
                for t in range(GT):
                    last = nc.tensor.transpose(banks[5][:, t * P:(t + 1) * P], od_t[:, t * P:(t + 1) * P], c("ident"))
                last.then_inc(self.turned, 1)

            def turn_stats(self, pe):
                pe.wait_ge(self.listed, 1)
                for t in range(GT):
                    last = nc.tensor.transpose(banks[4][:, t * P:(t + 1) * P], stats[:, t, :, :, :].rearrange("p h b s -> p (h b s)"), c("ident"))
                last.then_inc(self.listed_t, 1)
                pe.wait_ge(self.stats_kept, 1)

            def raise_head(self, pe, h):
                up = banks[self.UP[h]]
                nc.tensor.matmul(up[:, :], w1_x[:, :], x_t[:, bass.ds(self.g * GB, GB), CONV - 1:], start=True, stop=False)
                nc.tensor.matmul(up[:, :], w1_s[:, h, :], stats_t[:, :], start=False, stop=True).then_inc(self.raised, 1)

            def score(self, pe):
                for h in range(H0):
                    pe.wait_ge(self.bent, h + 1)
                    last = nc.tensor.matmul(banks[6][32 * h:32 * h + 32, :], w2_t[:, :], hidden[:, h, :], start=True, stop=True)
                last.then_inc(self.scored, 1)

            def turn_logits(self, pe):
                pe.wait_ge(self.logits_kept, 1)
                for t in range(GT):
                    last = nc.tensor.transpose(banks[7][:, t * P:(t + 1) * P], logits_t[:, t * P:(t + 1) * P], c("ident"))
                last.then_inc(self.by_token, 1)

            def project(self, pe):
                pe.wait_ge(self.mixed_up, 1)
                for t in range(GT):
                    last = nc.tensor.transpose(banks[0][:, t * P:(t + 1) * P], mixed[:, t * P:(t + 1) * P], c("ident"))
                last.then_inc(self.mixed_turned, 1)
                pe.wait_ge(self.mixed_kept, 1)
                for t in range(GT):
                    last = nc.tensor.matmul(banks[1][:, t * P:(t + 1) * P], mixed_t[:, t * P:(t + 1) * P], wo[:, :], start=True, stop=True)
                last.then_inc(self.projected, 1)

            def keep_outputs(self, act):
                act.wait_ge(self.turned, 1)
                nc.scalar.activation(branch_sq[:, 2, :], banks[5][:, :], ACT.Square).then_inc(self.od_square, 1)
                nc.scalar.copy(branch[:, 2, :], banks[5][:, :]).then_inc(self.od_evac, 1)

            def root_norms(self, act):
                act.wait_ge(self.means, 1)
                nc.scalar.activation(sums[:, 4, :], sums[:, 1, :], ACT.Sqrt).then_inc(self.norms, 1)

            def keep_stats(self, act):
                act.wait_ge(self.listed_t, 1)
                nc.scalar.copy(stats_t[:, :], banks[4][:, :]).then_inc(self.stats_kept, 1)

            def bend(self, act, h):
                act.wait_ge(self.raised, h + 1)
                nc.scalar.activation(hidden[:, h, :], banks[self.UP[h]][:, :], ACT.Gelu_apprx_tanh, bias=b1[:, 0:1]).then_inc(self.bent, 1)

            def keep_logits(self, act):
                act.wait_ge(self.scored, 1)
                nc.scalar.copy(logits_t[:, :], banks[6][:, :]).then_inc(self.logits_kept, 1)

            def exps(self, act):
                act.wait_ge(self.centred, 1)
                nc.scalar.activation(gate[1][:, :, :], gate[0][:, :, :], ACT.Exp).then_inc(self.exped, 1)

            def root_mixed(self, act):
                act.wait_ge(self.mean_sq, 1)
                nc.scalar.activation(small[:, 4, :], small[:, 2, :], ACT.Sqrt, bias=c("eps5"), scale=1.0 / DK).then_inc(self.rms, 1)

            def keep_mixed(self, act):
                act.wait_ge(self.mixed_turned, 1)
                nc.scalar.copy(mixed_t[:, :], banks[0][:, :]).then_inc(self.mixed_kept, 1)

            def root_norm(self, act):
                act.wait_ge(self.var_ready, 1)
                norm.root(nc, m).then_inc(self.sd_ready, 1)

            def reduce_outputs(self, dve):
                dve.wait_ge(self.od_square, 1)
                nc.vector.tensor_reduce(sum_of(1, 2), by_head(branch_sq, 2), X, ALU.add).then_inc(self.means, 1)
                dve.wait_ge(self.od_evac, 1)
                self.ch = Chain(dve, self.g_done)
                nc.vector.tensor_reduce(sum_of(0, 2), by_head(branch, 2), X, ALU.add)
                self.ch.link(nc.vector.tensor_reduce(sum_of(2, 2), by_head(branch, 2), X, ALU.add, apply_absolute_value=True))

            def list_stats(self, dve):
                ch = self.ch
                slot = lambda n: stats[:, :, :, 0:NBR, n].rearrange("p t h b -> p b (t h)")
                row = lambda n: sums[:, n, :].rearrange("p (b th) -> p b th", b=NBR)
                nc.vector.tensor_scalar(slot(0), row(0), 1.0 / DK, None, ALU.mult)
                nc.vector.tensor_scalar(slot(2), row(2), 1.0 / DK, None, ALU.mult)
                ch.link(nc.vector.tensor_tensor(sums[:, 3, :], sums[:, 0, :], sums[:, 0, :], ALU.mult))
                dve.wait_ge(self.means, 1)
                ch.link(nc.vector.scalar_tensor_tensor(sums[:, 5, :], sums[:, 3, :], -1.0 / DK, sums[:, 1, :], ALU.mult, ALU.add))
                nc.vector.tensor_scalar(slot(1), row(5), 1.0 / DK, None, ALU.mult)
                dve.wait_ge(self.norms, 1)
                nc.vector.tensor_copy(slot(3), row(4)).then_inc(self.listed, 1)

            def centre(self, dve):
                ch = self.ch
                over = lambda n: small[:, n, :].unsqueeze(2).broadcast_to([P, GT * H0, NBR])
                per_head = lambda t: t.rearrange("p (t h) n -> p t h n", t=GT)
                dve.wait_ge(self.by_token, 1)
                ch.link(nc.vector.tensor_tensor(per_head(gate[0][:, :, :]), banks[7][:, :].rearrange("p (t h n) -> p t h n", t=GT, h=H0)[:, :, :, 0:NBR],
                                                logit_bias[:, :, :].unsqueeze(1).broadcast_to([P, GT, H0, NBR]), ALU.add))
                ch.link(nc.vector.tensor_tensor(per_head(gate[0][:, :, :]), per_head(gate[0][:, :, :]),
                                                inv_temp[:, :].unsqueeze(1).unsqueeze(3).broadcast_to([P, GT, H0, NBR]), ALU.mult))
                ch.link(nc.vector.tensor_reduce(small[:, 0, :], gate[0][:, :, :], X, ALU.max))
                nc.vector.tensor_tensor(gate[0][:, :, :], gate[0][:, :, :], over(0), ALU.subtract).then_inc(self.centred, 1)

            def mix(self, dve):
                ch = self.ch
                over = lambda n: small[:, n, :].unsqueeze(2).broadcast_to([P, GT * H0, NBR])
                dve.wait_ge(self.exped, 1)
                ch.link(nc.vector.tensor_reduce(small[:, 1, :], gate[1][:, :, :], X, ALU.add))
                ch.link(nc.vector.reciprocal(small[:, 1, :], small[:, 1, :]))
                ch.link(nc.vector.tensor_tensor(gate[0][:, :, :], gate[1][:, :, :], over(1), ALU.mult))
                ch.link(nc.vector.tensor_scalar(gate[0][:, :, :], gate[0][:, :, :], 1.0 - 4.0 * EPS_FLOOR, EPS_FLOOR, ALU.mult, ALU.add))
                ch.link(nc.vector.tensor_tensor(branch_sq[:, :, :].rearrange("p b (th d) -> p b th d", d=DK),
                                                branch[:, :, :].rearrange("p b (th d) -> p b th d", d=DK),
                                                gate[0][:, :, :].rearrange("p th b -> p b th").unsqueeze(3).broadcast_to([P, NBR, GT * H0, DK]), ALU.mult))

            def sum_mixed(self, dve):
                ch = self.ch
                ch.link(nc.vector.tensor_tensor(branch[:, 0:2, :], branch_sq[:, 0:2, :], branch_sq[:, 2:4, :], ALU.add))
                ch.link(nc.vector.tensor_tensor(mixed[:, :], branch[:, 0, :], branch[:, 1, :], ALU.add))
                ch.link(nc.vector.tensor_tensor(branch[:, 2, :], mixed[:, :], mixed[:, :], ALU.mult))
                nc.vector.tensor_reduce(small[:, 2, :], branch[:, 2, :].rearrange("p (th d) -> p th d", d=DK), X, ALU.add).then_inc(self.mean_sq, 1)

            def scale_mixed(self, dve):
                dve.wait_ge(self.rms, 1)
                self.ch.link(nc.vector.reciprocal(small[:, 5, :], small[:, 4, :]))
                nc.vector.tensor_tensor(mixed[:, :].rearrange("p (th d) -> p th d", d=DK), mixed[:, :].rearrange("p (th d) -> p th d", d=DK),
                                        small[:, 5, :].unsqueeze(2).broadcast_to([P, GT * H0, DK]), ALU.mult).then_inc(self.mixed_up, 1)

            def norm_out(self, dve):
                dve.wait_ge(self.projected, 1)
                self.ch.link(nc.vector.tensor_tensor(x_res[:, :, :], x_all[:, bass.ds(self.g * GT, GT), :], banks[1][:, :].rearrange("p (t c) -> p t c", t=GT), ALU.add))
                norm.norm(nc, dve, self.ch, x_res[:, :, :], x1_all[:, bass.ds(self.g * GT, GT), :], self.var_ready, self.sd_ready, 1)

        def solve_and_gate(sv, gt):
            with nc.Block() as block:
                if sv:
                    @block.gpsimd
                    def _(pool):
                        sv.filter_short(pool)

                @block.tensor
                def _(pe):
                    if gt:
                        gt.turn_outputs(pe)
                    if sv:
                        sv.sum_squares(pe)
                        sv.spread_norms(pe)
                        sv.products(pe)
                    if gt:
                        gt.turn_stats(pe)
                    for h in range(H0):
                        if sv:
                            sv.apply(pe, h // GB, (h % GB,))
                        if gt:
                            gt.raise_head(pe, h)
                    if sv:
                        sv.apply(pe, 2)
                    if gt:
                        gt.score(pe)
                        gt.turn_logits(pe)
                    if sv:
                        sv.apply(pe, 3)
                        sv.apply(pe, 4)
                    if gt:
                        gt.project(pe)

                @block.scalar
                def _(act):
                    if gt:
                        gt.keep_outputs(act)
                    if sv:
                        sv.root(act)
                    if gt:
                        gt.root_norms(act)
                    if sv:
                        sv.place(act)
                    if gt:
                        gt.keep_stats(act)
                    for h in range(H0):
                        if sv:
                            sv.power(act, h // GB, (h % GB,))
                        if gt:
                            gt.bend(act, h)
                    if sv:
                        sv.power(act, 2)
                    if gt:
                        gt.keep_logits(act)
                    if gt:
                        gt.exps(act)
                    if sv:
                        sv.power(act, 3)
                    if gt:
                        gt.root_mixed(act)
                        gt.keep_mixed(act)
                        gt.root_norm(act)

                @block.vector
                def _(dve):
                    if sv:
                        sv.square(dve)
                    if gt:
                        gt.reduce_outputs(dve)
                    if sv:
                        sv.invert(dve)
                    if gt:
                        gt.list_stats(dve)
                    if sv:
                        sv.scale(dve)
                        sv.mask(dve)
                        sv.add(dve, 0)
                        sv.add(dve, 1)
                        sv.add(dve, 2)
                    if gt:
                        gt.centre(dve)
                        gt.mix(dve)
                    if sv:
                        sv.add(dve, 3)
                    if gt:
                        gt.sum_mixed(dve)
                        gt.scale_mixed(dve)
                    if sv:
                        sv.add(dve, 4)
                        sv.turn_keys(dve)
                    if gt:
                        gt.norm_out(dve)

        def scan(g):
            corrected, fixed, stepped, advanced, scanned = s.sem("corrected"), s.sem("fixed"), s.sem("stepped"), s.sem("advanced"), s.sem("scanned")
            filtered, fir_copied, evacuated, squares = s.sem("filtered"), s.sem("fir_copied"), s.sem("evacuated"), s.sem("squares")
            with nc.Block() as block:
                @block.tensor
                def _(pe):
                    def each(i):
                        return [(b, h, b * SCH + i) for b in range(GB) for h in range(H0)]

                    def outputs(i, sequence):
                        for b, h, n in each(i):
                            if b != sequence:
                                continue
                            hs = slice(32 * h, 32 * h + 32)
                            if i:
                                nc.tensor.matmul(chunk(banks[2], h, n), state[hs, i, b, :], chunk(unit[:, 1, :], h, n), start=True, stop=False)
                            last = nc.tensor.matmul(chunk(banks[2], h, n), solve[hs, n, DK:2 * DK], chunk(attn, h, n), start=(i == 0), stop=True)
                        return last

                    for i in range(SCH):
                        if i:
                            pe.wait_ge(advanced, i)
                            for b, h, n in each(i):
                                last = nc.tensor.matmul(chunk(banks[0], h, b), chunk(w_t, h, n), state[32 * h:32 * h + 32, i, b, :], start=True, stop=True)
                            last.then_inc(corrected, 1)
                            outputs(i - 1, 0)
                            pe.wait_ge(fixed, i)
                        if i < SCH - 1:
                            for b, h, n in each(i):
                                last = nc.tensor.matmul(chunk(banks[1], h, b), chunk(k_tok, h, n), solve[32 * h:32 * h + 32, n, DK:2 * DK], start=True, stop=True)
                            last.then_inc(stepped, 1)
                        if i:
                            outputs(i - 1, 1)
                        if i < GT:
                            at = slice((i % 2) * P, (i % 2 + 1) * P)
                            nc.tensor.transpose(banks[4][:, i * P:(i + 1) * P], short[(FIRS - 1) % 2][:, i // 2, at], c("ident"))
                            last = nc.tensor.transpose(banks[3][:, i * P:(i + 1) * P], v_s[:, i // 2, FIRS - 1 + at.start:FIRS - 1 + at.stop], c("ident"))
                            if i == GT - 1:
                                last.then_inc(filtered, 1)
                    outputs(SCH - 1, 0)
                    outputs(SCH - 1, 1).then_inc(scanned, 1)

                @block.gpsimd
                def _(pool):
                    nc.gpsimd.tensor_copy(branch[:, 1, :].rearrange("p (t c) -> p t c", t=GT), fir_long[:, bass.ds(g * GT, GT), :]).then_inc(fir_copied, 1)

                @block.scalar
                def _(act):
                    act.wait_ge(fir_copied, 1)
                    nc.scalar.activation(branch_sq[:, 1, :], branch[:, 1, :], ACT.Square).then_inc(squares, 1)
                    act.wait_ge(filtered, 1)
                    for n, br in enumerate((3, 0)):
                        nc.scalar.copy(branch[:, br, :], banks[3 + n][:, :]).then_inc(evacuated, 1)
                        nc.scalar.activation(branch_sq[:, br, :], banks[3 + n][:, :], ACT.Square).then_inc(squares, 1)
                    act.wait_ge(scanned, 1)
                    nc.scalar.copy(od_t[:, :], banks[2][:, :])

                @block.vector
                def _(dve):
                    def take_stats(k):
                        n, kind = divmod(k, 3)
                        br = (1, 3, 0)[n]
                        if kind == 0:
                            dve.wait_ge(*((fir_copied, 1) if n == 0 else (evacuated, n)))
                        if kind == 2:
                            dve.wait_ge(squares, n + 1)
                        nc.vector.tensor_reduce(sum_of((0, 2, 1)[kind], br), by_head(branch if kind < 2 else branch_sq, br), X, ALU.add,
                                                apply_absolute_value=(kind == 1))

                    for i in range(SCH):
                        values = solve[:, i::SCH, DK:2 * DK]
                        if i:
                            dve.wait_ge(corrected, i)
                            nc.vector.tensor_tensor(values, values, banks[0][:, 0:GB * DK].rearrange("p (b d) -> p b d", b=GB),
                                                    ALU.subtract).then_inc(fixed, 1)
                            if i >= 5:
                                take_stats(2 * i - 7)
                        if i < SCH - 1:
                            dve.wait_ge(stepped, i + 1)
                            new = banks[1][:, 0:GB * DK].rearrange("p (b d) -> p b d", b=GB)
                            if i:
                                dve.wait_ge(advanced, i)
                                nc.vector.tensor_tensor(state[:, i + 1, :, :], state[:, i, :, :], new, ALU.add).then_inc(advanced, 1)
                            else:
                                nc.vector.tensor_copy(state[:, 1, :, :], new).then_inc(advanced, 1)
                            if i in (1, 2, 3):
                                take_stats(i - 1)
                            if i in (5, 6):
                                take_stats(2 * i - 6)
                    take_stats(8)
            s.clear()

        solve_and_gate(Solve(0), None)
        scan(0)
        with nc.Fori(0, GROUPS - 1) as g:
            solve_and_gate(Solve(g + 1), Gate(g))
            scan(g + 1)
        solve_and_gate(None, Gate(GROUPS - 1))
        s.clear()
    params.memory.clear()


def head_norm(nc, dve, ch, x, scratch, out, var, sd, var_ready, sd_ready, turn):
    tiles, width = x.shape[1], x.shape[2]
    wide = lambda t: t.unsqueeze(2).broadcast_to([P, tiles, width])
    ch.link(nc.vector.tensor_reduce(var, x, X, ALU.add))
    ch.link(nc.vector.tensor_scalar(var, var, -1.0 / width, None, ALU.mult))
    ch.link(nc.vector.tensor_tensor(x, x, wide(var), ALU.add))
    ch.link(nc.vector.tensor_tensor(scratch, x, x, ALU.mult))
    ch.link(nc.vector.tensor_reduce(var, scratch, X, ALU.add))
    nc.vector.tensor_scalar(var, var, 1.0 / width, 1e-5, ALU.mult, ALU.add).then_inc(var_ready, 1)
    dve.wait_ge(sd_ready, turn)
    ch.link(nc.vector.reciprocal(sd, sd))
    ch.link(nc.vector.tensor_tensor(out, x, wide(sd), ALU.mult))


class LayerNorm:

    def __init__(self, s, name, tiles):
        self.stats, self.mean_var, self.sd = s.sb(name + "_stats", [P, tiles, 6]), s.sb(name + "_mean_var", [P, tiles, 2]), s.sb(name + "_sd", [P, tiles])

    def root(self, nc, m, at=slice(None)):
        return nc.scalar.activation(self.sd[:, at], self.mean_var[:, at, 1], ACT.Sqrt, bias=m.c("eps5"))

    def norm(self, nc, dve, ch, x, out, var_ready, sd_ready, turn, first=0):
        self.take_stats(nc, ch, x, var_ready, first)
        return self.finish(nc, dve, ch, x, out, sd_ready, turn, first)

    def take_stats(self, nc, ch, x, var_ready, first=0):
        tiles = range(x.shape[1])
        for t in tiles:
            last = nc.vector.bn_stats(self.stats[:, first + t, :], x[:, t, :])
        ch.link(last)
        for t in tiles:
            last = nc.vector.bn_aggr(self.mean_var[:, first + t, :], self.stats[:, first + t, :])
        last.then_inc(var_ready, 1)

    def finish(self, nc, dve, ch, x, out, sd_ready, turn, first=0):
        tiles = range(x.shape[1])
        dve.wait_ge(sd_ready, turn)
        sd = self.sd[:, first:first + len(tiles)]
        ch.link(nc.vector.reciprocal(sd, sd))
        for t in tiles:
            last = nc.vector.tensor_scalar(out[:, t, :], x[:, t, :], self.mean_var[:, first + t, 0:1], self.sd[:, first + t:first + t + 1],
                                           ALU.subtract, ALU.mult)
        return last


def layer0_attention(nc, m, params, weights, x1_all, res_all, h_all, pick_all):
    banks, c, psum = m.banks, m.c, m.psum
    QKV, QK, HEADS = (NQ + 2 * NKV) * HD0, (NQ + NKV) * HD0, NQ + NKV
    SC = 3 * P
    with ExitStack() as ctx:
        s = Memory(nc, ctx, "attn0_")
        w_qkv, wo, wg, wr, ln1, ln2, bg = params.w_qkv, params.wo, params.wg, params.wr, params.ln1, params.ln2, params.bg
        b_qkv, qk_w, bo, br, loaded = params.b_qkv, params.qk_w, params.bo, params.br, params.loaded
        bound = s.sb("bound", [P, 3])
        h, h_t, sq = s.sb("h", [P, GT, P]), s.sb("h_t", [P, GTOK]), s.sb("sq", [P, GT, P])
        qkv = s.sb("qkv", [P, GT, QKV])
        rot = [s.sb(f"rot{n}", [P, GT, QK]) for n in range(2)]
        small = s.sb("small", [P, 4, GT])
        head_ms = s.sb("head_ms", [P, GT, HEADS])
        q_pad, k_pad = s.sb("q_pad", [P, GT, REP, NKV, 32]), s.sb("k_pad", [P, GT, NKV, 32])
        q_t, k_t = s.sb("q_t", [P, REP, GTOK]), s.sb("k_t", [P, NKV, GTOK])
        v_one = s.sb("v_one", [P, GT, NKV, 32])
        out_t = s.sb("out_t", [P, GB, REP, SEQ])
        probs = s.sb("probs", [P, 3, 2, SC])
        inv = s.sb("inv", [P, GT, NQ])
        att, att_t, gate_t = s.sb("att", [P, GT, P]), s.sb("att_t", [P, GTOK]), s.sb("gate_t", [P, GTOK])
        x2 = s.sb("x2", [P, GT, P])
        logits, best = s.sb("logits", [P, GT, E]), s.sb("best", [P, GT])
        done0 = s.sem("done0")
        with nc.Block() as block:
            @block.gpsimd
            def _(pool):
                nc.gpsimd.memset(q_pad[:, :, :, :, :], 0.0)
                nc.gpsimd.memset(k_pad[:, :, :, :], 0.0)
                nc.gpsimd.memset(k_t[:, :, :], 0.0)
                nc.gpsimd.memset(v_one[:, :, :, HD0 + 1:], 0.0)
                nc.gpsimd.memset(v_one[:, :, :, HD0:HD0 + 1], 1.0)

            @block.vector
            def _(dve):
                ch = Chain(dve, done0)
                dve.wait_ge(loaded, 16 * params.loads)
                nc.vector.tensor_scalar(w_qkv[:, :], w_qkv[:, :], ln1[:, 0:1], None, ALU.mult)
                nc.vector.tensor_scalar(wr[:, :], wr[:, :], ln2[:, 0:1], None, ALU.mult)
                nc.vector.tensor_tensor(wg[:, :], wg[:, :], c("head_ones"), ALU.mult)
                nc.vector.tensor_reduce(bound[:, 0:1], qk_w[:, 0:NQ * HD0], X, ALU.max, apply_absolute_value=True)
                ch.link(nc.vector.tensor_reduce(bound[:, 1:2], qk_w[:, NQ * HD0:], X, ALU.max, apply_absolute_value=True))
                ch.link(nc.vector.tensor_tensor(bound[:, 2:3], bound[:, 0:1], bound[:, 1:2], ALU.mult))
                nc.vector.tensor_scalar(bound[:, 2:3], bound[:, 2:3], -float(HD0) ** 0.5, None, ALU.mult)
        s.clear()

        weights.fetch()
        x1 = lambda g: x1_all[:, bass.ds(g * GT, GT), :]
        wide = lambda t: t.unsqueeze(2).broadcast_to([P, GT, P])

        class Projection:

            def __init__(self, g):
                self.g = g
                self.squared, self.ms_ready, self.root_ready, self.turned, self.kept, self.projected, self.d_done = (s.sem(n) for n in (
                    "squared", "ms_ready", "root_ready", "turned", "kept", "projected", "d_done"))

            def square(self, act):
                nc.scalar.activation(sq[:, :, :], x1(self.g), ACT.Square).then_inc(self.squared, 1)

            def root(self, act):
                act.wait_ge(self.ms_ready, 1)
                nc.scalar.activation(small[:, 1, :], small[:, 0, :], ACT.Sqrt, bias=c("eps6"), scale=1.0 / D).then_inc(self.root_ready, 1)

            def keep(self, act):
                act.wait_ge(self.turned, 1)
                nc.scalar.copy(h_t[:, :], banks[4]).then_inc(self.kept, 1)

            def head_roots(self, act):
                act.wait_ge(self.ms_ready, 2)
                nc.scalar.activation(head_ms[:, :, :], head_ms[:, :, :], ACT.Sqrt, bias=c("eps6"), scale=1.0 / HD0).then_inc(self.root_ready, 1)

            def turn(self, pe):
                pe.wait_ge(self.d_done, 2)
                for t in range(GT):
                    last = nc.tensor.transpose(banks[4][:, t * P:(t + 1) * P], h[:, t, :], c("ident"))
                last.then_inc(self.turned, 1)

            def project(self, pe):
                pe.wait_ge(self.kept, 1)
                for t in range(GT):
                    last = nc.tensor.matmul(psum[:, 4 + t // 2, (t % 2) * 256:(t % 2) * 256 + QKV], h_t[:, t * P:(t + 1) * P], w_qkv[:, :],
                                            start=True, stop=True)
                last.then_inc(self.projected, 1)

            def norm(self, dve):
                self.ch = ch = Chain(dve, self.d_done)
                dve.wait_ge(self.squared, 1)
                nc.vector.tensor_reduce(small[:, 0, :], sq[:, :, :], X, ALU.add).then_inc(self.ms_ready, 1)
                dve.wait_ge(self.root_ready, 1)
                ch.link(nc.vector.reciprocal(small[:, 2, :], small[:, 1, :]))
                ch.link(nc.vector.tensor_tensor(h[:, :, :], x1(self.g), wide(small[:, 2, :]), ALU.mult))

            def rotate(self, dve):
                ch = self.ch
                dve.wait_ge(self.projected, 1)
                ch.link(nc.vector.tensor_tensor(qkv[:, :, :].rearrange("p (a b) n -> p a b n", b=2),
                                                psum[:, 4:6, :].rearrange("p a (b n) -> p a b n", b=2)[:, :, :, 0:QKV],
                                                b_qkv[:, :].unsqueeze(1).unsqueeze(1).broadcast_to([P, 2, 2, QKV]), ALU.add))
                half = HD0 // 2
                halves = lambda t: t.rearrange("p t (h d) -> p t h d", d=half)
                for b in range(GB):
                    for n, name in enumerate(("cos", "sin")):
                        table = c(name).rearrange("p (t d) -> p t d", d=half).unsqueeze(2).broadcast_to([P, 2, 2 * HEADS, half])
                        last = nc.vector.tensor_tensor(halves(rot[n][:, 2 * b:2 * b + 2, :]), halves(qkv[:, 2 * b:2 * b + 2, 0:QK]), table, ALU.mult)
                ch.link(last)
                lo = lambda t: halves(t)[:, :, 0::2, :]
                hi = lambda t: halves(t)[:, :, 1::2, :]
                nc.vector.tensor_tensor(lo(qkv[:, :, 0:QK]), lo(rot[0][:, :, :]), hi(rot[1][:, :, :]), ALU.subtract)
                ch.link(nc.vector.tensor_tensor(hi(qkv[:, :, 0:QK]), lo(rot[1][:, :, :]), hi(rot[0][:, :, :]), ALU.add))
                ch.link(nc.vector.tensor_tensor(rot[0][:, :, :], qkv[:, :, 0:QK], qkv[:, :, 0:QK], ALU.mult))
                nc.vector.tensor_reduce(head_ms[:, :, :], rot[0][:, :, :].rearrange("p t (h d) -> p t h d", d=HD0), X, ALU.add).then_inc(self.ms_ready, 1)

            def weigh_heads(self, dve):
                ch = self.ch
                dve.wait_ge(self.root_ready, 2)
                ch.link(nc.vector.reciprocal(head_ms[:, :, :], head_ms[:, :, :]))
                ch.link(nc.vector.tensor_tensor(rot[1][:, :, :].rearrange("p t (h d) -> p t h d", d=HD0),
                                                qkv[:, :, 0:QK].rearrange("p t (h d) -> p t h d", d=HD0),
                                                head_ms[:, :, :].unsqueeze(3).broadcast_to([P, GT, HEADS, HD0]), ALU.mult))
                for r in range(REP):
                    by_key = lambda t: t[..., 0:NQ * HD0].rearrange("p t (i r d) -> p t r i d", r=REP, d=HD0)[:, :, r, :, :]
                    nc.vector.tensor_tensor(q_pad[:, :, r, :, 0:HD0], by_key(rot[1][:, :, :]), by_key(qk_w[:, :].unsqueeze(1).broadcast_to([P, GT, QK])), ALU.mult)
                nc.vector.tensor_tensor(k_pad[:, :, :, 0:HD0], rot[1][:, :, NQ * HD0:].rearrange("p t (i d) -> p t i d", d=HD0),
                                        qk_w[:, NQ * HD0:].rearrange("p (i d) -> p i d", d=HD0).unsqueeze(1).broadcast_to([P, GT, NKV, HD0]), ALU.mult)

        class Turned:

            def __init__(self):
                self.q_turned, self.keys_left, self.queries_left = s.sem("q_turned"), s.sem("keys_left"), s.sem("queries_left")

            def turn(self, pe, u):
                if u == 3:
                    pe.wait_ge(self.keys_left, 1)
                if u == 4:
                    pe.wait_ge(self.queries_left, 1)
                for t in range(GT):
                    src = q_pad[:, t, u - 1, :, :] if u else k_pad[:, t, :, :]
                    last = nc.tensor.transpose(banks[5 + u % 3][:, t * P:(t + 1) * P], src.rearrange("p i d -> p (i d)"), c("ident"))
                last.then_inc(self.q_turned, 1)

            def keep_keys(self, dve):
                dve.wait_ge(self.q_turned, 1)
                for i in range(NKV):
                    last = nc.vector.tensor_copy(k_t[32 * i:32 * i + 32, i, :], banks[5][32 * i:32 * i + 32, :])
                last.then_inc(self.keys_left, 1)
                nc.vector.tensor_copy(v_one[:, :, :, 0:HD0], qkv[:, :, QK:].rearrange("p t (i d) -> p t i d", d=HD0))

            def keep_queries(self, act, u):
                act.wait_ge(self.q_turned, u + 1)
                nc.scalar.copy(q_t[:, u - 1, :], banks[5 + u % 3]).then_inc(self.queries_left, 1)

        def first_projection():
            pr = Projection(0)
            with nc.Block() as block:
                @block.scalar
                def _(act):
                    pr.square(act)
                    pr.root(act)
                    pr.keep(act)
                    pr.head_roots(act)

                @block.tensor
                def _(pe):
                    pr.turn(pe)
                    pr.project(pe)

                @block.vector
                def _(dve):
                    pr.norm(dve)
                    pr.rotate(dve)
                    pr.weigh_heads(dve)

            tu = Turned()
            with nc.Block() as block:
                @block.tensor
                def _(pe):
                    for u in range(REP + 1):
                        tu.turn(pe, u)

                @block.scalar
                def _(act):
                    for u in range(1, REP + 1):
                        tu.keep_queries(act, u)

                @block.vector
                def _(dve):
                    tu.keep_keys(dve)
            s.clear()

        def group(g, beside):
            scored, exped, masked, used, summed = s.sem("scored"), s.sem("exped"), s.sem("masked"), s.sem("used"), s.sem("summed")
            turns = [(b, r, i2) for b in range(GB) for r in range(REP) for i2 in range(2)]
            pr = Projection(g + 1) if beside else None
            with nc.Block() as block:
                @block.tensor
                def _(pe):
                    def score(n):
                        b, r, i2 = turns[n]
                        if n >= 2:
                            pe.wait_ge(exped, n - 1)
                        for a in range(2):
                            i = 2 * i2 + a
                            dst, k0, k1 = banks[2 * (n % 2) + a], b * SEQ, b * SEQ + P
                            nc.tensor.matmul(dst[:, 0:2 * P], k_t[:, i, k0:k0 + P], q_t[:, r, k0:k0 + SEQ], start=True, stop=True)
                            last = nc.tensor.matmul(dst[:, 2 * P:SC], k_t[:, i, k1:k1 + P], q_t[:, r, k1:k1 + P], start=True, stop=True)
                        last.then_inc(scored, 1)

                    def weigh(n):
                        b, r, i2 = turns[n]
                        pe.wait_ge(masked, n + 1)
                        if b and i2 == 0 and r % 2 == 0:
                            pe.wait_ge(summed, r // 2 + 1)
                        for a in range(2):
                            i = 2 * i2 + a
                            p, dst = probs[:, n % 3, a, :], banks[6 + r // 2][32 * i:32 * i + 32, (r % 2) * SEQ:(r % 2 + 1) * SEQ]
                            nc.tensor.matmul(dst, v_one[:, 2 * b, i, :], p[:, 0:2 * P], start=True, stop=False, skip_group_check=True)
                            last = nc.tensor.matmul(dst[:, P:], v_one[:, 2 * b + 1, i, :], p[:, 2 * P:SC], start=False, stop=True, skip_group_check=True)
                        last.then_inc(used, 1)

                    for n in range(len(turns)):
                        score(n)
                        if n >= 2:
                            weigh(n - 2)
                        if beside and n == 3:
                            pr.turn(pe)
                        if beside and n == 4:
                            pr.project(pe)
                    weigh(len(turns) - 2)
                    weigh(len(turns) - 1)

                @block.gpsimd
                def _(pool):
                    for n in range(len(turns)):
                        pool.wait_ge(exped, n + 1)
                        diagonal = probs[:, n % 3, :, :].rearrange("p a (k c) -> p a k c", c=P)[:, :, 0::2, :]
                        nc.gpsimd.tensor_tensor(diagonal, diagonal, c("upto").unsqueeze(1).unsqueeze(1).broadcast_to([P, 2, 2, P]), ALU.mult).then_inc(masked, 1)

                @block.scalar
                def _(act):
                    if beside:
                        pr.square(act)
                    for n in range(len(turns)):
                        act.wait_ge(scored, n + 1)
                        if n >= 3:
                            act.wait_ge(used, n - 2)
                        nc.scalar.activation(probs[:, n % 3, :, :], psum[:, 2 * (n % 2):2 * (n % 2) + 2, 0:SC], ACT.Exp,
                                             bias=bound[:, 2:3], scale=float(HD0) ** -0.5).then_inc(exped, 1)
                        if beside and n == 0:
                            pr.root(act)
                        if beside and n == 3:
                            pr.keep(act)
                        if beside and n == 10:
                            pr.head_roots(act)

                @block.vector
                def _(dve):
                    def keep_sums(b, k):
                        dve.wait_ge(used, len(turns) // GB * b + 4 * (k + 1))
                        nc.vector.tensor_copy(out_t[:, b, 2 * k:2 * k + 2, :], banks[6 + k].rearrange("p (r t) -> p r t", r=2)).then_inc(summed, 1)

                    if beside:
                        pr.norm(dve)
                    keep_sums(0, 0)
                    if beside:
                        pr.rotate(dve)
                    keep_sums(0, 1)
                    if beside:
                        pr.weigh_heads(dve)
                    keep_sums(1, 0)
                    keep_sums(1, 1)

            by_token, att_ready, inverted = s.sem("by_token"), s.sem("att_ready"), s.sem("inverted")
            att_turned, att_kept, gated, gate_up, multiplied, out_ready = (s.sem(n) for n in (
                "att_turned", "att_kept", "gated", "gate_up", "multiplied", "out_ready"))
            x2_sq, r_ready, r_root, h_turned, h_kept, routed, e_done = (s.sem(n) for n in (
                "x2_sq", "r_ready", "r_root", "h_turned", "h_kept", "routed", "e_done"))
            tu = Turned() if beside else None
            with nc.Block() as block:
                @block.tensor
                def _(pe):
                    for b in range(GB):
                        for r in range(REP):
                            for t in range(2):
                                at = ((r % 2) * 2 + t) * P
                                last = nc.tensor.transpose(banks[4 + 2 * b + r // 2][:, at:at + P], out_t[:, b, r, t * P:(t + 1) * P], c("ident"))
                        last.then_inc(by_token, 1)
                    for t in range(GT):
                        if t % 2 == 0:
                            pe.wait_ge(att_ready, t // 2 + 1)
                        last = nc.tensor.transpose(banks[0][:, t * P:(t + 1) * P], att[:, t, :], c("ident"))
                    last.then_inc(att_turned, 1)
                    if beside:
                        tu.turn(pe, 0)
                    pe.wait_ge(att_kept, 1)
                    nc.tensor.matmul(banks[1], wg[:, :], att_t[:, :], start=True, stop=True).then_inc(gated, 1)
                    if beside:
                        tu.turn(pe, 1)
                        tu.turn(pe, 2)
                    pe.wait_ge(multiplied, 1)
                    for t in range(GT):
                        last = nc.tensor.matmul(banks[2][:, t * P:(t + 1) * P], att_t[:, t * P:(t + 1) * P], wo[:, :], start=True, stop=True)
                    last.then_inc(out_ready, 1)
                    if beside:
                        tu.turn(pe, 3)
                        tu.turn(pe, 4)
                    pe.wait_ge(e_done, 3)
                    for t in range(GT):
                        last = nc.tensor.transpose(banks[3][:, t * P:(t + 1) * P], h[:, t, :], c("ident"))
                    last.then_inc(h_turned, 1)
                    pe.wait_ge(h_kept, 1)
                    for t in range(GT):
                        last = nc.tensor.matmul(banks[4][:, t * E:(t + 1) * E], h_t[:, t * P:(t + 1) * P], wr[:, :], start=True, stop=True)
                    last.then_inc(routed, 1)

                @block.scalar
                def _(act):
                    act.wait_ge(att_turned, 1)
                    nc.scalar.copy(att_t[:, :], banks[0]).then_inc(att_kept, 1)
                    act.wait_ge(gated, 1)
                    nc.scalar.activation(gate_t[:, :], banks[1], ACT.Sigmoid, bias=bg[:, 0:1]).then_inc(gate_up, 1)
                    if beside:
                        tu.keep_queries(act, 1)
                        tu.keep_queries(act, 2)
                    act.wait_ge(e_done, 2)
                    nc.scalar.activation(sq[:, :, :], x2[:, :, :], ACT.Square).then_inc(x2_sq, 1)
                    act.wait_ge(r_ready, 1)
                    nc.scalar.activation(small[:, 1, :], small[:, 0, :], ACT.Sqrt, bias=c("eps6"), scale=1.0 / D).then_inc(r_root, 1)
                    if beside:
                        tu.keep_queries(act, 3)
                    act.wait_ge(h_turned, 1)
                    nc.scalar.copy(h_t[:, :], banks[3]).then_inc(h_kept, 1)
                    if beside:
                        tu.keep_queries(act, 4)

                @block.gpsimd
                def _(pool):
                    pool.wait_ge(e_done, 2)
                    nc.gpsimd.tensor_tensor(res_all[:, bass.ds(g * GT, GT), :], x2[:, :, :], x1(g), ALU.add)

                @block.vector
                def _(dve):
                    ch = Chain(dve, e_done)
                    for b in range(GB):
                        dve.wait_ge(by_token, b + 1)
                        sums = psum[:, 4 + 2 * b:6 + 2 * b, :].rearrange("p k (r t i d) -> p t (k r) i d", r=2, t=2, i=NKV)
                        for t in range(2):
                            last = nc.vector.reciprocal(inv[:, 2 * b + t, :].rearrange("p (i r) -> p r i", r=REP).unsqueeze(3), sums[:, t, :, :, HD0:HD0 + 1])
                        last.then_inc(inverted, 1)
                        dve.wait_ge(inverted, b + 1)
                        for t in range(2):
                            last = nc.vector.tensor_tensor(att[:, 2 * b + t, :].rearrange("p (i r d) -> p r i d", r=REP, d=HD0), sums[:, t, :, :, 0:HD0],
                                                           inv[:, 2 * b + t, :].rearrange("p (i r) -> p r i", r=REP).unsqueeze(3).broadcast_to([P, REP, NKV, HD0]), ALU.mult)
                        last.then_inc(att_ready, 1)
                    if beside:
                        tu.keep_keys(dve)
                    dve.wait_ge(gate_up, 1)
                    nc.vector.tensor_tensor(att_t[:, :], att_t[:, :], gate_t[:, :], ALU.mult).then_inc(multiplied, 1)
                    dve.wait_ge(out_ready, 1)
                    ch.link(nc.vector.tensor_tensor(x2[:, :, :], banks[2].rearrange("p (t c) -> p t c", t=GT),
                                                    bo[:, :].unsqueeze(1).broadcast_to([P, GT, P]), ALU.add))
                    ch.link(nc.vector.tensor_tensor(x2[:, :, :], x2[:, :, :], x1(g), ALU.add))
                    dve.wait_ge(x2_sq, 1)
                    nc.vector.tensor_reduce(small[:, 0, :], sq[:, :, :], X, ALU.add).then_inc(r_ready, 1)
                    dve.wait_ge(r_root, 1)
                    nc.vector.reciprocal(small[:, 2, :], small[:, 1, :]).then_inc(r_ready, 1)
                    dve.wait_ge(r_ready, 2)
                    ch.link(nc.vector.tensor_tensor(h[:, :, :], x2[:, :, :], wide(small[:, 2, :]), ALU.mult))
                    nc.vector.tensor_copy(h_all[:, bass.ds(g * GT, GT), 0:P], h[:, :, :])
                    dve.wait_ge(routed, 1)
                    ch.link(nc.vector.tensor_tensor(logits[:, :, :], banks[4][:, 0:GT * E].rearrange("p (t e) -> p t e", t=GT),
                                                    br[:, :].unsqueeze(1).broadcast_to([P, GT, E]), ALU.add))
                    pick_first(nc, ch, m, logits, best, pick_all[:, bass.ds(g * GT, GT), :])
            s.clear()

        first_projection()
        with nc.Fori(0, GROUPS - 1) as g:
            group(g, True)
        group(GROUPS - 1, False)
    params.memory.clear()


def pick_first(nc, ch, m, logits, best, out):
    wide = best[:, :].unsqueeze(2).broadcast_to([P, GT, E])
    ch.link(nc.vector.tensor_reduce(best[:, :], logits[:, :, :], X, ALU.max))
    ch.link(nc.vector.tensor_tensor(logits[:, :, :], logits[:, :, :], wide, ALU.is_ge))
    ch.link(nc.vector.scalar_tensor_tensor(logits[:, :, :], logits[:, :, :], -float(E), m.c("experts").unsqueeze(1).broadcast_to([P, GT, E]),
                                           ALU.mult, ALU.add))
    ch.link(nc.vector.tensor_reduce(best[:, :], logits[:, :, :], X, ALU.min))
    ch.link(nc.vector.tensor_tensor(out, logits[:, :, :], wide, ALU.is_equal))


class ExpertWeights:

    def __init__(self, nc, io, m, ctx, layer):
        s = self.memory = Memory(nc, ctx, f"weights{layer}_")
        self.F1 = 512
        self.F2 = 256 if layer == 0 else 512
        self.w1, self.w2 = s.sb("w1", [P, E, self.F1]), s.sb("w2", [P, E, self.F2 // P, P])
        self.b1, self.b2 = s.sb("b1", [P, E * self.F1 // P]), s.sb("b2", [P, E])
        self.row_w = s.sb("row_w", [P, 1])
        self.loaded, self.filled, self.slots_emptied = s.sem("loaded"), s.sem("filled"), s.sem("slots_emptied")
        self.loads = 5 if layer == 0 else 4
        self.nc, self.io, self.layer, self.m = nc, io, layer, m

    def fetch(self):
        nc, io, layer, empty = self.nc, self.io, self.layer, self.m.empty
        filled = self.filled
        with nc.Block() as block:
            @block.vector
            def _(dve):
                if layer == 0:
                    nc.vector.memset(empty[:, :, 0:P], 0.0)
                    nc.vector.tensor_copy(empty[:, :, P], self.m.c("empty_ids")).then_inc(filled, 1)

            @block.sync
            def _(sp):
                sp.dma_start(self.b1[:, :], io[f"experts{layer}_b1"]).then_inc(self.loaded, 16)
                sp.dma_start(self.b2[:, :], io[f"experts{layer}_b2"]).then_inc(self.loaded, 16)
                sp.dma_start(self.w1[:, :, :], io[f"experts{layer}_W1"].rearrange("e d f -> d e f")).then_inc(self.loaded, 16)
                sp.dma_start(self.w2[:, :, :, :], io[f"experts{layer}_W2"].rearrange("e (c f) d -> f e c d", f=P)).then_inc(self.loaded, 16)
                if layer == 0:
                    sp.dma_start(self.row_w[:, :], io["ln2"]).then_inc(self.loaded, 16)
                if layer == 0:
                    sp.wait_ge(filled, 1)
                sp.dma_start(io[f"sorted{layer}"].rearrange("(t p) d -> p t d", p=P), empty[:, :, :]).then_inc(self.slots_emptied, 16)


def experts(nc, io, m, layer, weights, h_all, pick_all, norm, next_params=None):
    banks, c = m.banks, m.c
    F1, F2, w1, w2, b1, b2, row_w = weights.F1, weights.F2, weights.w1, weights.w2, weights.b1, weights.b2, weights.row_w
    CH = F2 // P
    slots_in, slots_out = io[f"sorted{layer}"], io[f"expert_out{layer}"]
    with ExitStack() as ctx:
        s = Memory(nc, ctx, f"moe{layer}_")
        b2_parts, b2_rows = s.sb("b2_parts", [P, 3, E], BF16), s.sb("b2_rows", [P, E * P], BF16)
        ones16 = s.sb("ones16", [P, P], BF16)
        PAD = 8
        counts = [s.sb(f"counts{n}", [P, PAD + TILES, E]) for n in range(2)]
        total = s.sb("total", [P, TILES, E])
        over = s.sb("over", [P, E, 16])
        ends = [s.sb(f"ends{n}", [P, PAD + E]) for n in range(2)]
        need, begin = s.sb("need", [P, E]), s.sb("begin", [P, E])
        base = s.sb("base", [P, TILES, E])
        slot_f, slot = s.sb("slot_f", [P, TILES]), s.sb("slot", [P, TILES], I32)
        past = s.sb("past", [P, SLOT_TILES, E])
        owner_f, owner = s.sb("owner_f", [P, SLOT_TILES]), s.sb("owner", [P, SLOT_TILES], I32)
        TURN = 4
        x_in = [s.sb(f"x_in{k}", [P, P + 1]) for k in range(TURN)]
        row = [s.sb(f"row{k}", [P, 1], I32) for k in range(TURN)]
        x_t = [s.sb(f"x_t{k}", [P, P]) for k in range(2)]
        w1_now = [s.sb(f"w1_now{k}", [P, F1]) for k in range(2)]
        side = [s.sb(f"side{k}", [P, 256]) for k in range(2)]
        hid = [s.sb(f"hid{k}", [P, F2]) for k in range(TURN)]
        y = [s.sb(f"y{k}", [P, P]) for k in range(TURN)]

        powers = s.sb("powers", [P, H1, 3 * P]) if next_params else None

        zeroed, counted, d_done, placed, scattered = (s.sem(n) for n in ("zeroed", "counted", "d_done", "placed", "scattered"))
        split, bias_out = s.sem("split"), s.sem("bias_out")
        with nc.Block() as block:
            @block.sync
            def _(sp):
                sp.wait_ge(split, 1)
                for n in range(3):
                    sp.dma_start(b2_rows[32 * n:32 * n + 1, :], b2_parts[:, n, :]).then_inc(bias_out, 16)
                sp.wait_ge(bias_out, 3 * 16)

            @block.tensor
            def _(pe):
                nc.tensor.matmul(banks[0][:, 0:TILES * E], c("before"), pick_all[:, :, :], start=True, stop=True).then_inc(counted, 1)
                nc.tensor.matmul(banks[1][:, 0:TILES * E], c("ones"), pick_all[:, :, :], start=True, stop=True).then_inc(counted, 1)

            @block.gpsimd
            def _(pool):
                for t in counts:
                    nc.gpsimd.memset(t[:, 0:PAD, :], 0.0)
                for t in ends:
                    nc.gpsimd.memset(t[:, 0:PAD], 0.0)
                nc.gpsimd.tensor_copy(h_all[:, :, P], c("token_ids")).then_inc(zeroed, 1)
                pool.wait_ge(zeroed, 1)
                pool.wait_ge(weights.slots_emptied, 16)
                pool.wait_ge(placed, 1)
                for t in range(TILES):
                    nc.gpsimd.indirect_dma_start(slots_in, bass.IndirectOffsetOnAxis(ap=slot[:, t:t + 1], axis=0), h_all[:, t, :], None).then_inc(scattered, 16)
                pool.wait_ge(scattered, 16 * TILES)

            @block.vector
            def _(dve):
                ch = Chain(dve, d_done)
                if next_params:
                    next_params.negate(nc, dve)
                dve.wait_ge(zeroed, 1)
                dve.wait_ge(counted, 2)
                tile_e = lambda t: t.rearrange("p (t e) -> p t e", e=E)
                nc.vector.tensor_copy(total[:, :, :], tile_e(banks[1][:, 0:TILES * E]))
                ch.link(nc.vector.tensor_copy(counts[0][:, PAD:, :], tile_e(banks[1][:, 0:TILES * E])))
                for n, step in enumerate((1, 2, 4, 8)):
                    a, b = counts[n % 2], counts[(n + 1) % 2]
                    ch.link(nc.vector.tensor_tensor(b[:, PAD:, :], a[:, PAD:, :], a[:, PAD - step:PAD - step + TILES, :], ALU.add))
                upto = counts[0][:, PAD:, :]
                ch.link(nc.vector.tensor_tensor(over[:, :, :], upto[:, TILES - 1, :].unsqueeze(2).broadcast_to([P, E, 16]),
                                                c("tile_starts").unsqueeze(1).broadcast_to([P, E, 16]), ALU.is_gt))
                ch.link(nc.vector.tensor_reduce(need[:, :], over[:, :, :], X, ALU.add))
                ch.link(nc.vector.tensor_copy(ends[0][:, PAD:], need[:, :]))
                for n, step in enumerate((1, 2, 4)):
                    a, b = ends[n % 2], ends[(n + 1) % 2]
                    ch.link(nc.vector.tensor_tensor(b[:, PAD:], a[:, PAD:], a[:, PAD - step:PAD - step + E], ALU.add))
                end = ends[1][:, PAD:]
                ch.link(nc.vector.tensor_tensor(begin[:, :], end, need[:, :], ALU.subtract))
                ch.link(nc.vector.tensor_tensor(base[:, :, :], upto, total[:, :, :], ALU.subtract))
                ch.link(nc.vector.scalar_tensor_tensor(base[:, :, :], begin[:, :].unsqueeze(1).broadcast_to([P, TILES, E]), float(P), base[:, :, :],
                                                       ALU.mult, ALU.add))
                ch.link(nc.vector.tensor_tensor(base[:, :, :], base[:, :, :], tile_e(banks[0][:, 0:TILES * E]), ALU.add))
                ch.link(nc.vector.tensor_tensor(base[:, :, :], base[:, :, :], pick_all[:, :, :], ALU.mult))
                ch.link(nc.vector.tensor_reduce(slot_f[:, :], base[:, :, :], X, ALU.add))
                nc.vector.tensor_copy(slot[:, :], slot_f[:, :]).then_inc(placed, 1)
                ch.link(nc.vector.tensor_tensor(past[:, :, :], c("slots").unsqueeze(2).broadcast_to([P, SLOT_TILES, E]),
                                                end.unsqueeze(1).broadcast_to([P, SLOT_TILES, E]), ALU.is_ge))
                ch.link(nc.vector.tensor_reduce(owner_f[:, :], past[:, :, :], X, ALU.add))
                ch.link(nc.vector.tensor_scalar(owner_f[:, :], owner_f[:, :], float(E - 1), None, ALU.min))
                nc.vector.tensor_copy(owner[:, :], owner_f[:, :])
                nc.vector.memset(ones16[:, :], 1.0)
                nc.vector.memset(b2_rows[:, :], 0.0)
                dve.wait_ge(weights.loaded, weights.loads * 16)
                if layer == 0:
                    nc.vector.tensor_scalar(w1[:, :, :], w1[:, :, :], row_w[:, 0:1], None, ALU.mult)
                for n in range(3):
                    ch.link(nc.vector.tensor_copy(b2_parts[:, n, :], b2[:, :]))
                    if n < 2:
                        ch.link(nc.vector.tensor_tensor(b2[:, :], b2[:, :], b2_parts[:, n, :], ALU.subtract))
                nc.vector.tensor_scalar(need[:, :], need[:, :], 1.0, None, ALU.mult).then_inc(split, 1)
                if next_params:
                    next_params.sum_powers(nc, m, dve, ch, powers)

            @block.scalar
            def _(act):
                if next_params:
                    next_params.raise_powers(nc, m, act, powers)
        s.clear()

        x_here, y_out = [s.sem(f"x_here{k}") for k in range(TURN)], [s.sem(f"y_out{k}") for k in range(TURN)]
        turned, x_kept, rows_kept, staged, raised, sided, bent, bent_too, lowered, y_kept = (s.sem(n) for n in (
            "turned", "x_kept", "rows_kept", "staged", "raised", "sided", "bent", "bent_too", "lowered", "y_kept"))
        def passed(eng, sem, j, back=0):
            if not (isinstance(j, int) and j - back < 0):
                eng.wait_ge(sem, j + (1 - back))

        class OwnerRegisters:

            def __init__(self, engine, before, behind):
                self.engine, self.before, self.behind = engine, before, behind

            def load(self, i):
                self.first = 0 if isinstance(i, int) and i == 0 else self.before
                last = 0 if isinstance(i, int) and i > 0 else self.behind
                _, self.found = nc.values_load_multi_w_load_instructions(owner[0:1, bass.ds(i * TURN - self.first, self.first + TURN + last)],
                                                                         engines=[self.engine], min_val=0, max_val=E - 1)

            def of(self, j, k, back=0):
                drained = TURN if isinstance(j, int) and j >= SLOT_TILES else 0
                return self.found[self.first + drained + k - back]

        def is_tile(j, back=0):
            return not isinstance(j, int) or 0 <= j - back < SLOT_TILES

        def steps(eng_fori, step, begin=lambda i: None):
            turns = SLOT_TILES // TURN
            begin(0)
            for k in range(TURN):
                step(k, 0, k)
            with eng_fori(1, turns - 1) as i:
                begin(i)
                for k in range(TURN):
                    step(i * TURN + k, i, k)
            begin(turns - 1)
            for j in range(SLOT_TILES - TURN, SLOT_TILES + 3):
                step(j, j // TURN, j % TURN)

        with nc.Block() as block:
            @block.gpsimd
            def _(pool):
                def step(j, i, k):
                    if is_tile(j, 3):
                        b = (k - 3) % TURN
                        passed(pool, rows_kept, j, 3)
                        passed(pool, y_kept, j, 3)
                        nc.gpsimd.indirect_dma_start(slots_out, bass.IndirectOffsetOnAxis(ap=row[b][:, 0:1], axis=0), y[b][:, :], None).then_inc(y_out[b], 16)
                    if is_tile(j):
                        pool.wait_ge(x_here[k], i * 16 + 16)
                        if i > 0:
                            pool.wait_ge(y_out[k], i * 16)
                        nc.gpsimd.tensor_copy(row[k][:, :], x_in[k][:, P:]).then_inc(rows_kept, 1)

                for j in range(SLOT_TILES + 3):
                    step(j, j // TURN, j % TURN)
                for k in range(TURN):
                    pool.wait_ge(y_out[k], 16 * SLOT_TILES // TURN)

            @block.sync
            def _(sp):
                def load(j, k):
                    sp.dma_start(x_in[k][:, :], slots_in[bass.ds(j * P, P), :]).then_inc(x_here[k], 16)

                def step(j, i, k):
                    if is_tile(j, 1) and is_tile(j, 1 - TURN):
                        passed(sp, turned, j, 1)
                        passed(sp, rows_kept, j, 1)
                        load(j + TURN - 1, (k - 1) % TURN)

                for k in range(TURN):
                    load(k, k)
                steps(nc.sync.Fori, step)

            @block.tensor
            def _(pe):
                def turn_tokens(j, i, k):
                    pe.wait_ge(x_here[k], i * 16 + 16)
                    passed(pe, x_kept, j, 2)
                    nc.tensor.transpose(banks[k % 2][:, 0:P], x_in[k][:, 0:P], c("ident")).then_inc(turned, 1)

                owners = OwnerRegisters(mybir.EngineType.PE, 2, 0)

                def step(j, i, k):
                    if is_tile(j, -1):
                        turn_tokens(j + 1, i + (k + 1) // TURN, (k + 1) % TURN)
                    if is_tile(j):
                        passed(pe, x_kept, j)
                        passed(pe, staged, j)
                        passed(pe, bent, j, 2)
                        if layer == 1:
                            passed(pe, bent_too, j, 2)
                        for n in range(F1 // P):
                            last = nc.tensor.matmul(banks[2 + 2 * (k % 2) + n // 2][:, (n % 2) * P:(n % 2 + 1) * P],
                                                    w1_now[k % 2][:, n * P:(n + 1) * P], x_t[k % 2][:, :], start=True, stop=True)
                        last.then_inc(raised, 1)
                    if is_tile(j, 2):
                        passed(pe, bent, j, 2)
                        if layer == 1:
                            passed(pe, bent_too, j, 2)
                        passed(pe, y_kept, j, 4)
                        down = banks[6 + k % 2][:, 0:P]
                        who = owners.of(j, k, 2)
                        for n in range(CH):
                            nc.tensor.matmul(down, hid[(k - 2) % TURN][:, n * P:(n + 1) * P],
                                             w2[:, :, :, :].rearrange("p e c d -> p (e c d)")[:, bass.ds(who * (CH * P) + n * P, P)], start=(n == 0), stop=False)
                        nc.tensor.matmul(down, ones16[:, :], b2_rows[:, bass.ds(who * P, P)], start=False, stop=True).then_inc(lowered, 1)

                turn_tokens(0, 0, 0)
                steps(nc.tensor.Fori, step, owners.load)

            @block.scalar
            def _(act):
                owners = OwnerRegisters(mybir.EngineType.Activation, 0, 1)

                def stage(j, k, who):
                    passed(act, raised, j, 2)
                    nc.scalar.copy(w1_now[k % 2][:, :], w1[:, :, :].rearrange("p e f -> p (e f)")[:, bass.ds(who * F1, F1)]).then_inc(staged, 1)

                def load(i):
                    owners.load(i)
                    if isinstance(i, int) and i == 0:
                        stage(0, 0, owners.of(0, 0))

                def step(j, i, k):
                    if is_tile(j, -1):
                        stage(j + 1, k + 1, owners.of(j, k, -1))
                    if is_tile(j):
                        passed(act, raised, j)
                        passed(act, *((bent, j, 2) if layer == 0 else (lowered, j, TURN)))
                        for n in (2, 3) if layer == 0 else (0, 1):
                            bias = b1[:, bass.ds(owners.of(j, k) * (F1 // P) + n, 1)]
                            src = banks[2 + 2 * (k % 2) + n // 2][:, (n % 2) * P:(n % 2 + 1) * P]
                            if layer == 0:
                                last = nc.scalar.activation(side[k % 2][:, (n - 2) * P:(n - 1) * P], src, ACT.Sigmoid, bias=bias)
                            else:
                                last = nc.scalar.activation(hid[k % TURN][:, n * P:(n + 1) * P], src, ACT.Relu, bias=bias)
                        last.then_inc(sided if layer == 0 else bent, 1)

                steps(nc.scalar.Fori, step, load)

            @block.vector
            def _(dve):
                owners = OwnerRegisters(mybir.EngineType.DVE, 0, 0)

                def keep_tokens(j, k):
                    passed(dve, turned, j)
                    passed(dve, raised, j, 2)
                    nc.vector.tensor_copy(x_t[k % 2][:, :], banks[k % 2][:, 0:P]).then_inc(x_kept, 1)

                def step(j, i, k):
                    if is_tile(j, -1):
                        keep_tokens(j + 1, k + 1)
                    if is_tile(j):
                        passed(dve, sided if layer == 0 else raised, j)
                        passed(dve, lowered, j, TURN)
                        for n in (0, 1) if layer == 0 else (2, 3):
                            bias = b1[:, bass.ds(owners.of(j, k) * (F1 // P) + n, 1)]
                            src, dst = banks[2 + 2 * (k % 2) + n // 2][:, (n % 2) * P:(n % 2 + 1) * P], hid[k % TURN][:, n * P:(n + 1) * P]
                            if layer == 0:
                                last = nc.vector.scalar_tensor_tensor(dst, src, bias, side[k % 2][:, n * P:(n + 1) * P], ALU.add, ALU.mult)
                            else:
                                last = nc.vector.tensor_scalar(dst, src, bias, 0.0, ALU.add, ALU.max)
                        last.then_inc(bent if layer == 0 else bent_too, 1)
                    if is_tile(j, 2):
                        passed(dve, lowered, j, 2)
                        passed(dve, rows_kept, j, 2)
                        nc.vector.tensor_copy(y[(k - 2) % TURN][:, :], banks[6 + k % 2][:, 0:P]).then_inc(y_kept, 1)

                keep_tokens(0, 0)
                steps(nc.vector.Fori, step, owners.load)
        norm_all(nc, m, s, slots_out, norm)
        s.clear()
    weights.memory.clear()


def layer1_attention(nc, m, params, weights, x_all, x4_all, h_all, pick_all, prob_all):
    banks, c, psum = m.banks, m.c, m.psum
    SETS = H1 // 4
    SC = 3 * P
    with ExitStack() as ctx:
        s = Memory(nc, ctx, "attn1_")
        w_in, w_v, wo, wr, gamma, beta = params.w_in, params.w_v, params.wo, params.wr, params.gamma, params.beta
        bo, br, ln_g, ln_b, loaded = params.bo, params.br, params.ln_g, params.ln_b, params.loaded
        w_q, w_k = s.sb("w_q", [P, SETS, 4, 32]), s.sb("w_k", [P, SETS, 4, 32])
        wo_g, beta_rep = s.sb("wo_g", [P, P]), s.sb("beta_rep", [P, P])
        decay = params.decay
        id16, neg16 = s.sb("id16", [P, P], BF16), s.sb("neg16", [P, P], BF16)
        x_in, x_t = s.sb("x_in", [P, GT, P]), s.sb("x_t", [P, GTOK])
        q_t, k_t = s.sb("q_t", [P, SETS, GTOK]), s.sb("k_t", [P, SETS, 4, GTOK])
        v_one = s.sb("v_one", [P, GT, H1, 32])
        sums_t = s.sb("sums_t", [P, GB, SETS, SEQ])
        scores = s.sb("scores", [P, 3, 2, SC])
        top, minus_top = s.sb("top", [P, 3, 2, 2]), s.sb("minus_top", [P, 3, 2, 2])
        probs_t = s.sb("probs_t", [P, 2, 2, SC])
        inv = s.sb("inv", [P, GT, H1])
        out, out_n, out_t, scratch = s.sb("out", [P, GT, P]), s.sb("out_n", [P, GT, P]), s.sb("out_t", [P, GTOK]), s.sb("scratch", [P, GT, P])
        x5_t = s.sb("x5_t", [P, GTOK])
        x4, z = s.sb("x4", [P, GT, P]), s.sb("z", [P, GT, P])
        var, sd = s.sb("var", [P, 1, GT * H1]), s.sb("sd", [P, 1, GT * H1])
        norm4, norm5 = LayerNorm(s, "norm4", GT), LayerNorm(s, "norm5", GT)
        logits, best = s.sb("logits", [P, GT, E]), s.sb("best", [P, GT])
        exps, total = s.sb("exps", [P, GT, E]), s.sb("total", [P, GT])
        biased, beta_up, zeroed = (s.sem(n) for n in ("biased", "beta_up", "zeroed"))
        with nc.Block() as block:
            @block.gpsimd
            def _(pool):
                nc.gpsimd.memset(v_one[:, :, :, HD1 + 1:], 0.0)
                nc.gpsimd.memset(v_one[:, :, :, HD1:HD1 + 1], 1.0)
                nc.gpsimd.memset(k_t[:, :, :, :], 0.0)
                nc.gpsimd.memset(w_q[:, :, :, :], 0.0)
                nc.gpsimd.memset(w_k[:, :, :, :], 0.0).then_inc(zeroed, 1)

            @block.tensor
            def _(pe):
                pe.wait_ge(beta_up, 1)
                nc.tensor.matmul(banks[0][:, 0:P], beta_rep[:, :], wo[:, :], start=True, stop=True).then_inc(biased, 1)

            @block.vector
            def _(dve):
                dve.wait_ge(loaded, 16 * params.loads)
                nc.vector.tensor_copy(beta_rep[:, :], beta[:, 0:1].broadcast_to([P, P])).then_inc(beta_up, 1)
                nc.vector.tensor_scalar(wo_g[:, :], wo[:, :], gamma[:, 0:1], None, ALU.mult)
                nc.vector.tensor_copy(id16[:, :], c("ident"))
                nc.vector.tensor_copy(neg16[:, :], c("neg_ts"))
                dve.wait_ge(zeroed, 1)
                for n, w in enumerate((w_q, w_k)):
                    nc.vector.tensor_copy(w[:, :, :, 0:HD1], w_in[:, n, :].rearrange("p (s i d) -> p s i d", s=SETS, d=HD1))
                dve.wait_ge(biased, 1)
                nc.vector.tensor_tensor(bo[:, :], bo[:, :], banks[0][:, 0:P], ALU.add)
        s.clear()
        weights.fetch()

        x_now = lambda g: x_all[:, bass.ds(g * GT, GT), :]

        class Projection:
            BANK = (5, 6, 7, 4, 5)

            def __init__(self, g):
                self.g = g
                self.copied, self.turned, self.kept, self.projected, self.keys_left = (s.sem(n) for n in (
                    "x_copied", "turned", "kept", "projected", "keys_left"))

            def copy_tokens(self, pool):
                nc.gpsimd.tensor_copy(x_in[:, :, :], x_now(self.g)).then_inc(self.copied, 1)

            def turn(self, pe):
                pe.wait_ge(self.copied, 1)
                for t in range(GT):
                    last = nc.tensor.transpose(banks[4][:, t * P:(t + 1) * P], x_in[:, t, :], c("ident"))
                last.then_inc(self.turned, 1)

            def keep(self, act):
                act.wait_ge(self.turned, 1)
                nc.scalar.copy(x_t[:, :], banks[4]).then_inc(self.kept, 1)

            def project(self, pe, units):
                pe.wait_ge(self.kept, 1)
                for u in units:
                    if u < 4:
                        w = (w_k, w_q)[u // SETS]
                        last = nc.tensor.matmul(banks[self.BANK[u]], w[:, u % SETS, :, :].rearrange("p i d -> p (i d)"), x_t[:, :], start=True, stop=True)
                    else:
                        pe.wait_ge(self.keys_left, 1)
                        for t in range(GT):
                            last = nc.tensor.matmul(banks[self.BANK[u]][:, t * P:(t + 1) * P], x_t[:, t * P:(t + 1) * P], w_v[:, :], start=True, stop=True)
                    last.then_inc(self.projected, 1)

            def keep_queries(self, act):
                for st in range(SETS):
                    act.wait_ge(self.projected, SETS + st + 1)
                    nc.scalar.copy(q_t[:, st, :], banks[self.BANK[SETS + st]])

            def keep_keys(self, eng, copy, st):
                eng.wait_ge(self.projected, st + 1)
                for i in range(4):
                    last = copy(k_t[32 * i:32 * i + 32, st, i, :], banks[self.BANK[st]][32 * i:32 * i + 32, :])
                if st == 0:
                    last.then_inc(self.keys_left, 1)

            def keep_values(self, dve):
                dve.wait_ge(self.projected, 2 * SETS + 1)
                nc.vector.tensor_copy(v_one[:, :, :, 0:HD1], banks[self.BANK[4]].rearrange("p (t h d) -> p t h d", t=GT, d=HD1))

        def first_projection():
            pr = Projection(0)
            with nc.Block() as block:
                @block.gpsimd
                def _(pool):
                    pr.copy_tokens(pool)

                @block.tensor
                def _(pe):
                    pr.turn(pe)
                    pr.project(pe, range(5))

                @block.scalar
                def _(act):
                    pr.keep(act)
                    pr.keep_keys(act, nc.scalar.copy, 1)
                    pr.keep_queries(act)

                @block.vector
                def _(dve):
                    pr.keep_keys(dve, nc.vector.tensor_copy, 0)
                    pr.keep_values(dve)
            s.clear()

        def group(g, beside):
            scored, scaled, topped, negated, exped, flipped, moved, weighed, c_done = (s.sem(n) for n in (
                "scored", "scaled", "topped", "negated", "exped", "flipped", "moved", "weighed", "c_done"))
            copied, by_token = s.sem("copied"), s.sem("by_token")
            turns = [(b, h) for b in range(GB) for h in range(0, H1, 2)]
            N = len(turns)
            with nc.Block() as block:
                @block.tensor
                def _(pe):
                    def score(n):
                        b, h0 = turns[n]
                        if n >= 2:
                            pe.wait_ge(scaled, n - 1)
                        for a in range(2):
                            st, i = divmod(h0 + a, 4)
                            dst = banks[2 * (n % 2) + a]
                            t0, t1 = b * SEQ, b * SEQ + P
                            nc.tensor.matmul(dst[:, 0:P], q_t[:, st, t0:t0 + P], k_t[:, st, i, t0:t0 + P], start=True, stop=False, skip_group_check=True)
                            nc.tensor.matmul(dst[:, P:SC], q_t[:, st, t1:t1 + P], k_t[:, st, i, t0:t0 + SEQ], start=False, stop=False, skip_group_check=True)
                            nc.tensor.matmul(dst[:, 0:P], id16[:, :], neg16[:, :], start=False, stop=False, skip_group_check=True)
                            last = nc.tensor.matmul(dst[:, 2 * P:SC], id16[:, :], neg16[:, :], start=False, stop=True, skip_group_check=True)
                        last.then_inc(scored, 1)

                    def flip(n):
                        pe.wait_ge(exped, n + 1)
                        if n:
                            pe.wait_ge(moved, n)
                        for a in range(2):
                            for q in range(3):
                                last = nc.tensor.transpose(banks[4 + a][:, q * P:(q + 1) * P], scores[:, n % 3, a, q * P:(q + 1) * P], c("ident"))
                        last.then_inc(flipped, 1)

                    def weigh(n):
                        b, h0 = turns[n]
                        pe.wait_ge(moved, n + 1)
                        for a in range(2):
                            (st, i), p = divmod(h0 + a, 4), probs_t[:, n % 2, a, :]
                            dst = banks[6 + b][32 * i:32 * i + 32, st * SEQ:(st + 1) * SEQ]
                            nc.tensor.matmul(dst, v_one[:, 2 * b, h0 + a, :], p[:, 0:2 * P], start=True, stop=False, skip_group_check=True)
                            last = nc.tensor.matmul(dst[:, P:], v_one[:, 2 * b + 1, h0 + a, :], p[:, 2 * P:SC], start=False, stop=True, skip_group_check=True)
                        last.then_inc(weighed, 1)

                    for n in range(N + 3):
                        if n < N:
                            score(n)
                        if 2 <= n < N + 2:
                            flip(n - 2)
                        if n >= 3:
                            weigh(n - 3)
                    for b in range(GB):
                        pe.wait_ge(copied, b + 1)
                        for t in range(2):
                            for st in range(SETS):
                                last = nc.tensor.transpose(banks[b][:, (t * SETS + st) * P:(t * SETS + st + 1) * P], sums_t[:, b, st, t * P:(t + 1) * P], c("ident"))
                        last.then_inc(by_token, 1)

                @block.scalar
                def _(act):
                    def exps(n):
                        act.wait_ge(negated, n + 1)
                        for a in range(2):
                            for q, at in enumerate((slice(0, P), slice(P, SC))):
                                part = scores[:, n % 3, a, at]
                                last = nc.scalar.activation(part, part, ACT.Exp, bias=minus_top[:, n % 3, q, a:a + 1])
                        last.then_inc(exped, 1)

                    def move(n):
                        act.wait_ge(flipped, n + 1)
                        if n >= 2:
                            act.wait_ge(weighed, n - 1)
                        nc.scalar.copy(probs_t[:, n % 2, :, :], psum[:, 4:6, 0:SC]).then_inc(moved, 1)

                    for n in range(N + 2):
                        if n >= 2:
                            move(n - 2)
                        if n < N:
                            exps(n)

                @block.vector
                def _(dve):
                    ch = Chain(dve, c_done)
                    for n in range(N):
                        dve.wait_ge(scored, n + 1)
                        if n >= 3:
                            dve.wait_ge(flipped, n - 2)
                        k = 2 * (n % 2)
                        nc.vector.tensor_tensor(scores[:, n % 3, :, :], psum[:, k:k + 2, 0:SC],
                                                decay[:, :].unsqueeze(1).broadcast_to([P, 2, SC]), ALU.mult).then_inc(scaled, 1)
                        dve.wait_ge(scaled, n + 1)
                        nc.vector.tensor_reduce(top[:, n % 3, 0, :], scores[:, n % 3, :, 0:P], X, ALU.max)
                        nc.vector.tensor_reduce(top[:, n % 3, 1, :], scores[:, n % 3, :, P:SC], X, ALU.max).then_inc(topped, 1)
                        dve.wait_ge(topped, n + 1)
                        nc.vector.tensor_scalar(minus_top[:, n % 3, :, :], top[:, n % 3, :, :], -1.0, None, ALU.mult).then_inc(negated, 1)
                    for b in range(GB):
                        dve.wait_ge(weighed, N // GB * (b + 1))
                        nc.vector.tensor_copy(sums_t[:, b, :, :], banks[6 + b].rearrange("p (k t) -> p k t", k=SETS)).then_inc(copied, 1)
                    for b in range(GB):
                        dve.wait_ge(by_token, b + 1)
                        o = banks[b].rearrange("p (t h d) -> p t h d", t=2, d=32)
                        ch.link(nc.vector.reciprocal(inv[:, 2 * b:2 * b + 2, :].unsqueeze(3), o[:, :, :, HD1:HD1 + 1]))
                        nc.vector.tensor_tensor(out[:, 2 * b:2 * b + 2, :].rearrange("p t (h d) -> p t h d", d=HD1), o[:, :, :, 0:HD1],
                                                inv[:, 2 * b:2 * b + 2, :].unsqueeze(3).broadcast_to([P, 2, H1, HD1]), ALU.mult)

            pr = Projection(g + 1) if beside else None
            var_ready, sd_ready, head_normed, out_turned, out_kept, out_ready = (s.sem(n) for n in (
                "var_ready", "sd_ready", "head_normed", "out_turned", "out_kept", "out_ready"))
            x4_up, z_up, x4_turned, x4_kept, routed, shifted, raised, f_done, p_done = (s.sem(n) for n in (
                "x4_up", "z_up", "x4_turned", "x4_kept", "routed", "shifted", "raised", "f_done", "p_done"))
            with nc.Block() as block:
                @block.tensor
                def _(pe):
                    if beside:
                        pr.turn(pe)
                        pr.project(pe, (0, 1))
                    pe.wait_ge(head_normed, 1)
                    for t in range(GT):
                        last = nc.tensor.transpose(banks[0][:, t * P:(t + 1) * P], out_n[:, t, :], c("ident"))
                    last.then_inc(out_turned, 1)
                    pe.wait_ge(out_kept, 1)
                    for t in range(GT):
                        last = nc.tensor.matmul(banks[1][:, t * P:(t + 1) * P], out_t[:, t * P:(t + 1) * P], wo_g[:, :], start=True, stop=True)
                    last.then_inc(out_ready, 1)
                    if beside:
                        pr.project(pe, (2, 3, 4))
                    pe.wait_ge(x4_up, 1)
                    for t in range(GT):
                        last = nc.tensor.transpose(banks[2][:, t * P:(t + 1) * P], x4[:, t, :], c("ident"))
                    last.then_inc(x4_turned, 1)
                    pe.wait_ge(x4_kept, 1)
                    for t in range(GT):
                        last = nc.tensor.matmul(banks[3][:, t * E:(t + 1) * E], x5_t[:, t * P:(t + 1) * P], wr[:, :], start=True, stop=True)
                    last.then_inc(routed, 1)

                @block.scalar
                def _(act):
                    if beside:
                        pr.keep(act)
                    act.wait_ge(var_ready, 1)
                    nc.scalar.activation(sd[:, 0, :], var[:, 0, :], ACT.Sqrt).then_inc(sd_ready, 1)
                    act.wait_ge(out_turned, 1)
                    nc.scalar.copy(out_t[:, :], banks[0]).then_inc(out_kept, 1)
                    if beside:
                        pr.keep_keys(act, nc.scalar.copy, 1)
                        pr.keep_queries(act)
                    act.wait_ge(var_ready, 2)
                    norm4.root(nc, m).then_inc(sd_ready, 1)
                    act.wait_ge(var_ready, 3)
                    norm5.root(nc, m).then_inc(sd_ready, 1)
                    act.wait_ge(x4_turned, 1)
                    nc.scalar.copy(x5_t[:, :], banks[2]).then_inc(x4_kept, 1)
                    act.wait_ge(shifted, 1)
                    nc.scalar.activation(exps[:, :, :], exps[:, :, :], ACT.Exp).then_inc(raised, 1)

                @block.gpsimd
                def _(pool):
                    if beside:
                        pr.copy_tokens(pool)
                    pool.wait_ge(x4_up, 1)
                    nc.gpsimd.tensor_copy(x4_all[:, bass.ds(g * GT, GT), :], x4[:, :, :])
                    pool.wait_ge(z_up, 1)
                    row = lambda t: t[:, :].unsqueeze(1).broadcast_to([P, GT, P])
                    nc.gpsimd.tensor_tensor(scratch[:, :, :], z[:, :, :], row(ln_g), ALU.mult).then_inc(p_done, 1)
                    pool.wait_ge(p_done, 1)
                    nc.gpsimd.tensor_tensor(h_all[:, bass.ds(g * GT, GT), 0:P], scratch[:, :, :], row(ln_b), ALU.add)

                @block.vector
                def _(dve):
                    ch = Chain(dve, f_done)
                    by_head = lambda t: t[:, :, :].rearrange("p t (h d) -> p (t h) d", d=HD1)
                    head_norm(nc, dve, ch, by_head(out), by_head(scratch), by_head(out_n), var[:, 0, :], sd[:, 0, :], var_ready, sd_ready, 1)
                    nc.vector.tensor_copy(total[:, :], sd[:, 0, 0:GT]).then_inc(head_normed, 1)
                    if beside:
                        pr.keep_keys(dve, nc.vector.tensor_copy, 0)
                    dve.wait_ge(out_ready, 1)
                    ch.link(nc.vector.tensor_tensor(x4[:, :, :], banks[1].rearrange("p (t c) -> p t c", t=GT), bo[:, :].unsqueeze(1).broadcast_to([P, GT, P]), ALU.add))
                    ch.link(nc.vector.tensor_tensor(z[:, :, :], x4[:, :, :], x_now(g), ALU.add))
                    norm4.norm(nc, dve, ch, z[:, :, :], x4[:, :, :], var_ready, sd_ready, 2).then_inc(x4_up, 1)
                    dve.wait_ge(x4_up, 1)
                    norm5.norm(nc, dve, ch, x4[:, :, :], z[:, :, :], var_ready, sd_ready, 3).then_inc(z_up, 1)
                    dve.wait_ge(routed, 1)
                    ch.link(nc.vector.tensor_tensor(logits[:, :, :], banks[3][:, 0:GT * E].rearrange("p (t e) -> p t e", t=GT),
                                                    br[:, :].unsqueeze(1).broadcast_to([P, GT, E]), ALU.add))
                    ch.link(nc.vector.tensor_reduce(total[:, :], logits[:, :, :], X, ALU.max))
                    nc.vector.tensor_tensor(exps[:, :, :], logits[:, :, :], total[:, :].unsqueeze(2).broadcast_to([P, GT, E]), ALU.subtract).then_inc(shifted, 1)
                    if beside:
                        pr.keep_values(dve)
                    dve.wait_ge(raised, 1)
                    ch.link(nc.vector.tensor_reduce(total[:, :], exps[:, :, :], X, ALU.add))
                    nc.vector.reciprocal(prob_all[:, bass.ds(g * GT, GT)], total[:, :])
                    pick_first(nc, ch, m, logits, best, pick_all[:, bass.ds(g * GT, GT), :])
            s.clear()

        first_projection()
        with nc.Fori(0, GROUPS - 1) as g:
            group(g, True)
        group(GROUPS - 1, False)
    params.memory.clear()


class Norm:

    def __init__(self, a, y, out, scale=None, store=None):
        self.a, self.y, self.out, self.scale, self.store = a, y, out, scale, store


def norm_all(nc, m, s, outputs, norm):
    STEPS = 4
    n = TILES // STEPS
    a, y, out, scale, store = norm.a, norm.y, norm.out, norm.scale, norm.store
    ln = LayerNorm(s, "norm", TILES)
    scaled, added, var_ready, sd_ready, done, normed, stored = (s.sem(x) for x in (
        "scaled", "added", "var_ready", "sd_ready", "done", "normed", "stored"))
    loaded = [s.sem(f"loaded{k}") for k in range(STEPS)]
    with nc.Block() as block:
        @block.gpsimd
        def _(pool):
            for k in range(STEPS):
                at = slice(n * k, n * k + n)
                pool.wait_ge(loaded[k], 16)
                if scale is not None:
                    nc.gpsimd.tensor_tensor(y[:, at, :], y[:, at, :], scale[:, at].unsqueeze(2).broadcast_to([P, n, P]), ALU.mult).then_inc(scaled, 1)
                    pool.wait_ge(scaled, k + 1)
                nc.gpsimd.tensor_tensor(y[:, at, :], y[:, at, :], a[:, at, :], ALU.add).then_inc(added, 1)

        @block.scalar
        def _(act):
            for k in range(STEPS):
                act.wait_ge(var_ready, k + 1)
                ln.root(nc, m, slice(n * k, n * k + n)).then_inc(sd_ready, 1)

        @block.vector
        def _(dve):
            ch = Chain(dve, done)
            for k in range(STEPS + 1):
                if k < STEPS:
                    at = slice(n * k, n * k + n)
                    dve.wait_ge(added, k + 1)
                    ln.take_stats(nc, ch, y[:, at, :], var_ready, n * k)
                if k >= 1:
                    at = slice(n * (k - 1), n * k)
                    ln.finish(nc, dve, ch, y[:, at, :], out[:, at, :], sd_ready, k, n * (k - 1)).then_inc(normed, 1)

        @block.sync
        def _(sp):
            by_token = lambda rows, k: rows.rearrange("(t p) d -> p t d", p=P)[:, n * k:n * k + n, :]
            for k in range(STEPS):
                sp.dma_start(y[:, n * k:n * k + n, :], by_token(outputs[0:TOKENS, :], k)).then_inc(loaded[k], 16)
            if store is not None:
                for k in range(STEPS):
                    sp.wait_ge(normed, k + 1)
                    sp.dma_start(by_token(store, k), out[:, n * k:n * k + n, :]).then_inc(stored, 16)
                sp.wait_ge(stored, 16 * STEPS)


def laid_out(i):
    a = {"consts": constants(), "x": i["L0_attn_hidden_states"].reshape(TOKENS, D)}
    for n in ("q", "k", "v"):
        a[f"W{n}_t"] = i[f"L0_attn_W{n}"].T
        a[f"conv_{n}_t"] = i[f"L0_attn_conv_{n}_w"].T.reshape(-1)
    a["Wb_t"] = i["L0_attn_Wb"].T
    a["w_qkv"] = np.concatenate([i[f"L0_ffn_W{n}"] for n in "qkv"], 1)
    a["b_qkv"] = np.concatenate([i[f"L0_ffn_b{n}"] for n in "qkv"])
    a["qk_w"] = np.concatenate([np.tile(i["L0_ffn_qn_w"], NQ), np.tile(i["L0_ffn_kn_w"], NKV)])
    a["ffn_Wo"], a["ffn_bo"], a["ffn_Wr"], a["ffn_br"] = (i[f"L0_ffn_{n}"] for n in ("Wo", "bo", "Wr", "br"))
    a["Wg_tiled"] = np.tile(i["L0_ffn_Wg"], (NQ, NQ))
    a["bg_tiled"] = np.tile(i["L0_ffn_bg"], NQ).reshape(P, 1)
    a["ln1"], a["ln2"] = i["L0_ffn_ln1_w"].reshape(P, 1), i["L0_ffn_ln2_w"].reshape(P, 1)
    for n in range(2):
        a[f"experts{n}_W1"], a[f"experts{n}_W2"] = i[f"L{n}_ffn_W1"], i[f"L{n}_ffn_W2"]
        a[f"experts{n}_b1"], a[f"experts{n}_b2"] = i[f"L{n}_ffn_b1"].reshape(-1, P).T, i[f"L{n}_ffn_b2"].reshape(P, -1)
    for n in ("Wq", "Wk", "Wv", "Wo", "bo", "theta"):
        a[f"L1_{n}"] = i[f"L1_attn_{n}"]
    a["L1_gamma"], a["L1_beta"] = i["L1_attn_gamma"].reshape(P, 1), i["L1_attn_beta"].reshape(P, 1)
    for n in ("Wr", "br", "ln_g", "ln_b"):
        a[f"L1_{n}"] = i[f"L1_ffn_{n}"]
    a["gate_w1x_t"] = i["L0_attn_gate_W1"][:, :D].T
    a["gate_w1s_t"] = i["L0_attn_gate_W1"][:, D:].T
    a["gate_w2_t"] = i["L0_attn_gate_W2"].T
    a["gate_b1"] = i["L0_attn_gate_b1"].reshape(P, 1)
    a["gate_b2"] = i["L0_attn_gate_b2"]
    a["copy_bias"] = i["L0_attn_gate_copy_bias"]
    a["log_temp"] = i["L0_attn_gate_log_temp"]
    a["o_norm"] = i["L0_attn_o_norm_w"].reshape(DK, 1)
    a["Wo_t"] = i["L0_attn_Wo"].T
    a["fir_short"] = i["L0_attn_fir_short_filt"].reshape(P, FIRS)
    a["fir_long_rev"] = i["L0_attn_fir_long_filt"].reshape(P, FIRL)[:, ::-1]
    return a


def kernel(**inputs):
    import concourse.bacc as bacc
    from concourse.bass_utils import run_bass_kernel_spmd

    nc = bacc.Bacc("TRN2", target_bir_lowering=False, num_devices=1)
    arrays = {k: np.ascontiguousarray(v) for k, v in laid_out(inputs).items()}
    io = {k: nc.dram_tensor(k, v.shape, mybir.dt.from_np(v.dtype), kind="ExternalInput").ap() for k, v in arrays.items()}
    for name, shape in SCRATCH.items():
        io[name] = nc.dram_tensor(name, shape, F32, kind="Internal").ap()
    out = nc.dram_tensor("out", (TOKENS, D), F32, kind="ExternalOutput").ap()
    build_program(nc, io, out)
    got = run_bass_kernel_spmd(nc, [arrays], core_ids=[0]).results[0]["out"]
    return got.reshape(BATCH, SEQ, D)
```
